# Optimizing a Trainium2 kernel written in Bass

```python
import numpy as np
import jax
import jax.numpy as jnp

def _softmax(x, axis=-1):
    return jax.nn.softmax(x, axis=axis)

def _gelu(x):
    return jax.nn.gelu(x, approximate=True)

def _silu(x):
    return jax.nn.silu(x)

def _sigmoid(x):
    return jax.nn.sigmoid(x)

def _layernorm(x, axis=-1, eps=1e-05):
    m = jnp.mean(x, axis=axis, keepdims=True)
    v = jnp.var(x, axis=axis, keepdims=True)
    return (x - m) / jnp.sqrt(v + eps)

def _scatter_add(tgt, idx, src, axis=0):
    return tgt.at[idx].add(src)

def _segment_sum(src, seg, n):
    return jax.ops.segment_sum(src, seg, n)
kernel_name = 'mk_vit_tower_d1_tok_img4096_r4_70a930'

def setup_inputs(seed: int=0):
    np.random.seed(seed)
    _w = jnp.asarray

    def _rec_inputs():
        import jax
        import jax.numpy as jnp
        _rk = jax.random.key(seed)
        x = -0.00348982 + 0.707501 * jax.random.normal(jax.random.fold_in(_rk, 1), (16, 128, 64, 2), jnp.float32)
        return x
    x = _rec_inputs()

    def _L0_tok_setup():
        import jax, jax.numpy as jnp
        import numpy as np
        H, N, S, CH, LEN = (128, 64, 128, 1, 1024)

        def _s4d_kernel(log_dt, C, B, inv_A_real, A_imag, L):
            dt = jnp.exp(log_dt)
            Cc = C[..., 0] + 1j * C[..., 1]
            Bc = B[..., 0] + 1j * B[..., 1]
            A = -jnp.exp(inv_A_real) + 1j * A_imag
            rep = H // A.shape[0]
            A = jnp.tile(A, (rep, 1))
            Bc = jnp.tile(Bc, (rep, 1))
            dtA = A * dt[:, None]
            Cc = Bc[None, :, :] * Cc
            Cc = Cc * (jnp.exp(dtA) - 1.0) / A
            ell = jnp.arange(L, dtype=jnp.float32)
            V = jnp.exp(dtA[:, :, None] * ell)
            K = 2.0 * jnp.einsum('chn,hnl->chl', Cc, V).real
            return K.astype(jnp.float32)
        key = jax.random.key(seed)
        k1, k2 = jax.random.split(key, 2)
        log_dt = jax.random.uniform(k1, (H,), minval=float(np.log(0.001)), maxval=float(np.log(0.1))).astype(jnp.float32)
        inv_A_real = jnp.full((S, N), float(np.log(0.5)), dtype=jnp.float32)
        A_imag = jnp.tile((np.pi * jnp.arange(N, dtype=jnp.float32))[None, :], (S, 1))
        B = jnp.stack([jnp.ones((S, N), jnp.float32), jnp.zeros((S, N), jnp.float32)], axis=-1)
        C = (jax.random.normal(k2, (CH, H, N, 2)) * 0.5 ** 0.5).astype(jnp.float32)
        return {'log_dt': log_dt, 'C': C, 'B': B, 'inv_A_real': inv_A_real, 'A_imag': A_imag, 'L': LEN}
    _L0_tok_all = _L0_tok_setup()
    _L0_tok_in = {k: v for k, v in _L0_tok_all.items() if k in ('log_dt', 'B', 'inv_A_real', 'A_imag')}
    del _L0_tok_all

    def _L0_attn_setup():
        import jax, jax.numpy as jnp
        import numpy as np
        import math
        B, L, D, H = (32, 128, 1024, 32)
        HD = D // H
        key = jax.random.key(seed)
        ks = jax.random.split(key, 9)
        s = 1.0 / math.sqrt(D)
        return {'x': jax.random.normal(ks[0], (B, L, D), jnp.float32), 'Wq': jax.random.normal(ks[1], (D, D), jnp.float32) * s, 'bq': jax.random.normal(ks[2], (D,), jnp.float32) * s, 'Wk': jax.random.normal(ks[3], (D, D), jnp.float32) * s, 'bk': jax.random.normal(ks[4], (D,), jnp.float32) * s, 'Wv': jax.random.normal(ks[5], (D, D), jnp.float32) * s, 'bv': jax.random.normal(ks[6], (D,), jnp.float32) * s, 'Wo': jax.random.normal(ks[7], (D, D), jnp.float32) * s, 'bo': jax.random.normal(ks[8], (D,), jnp.float32) * s}
    _L0_attn_all = _L0_attn_setup()
    _L0_attn_in = {k: v for k, v in _L0_attn_all.items() if k in ('Wq', 'bq', 'Wk', 'bk', 'Wv', 'bv', 'Wo', 'bo')}
    del _L0_attn_all

    def _L0_ffn_setup():
        import jax, jax.numpy as jnp
        import numpy as np
        H = 1024
        I = 2752
        R = 32
        NLEV = 16
        Q_ZERO = 7.5
        Q_STEP = 0.005
        LR_SCALE = 0.02

        def _qlinear(x, q, scale, A, Bm):
            w = (q.astype(jnp.float32) - Q_ZERO) * (scale * Q_STEP)[:, None]
            y = jnp.einsum('bsh,oh->bso', x, w)
            return y + LR_SCALE * (x @ A @ Bm)
        key = jax.random.key(seed)
        ks = jax.random.split(key, 13)
        B, S = (2, 512)
        inp = {'x': jax.random.normal(ks[0], (B, S, H), jnp.float32), 'gate_q': jax.random.randint(ks[1], (I, H), 0, NLEV, jnp.int32), 'gate_scale': jax.random.uniform(ks[2], (I,), jnp.float32), 'gate_A': jax.random.normal(ks[3], (H, R), jnp.float32), 'gate_B': jax.random.normal(ks[4], (R, I), jnp.float32), 'up_q': jax.random.randint(ks[5], (I, H), 0, NLEV, jnp.int32), 'up_scale': jax.random.uniform(ks[6], (I,), jnp.float32), 'up_A': jax.random.normal(ks[7], (H, R), jnp.float32), 'up_B': jax.random.normal(ks[8], (R, I), jnp.float32), 'down_q': jax.random.randint(ks[9], (H, I), 0, NLEV, jnp.int32), 'down_scale': jax.random.uniform(ks[10], (H,), jnp.float32), 'down_A': jax.random.normal(ks[11], (I, R), jnp.float32), 'down_B': jax.random.normal(ks[12], (R, H), jnp.float32)}
        return inp
    _L0_ffn_all = _L0_ffn_setup()
    _L0_ffn_in = {k: v for k, v in _L0_ffn_all.items() if k in ('gate_q', 'gate_scale', 'gate_A', 'gate_B', 'up_q', 'up_scale', 'up_A', 'up_B', 'down_q', 'down_scale', 'down_A', 'down_B')}
    del _L0_ffn_all
    return {'x': x, 'L0_tok_log_dt': _L0_tok_in['log_dt'], 'L0_tok_B': _L0_tok_in['B'], 'L0_tok_inv_A_real': _L0_tok_in['inv_A_real'], 'L0_tok_A_imag': _L0_tok_in['A_imag'], 'L0_attn_Wq': _L0_attn_in['Wq'], 'L0_attn_bq': _L0_attn_in['bq'], 'L0_attn_Wk': _L0_attn_in['Wk'], 'L0_attn_bk': _L0_attn_in['bk'], 'L0_attn_Wv': _L0_attn_in['Wv'], 'L0_attn_bv': _L0_attn_in['bv'], 'L0_attn_Wo': _L0_attn_in['Wo'], 'L0_attn_bo': _L0_attn_in['bo'], 'L0_ffn_gate_q': _L0_ffn_in['gate_q'], 'L0_ffn_gate_scale': _L0_ffn_in['gate_scale'], 'L0_ffn_gate_A': _L0_ffn_in['gate_A'], 'L0_ffn_gate_B': _L0_ffn_in['gate_B'], 'L0_ffn_up_q': _L0_ffn_in['up_q'], 'L0_ffn_up_scale': _L0_ffn_in['up_scale'], 'L0_ffn_up_A': _L0_ffn_in['up_A'], 'L0_ffn_up_B': _L0_ffn_in['up_B'], 'L0_ffn_down_q': _L0_ffn_in['down_q'], 'L0_ffn_down_scale': _L0_ffn_in['down_scale'], 'L0_ffn_down_A': _L0_ffn_in['down_A'], 'L0_ffn_down_B': _L0_ffn_in['down_B']}

def reference(x, L0_tok_log_dt, L0_tok_B, L0_tok_inv_A_real, L0_tok_A_imag, L0_attn_Wq, L0_attn_bq, L0_attn_Wk, L0_attn_bk, L0_attn_Wv, L0_attn_bv, L0_attn_Wo, L0_attn_bo, L0_ffn_gate_q, L0_ffn_gate_scale, L0_ffn_gate_A, L0_ffn_gate_B, L0_ffn_up_q, L0_ffn_up_scale, L0_ffn_up_A, L0_ffn_up_B, L0_ffn_down_q, L0_ffn_down_scale, L0_ffn_down_A, L0_ffn_down_B):
    import jax
    import jax.numpy as jnp

    def _L0_tok_ref(log_dt, C, B, inv_A_real, A_imag, L):
        import jax, jax.numpy as jnp
        import numpy as np
        H, N, S, CH, LEN = (128, 64, 128, 1, 1024)

        def _s4d_kernel(log_dt, C, B, inv_A_real, A_imag, L):
            dt = jnp.exp(log_dt)
            Cc = C[..., 0] + 1j * C[..., 1]
            Bc = B[..., 0] + 1j * B[..., 1]
            A = -jnp.exp(inv_A_real) + 1j * A_imag
            rep = H // A.shape[0]
            A = jnp.tile(A, (rep, 1))
            Bc = jnp.tile(Bc, (rep, 1))
            dtA = A * dt[:, None]
            Cc = Bc[None, :, :] * Cc
            Cc = Cc * (jnp.exp(dtA) - 1.0) / A
            ell = jnp.arange(L, dtype=jnp.float32)
            V = jnp.exp(dtA[:, :, None] * ell)
            K = 2.0 * jnp.einsum('chn,hnl->chl', Cc, V).real
            return K.astype(jnp.float32)
        return _s4d_kernel(log_dt, C, B, inv_A_real, A_imag, L)

    def _L0_attn_ref(x, Wq, bq, Wk, bk, Wv, bv, Wo, bo):
        import jax, jax.numpy as jnp
        import numpy as np
        import math
        B, L, D, H = (32, 128, 1024, 32)
        HD = D // H
        b, l, d = x.shape
        h, hd = (H, HD)
        q = (x @ Wq.T + bq).reshape(b, l, h, hd).transpose(0, 2, 1, 3)
        k = (x @ Wk.T + bk).reshape(b, l, h, hd).transpose(0, 2, 1, 3)
        v = (x @ Wv.T + bv).reshape(b, l, h, hd).transpose(0, 2, 1, 3)
        scores = jnp.einsum('bhqd,bhkd->bhqk', q, k) / math.sqrt(hd)
        causal = jnp.tril(jnp.ones((l, l), bool))
        scores = jnp.where(causal, scores, -jnp.inf)
        att = jax.nn.softmax(scores, axis=-1)
        out = jnp.einsum('bhqk,bhkd->bhqd', att, v)
        out = out.transpose(0, 2, 1, 3).reshape(b, l, d)
        return out @ Wo.T + bo

    def _L0_ffn_ref(x, gate_q, gate_scale, gate_A, gate_B, up_q, up_scale, up_A, up_B, down_q, down_scale, down_A, down_B):
        import jax, jax.numpy as jnp
        import numpy as np
        H = 1024
        I = 2752
        R = 32
        NLEV = 16
        Q_ZERO = 7.5
        Q_STEP = 0.005
        LR_SCALE = 0.02

        def _qlinear(x, q, scale, A, Bm):
            w = (q.astype(jnp.float32) - Q_ZERO) * (scale * Q_STEP)[:, None]
            y = jnp.einsum('bsh,oh->bso', x, w)
            return y + LR_SCALE * (x @ A @ Bm)
        g = _qlinear(x, gate_q, gate_scale, gate_A, gate_B)
        u = _qlinear(x, up_q, up_scale, up_A, up_B)
        h = jax.nn.silu(g) * u
        return _qlinear(h, down_q, down_scale, down_A, down_B)
    h = _L0_tok_ref(L0_tok_log_dt, x, L0_tok_B, L0_tok_inv_A_real, L0_tok_A_imag, 1024)
    h = h + _L0_attn_ref(_layernorm(h, axis=-1), L0_attn_Wq, L0_attn_bq, L0_attn_Wk, L0_attn_bk, L0_attn_Wv, L0_attn_bv, L0_attn_Wo, L0_attn_bo)
    h = h + _L0_ffn_ref(_layernorm(h, axis=-1), L0_ffn_gate_q, L0_ffn_gate_scale, L0_ffn_gate_A, L0_ffn_gate_B, L0_ffn_up_q, L0_ffn_up_scale, L0_ffn_up_A, L0_ffn_up_B, L0_ffn_down_q, L0_ffn_down_scale, L0_ffn_down_A, L0_ffn_down_B)
    return h

_drawn_inputs = setup_inputs


def setup_inputs(seed=0):
    import zlib

    import numpy as np

    out = dict(_drawn_inputs(seed))
    spreads = {'L0_tok_inv_A_real': (-0.6931471824645996, 0.2)}
    factors = {}
    for name, (base, spread) in spreads.items():
        noise = np.random.default_rng([zlib.crc32(name.encode()), seed]).standard_normal(out[name].shape)
        drawn = base * np.exp(spread * noise) if base else spread * noise
        out[name] = jnp.asarray(drawn.astype(out[name].dtype))
    for name, factor in factors.items():
        out[name] = (out[name] * factor).astype(out[name].dtype)
    return out
```

```python
import math
from contextlib import ExitStack

import concourse.bass as bass
from concourse import mybir

F32 = mybir.dt.float32
F32R = mybir.dt.float32r
F16 = mybir.dt.float16
BF16 = mybir.dt.bfloat16
I32 = mybir.dt.int32
ALU = mybir.AluOpType
ACT = mybir.ActivationFunctionType
X = mybir.AxisListType.X

P = 128
C, H, N = 16, 128, 64
D = 1024
KT = D // P
TOK = C * H
MAGIC = 1.5 * 2.0 ** 23
TWO_PI = 6.2831845
EPS = 1e-5


def bc(ap, n, at):
    shape = list(ap.shape)
    shape.insert(at, n)
    return ap.unsqueeze(at).broadcast_to(shape)


def start_free(nc, sems, count):
    for sem in sems:
        nc.sync.sem_inc(sem, count)


def apart(eng, passed, *waits):
    for sem, value in waits:
        eng.wait_ge(sem, value)
    eng.sem_inc(passed, 1)


class Chain:

    def __init__(self, eng, sem):
        self.eng, self.sem, self.count, self.turn = eng, sem, 0, 0

    def loop(self, it, n):
        self.turn = it * n

    def end(self, turns, n, first):
        assert self.count - first == n, (self.count - first, n)
        self.count, self.turn = first + turns * n, 0

    def mark(self, ins):
        self.count += 1
        ins.then_inc(self.sem, 1)
        return self.count

    def now(self):
        return self.turn + self.count

    def wait(self):
        self.eng.wait_ge(self.sem, self.now())

    def after(self, ins):
        self.mark(ins)
        self.wait()


def ssm_kernel(nc, ssm, cr, ci, x0t):
    HB = 16
    NB = H // HB
    sems = []
    with ExitStack() as st:
        def sb(name, shape, dt=F32):
            return st.enter_context(nc.sbuf_tensor(name, shape, dt))

        def sem(name):
            sems.append(nc.alloc_semaphore(name))
            return sems[-1]

        par = sb("ssm_par", [P, 5, H])
        cre, cim = sb("c_re", [P, H, C]), sb("c_im", [P, H, C])
        t01 = sb("ssm_t01", [P, 2, H])
        t = [t01[:, 0, :], t01[:, 1, :]] + [sb(f"ssm_t{k}", [P, H]) for k in range(2, 12)]
        er, ek, ew = sb("exp_r", [P, 2, H]), sb("exp_k", [P, 2, H]), sb("exp_w", [P, 2, H], I32)
        quarter = sb("quarter", [P, 1])
        jota = sb("jota", [P, P])
        iota1 = sb("iota1", [P, KT])
        u1, u2 = sb("u1", [P, H, C]), sb("u2", [P, H, C])
        tmp_u = sb("tmp_u", [P, H, C])
        v1r, v1i, mag1 = sb("v1r", [P, H, KT]), sb("v1i", [P, H, KT]), sb("mag1", [P, H, KT])
        tmp1 = sb("tmp1", [P, H, KT])
        ph = [sb(f"phase{s}", [P, HB, P]) for s in range(2)]
        rd = sb("rounded", [P, HB, P])
        za = [sb(f"decay{s}", [P, HB, P]) for s in range(2)]
        w1 = sb("w_first", [P, HB, KT, C])
        w2 = sb("w_second", [P, HB, KT, C])
        ww = [sb(f"w_{s}", [P, HB, KT * C]) for s in range(2)]
        ps = [st.enter_context(nc.psum_tensor(f"ssm_ps{b}", [P, 4, P], F32)) for b in range(4)]

        s_in, s_iota = sem("a_in"), sem("a_iota")
        s_dve, s_act, s_pool = sem("a_dve"), sem("a_act"), sem("a_pool")
        s_exp0, s_z, s_tr0, s_v1, s_u = sem("a_exp0"), sem("a_z"), sem("a_tr0"), sem("a_v1"), sem("a_u")
        s_turn0, s_sin0, s_passed = sem("a_turn0"), sem("a_sin0"), sem("a_passed")
        s_za, s_ph, s_trig, s_w2 = ([sem(f"a_{n}{s}") for s in range(2)] for n in ("za", "ph", "trig", "w2"))
        s_v2, s_w = ([sem(f"a_{n}{s}") for s in range(2)] for n in ("v2", "w"))
        s_mm = [[sem(f"a_mm{s}{b}") for b in range(4)] for s in range(2)]
        s_ev = [sem(f"a_ev{b}") for b in range(4)]
        logdt, inva, aim, br, bi = (par[:, k, :] for k in range(5))
        start_free(nc, [*s_mm[0], *s_mm[1], *s_w, *s_ev], 1)
        nc.all_engine_barrier()
        block = st.enter_context(nc.Block())

        @block.sync
        def _(sp):
            sp.dma_start(par[:], ssm).then_inc(s_in, 16)
            sp.dma_start(cre[:], cr).then_inc(s_in, 16)
            sp.dma_start(cim[:], ci).then_inc(s_in, 16)

        @block.gpsimd
        def _(pool):
            nc.gpsimd.iota(jota[:], [[1, P]], base=0, channel_multiplier=0, allow_small_or_imprecise_dtypes=True).then_inc(s_iota, 1)
            nc.gpsimd.iota(iota1[:], [[P, KT]], base=0, channel_multiplier=0, allow_small_or_imprecise_dtypes=True).then_inc(s_iota, 1)
            pool.wait_ge(s_iota, 4)
            pool.wait_ge(s_z, 1)
            chain = Chain(pool, s_pool)
            with pool.Fori(0, NB // 2) as it:
                chain.loop(it, 2)
                for s in range(2):
                    hb = bass.ds((it * 2 + s) * HB, HB)
                    pool.wait_ge(s_mm[s][3], it + 1)
                    nc.gpsimd.tensor_tensor(za[s][:], bc(t[2][:, hb], P, 2), bc(jota[:], HB, 1),
                                            ALU.mult).then_inc(s_za[s], 1)
                    if s == 0:
                        pool.wait_ge(s_u, 1)
                    chain.after(nc.gpsimd.tensor_tensor(w1[:], bc(u1[:, hb, :], KT, 2), bc(v1r[:, hb, :], C, 3), ALU.mult))
                    pool.wait_ge(s_w2[s], it + 1)
                    pool.wait_ge(s_mm[s][3], it + 1)
                    nc.gpsimd.tensor_tensor(ww[s][:].rearrange("p h (i c) -> p h i c", c=C), w1[:], w2[:],
                                            ALU.add).then_inc(s_w[s], 1)
                    pool.wait_ge(s_w[s], it + 2)

        @block.scalar
        def _(act):
            act.wait_ge(s_z, 1)
            nc.scalar.activation(t[4][:], t[2][:], ACT.Exp).then_inc(s_exp0, 1)
            nc.scalar.activation(t[5][:], t[2][:], ACT.Tanh, scale=0.5).then_inc(s_exp0, 1)
            act.wait_ge(s_v1, 1)
            nc.scalar.activation(mag1[:], mag1[:], ACT.Exp).then_inc(s_exp0, 1)
            act.wait_ge(s_turn0, 1)
            nc.scalar.activation(v1r[:], v1r[:], ACT.Sin, scale=TWO_PI).then_inc(s_sin0, 1)
            nc.scalar.activation(v1i[:], v1i[:], ACT.Sin, scale=TWO_PI).then_inc(s_sin0, 1)
            with act.Fori(0, NB // 2) as it:
                for s in range(2):
                    act.wait_ge(s_za[s], it + 1)
                    nc.scalar.activation(za[s][:], za[s][:], ACT.Exp).then_inc(s_trig[s], 1)
                    act.wait_ge(s_ph[s], it + 1)
                    nc.scalar.activation(ph[s][:], ph[s][:], ACT.Sin, scale=TWO_PI).then_inc(s_trig[s], 1)
                    for b in range(4):
                        apart(act, s_passed, (s_mm[s][b], it + 2))
                        nc.scalar.activation(x0t[:, :, bass.ds((it * 2 + s) * HB + 4 * b, 4)],
                                             ps[b][:].rearrange("p h m -> p m h"), ACT.Copy).then_inc(s_ev[b], 1)

        @block.vector
        def _(dve):
            chain = Chain(dve, s_dve)
            tt, ts = nc.vector.tensor_tensor, nc.vector.tensor_scalar
            nc.vector.memset(quarter[0:N, :], 0.25).then_inc(s_iota, 1)
            nc.vector.memset(quarter[N:P, :], 0.0).then_inc(s_iota, 1)
            dve.wait_ge(s_in, 48)
            chain.after(ts(er[:], par[:, 0:2, :], -87.0, 88.0, ALU.max, ALU.min))
            chain.after(ts(ek[:], er[:], 1.0 / math.log(2.0), None, ALU.mult))
            chain.after(ts(ek[:], ek[:], MAGIC, MAGIC, ALU.add, ALU.subtract))
            chain.mark(ts(ew[:], ek[:], 127.0, 2.0 ** 23, ALU.add, ALU.mult))
            chain.after(nc.vector.scalar_tensor_tensor(er[:], ek[:], -0.693359375, er[:], ALU.mult, ALU.add))
            chain.after(nc.vector.scalar_tensor_tensor(er[:], ek[:], 2.12194440e-4, er[:], ALU.mult, ALU.add))
            chain.after(ts(ek[:], er[:], 1 / math.factorial(7), None, ALU.mult))
            for k in range(6, 0, -1):
                chain.after(nc.vector.scalar_tensor_tensor(ek[:], ek[:], 1 / math.factorial(k), er[:], ALU.add, ALU.mult))
            chain.after(nc.vector.scalar_tensor_tensor(t01[:], ek[:], 1.0, ew[:].bitcast(F32), ALU.add, ALU.mult))
            chain.after(tt(t[2][:], t[1][:], t[0][:], ALU.mult))
            chain.after(ts(t[2][:], t[2][:], -1.0, None, ALU.mult))
            chain.after(tt(t[3][:], aim, t[0][:], ALU.mult))
            ts(t[3][:], t[3][:], 1.0 / (2 * math.pi), None, ALU.mult).then_inc(s_z, 1)
            dve.wait_ge(s_z, 1)
            dve.wait_ge(s_iota, 4)

            def fraction(out, whole):
                chain.after(ts(whole, out, MAGIC, MAGIC, ALU.add, ALU.subtract))
                chain.after(tt(out, out, whole, ALU.subtract))

            tt(mag1[:], bc(t[2][:], KT, 2), bc(iota1[:], H, 1), ALU.mult).then_inc(s_v1, 1)
            chain.mark(tt(v1i[:], bc(t[3][:], KT, 2), bc(iota1[:], H, 1), ALU.mult))
            chain.after(nc.vector.tensor_copy(t[6][:], t[3][:]))
            chain.after(ts(v1r[:], v1i[:], 0.25, None, ALU.add))
            fraction(v1i[:], tmp1[:])
            fraction(v1r[:], tmp1[:])
            ts(t[8][:], t[6][:], MAGIC, MAGIC, ALU.add, ALU.subtract).then_inc(s_turn0, 1)
            dve.wait_ge(s_turn0, 1)
            chain.after(tt(t[6][:], t[6][:], t[8][:], ALU.subtract))
            chain.after(ts(t[6][:], t[6][:], math.pi, None, ALU.mult))
            y, w, sin, cos = t[6], t[8], t[7], t[9]
            chain.after(tt(w[:], y[:], y[:], ALU.mult))
            chain.mark(ts(sin[:], w[:], 1 / math.factorial(13), None, ALU.mult))
            chain.after(ts(cos[:], w[:], 1 / math.factorial(12), None, ALU.mult))
            for k in range(5, 0, -1):
                chain.mark(nc.vector.scalar_tensor_tensor(sin[:], sin[:], (-1) ** k / math.factorial(2 * k + 1), w[:], ALU.add, ALU.mult))
                chain.after(nc.vector.scalar_tensor_tensor(cos[:], cos[:], (-1) ** k / math.factorial(2 * k), w[:], ALU.add, ALU.mult))
            chain.mark(ts(cos[:], cos[:], 1.0, None, ALU.add))
            chain.after(nc.vector.scalar_tensor_tensor(sin[:], sin[:], 1.0, y[:], ALU.add, ALU.mult))
            chain.after(tt(y[:], sin[:], cos[:], ALU.mult))
            chain.after(ts(y[:], y[:], 2.0, None, ALU.mult))
            dve.wait_ge(s_exp0, 3)
            dve.wait_ge(s_sin0, 2)
            chain.mark(tt(v1r[:], v1r[:], mag1[:], ALU.mult))
            chain.mark(tt(v1i[:], v1i[:], mag1[:], ALU.mult))
            chain.after(ts(t[8][:], t[4][:], 1.0, None, ALU.add))
            chain.after(tt(t[8][:], t[8][:], t[5][:], ALU.mult))
            chain.after(tt(t[7][:], t[7][:], t[7][:], ALU.mult))
            chain.after(tt(t[7][:], t[7][:], t[4][:], ALU.mult))
            chain.after(ts(t[7][:], t[7][:], -2.0, None, ALU.mult))
            chain.mark(tt(t[6][:], t[6][:], t[4][:], ALU.mult))
            chain.after(tt(t[7][:], t[7][:], t[8][:], ALU.add))
            chain.mark(tt(t[8][:], br, t[7][:], ALU.mult))
            chain.mark(tt(t[9][:], bi, t[6][:], ALU.mult))
            chain.mark(tt(t[10][:], br, t[6][:], ALU.mult))
            chain.after(tt(t[11][:], bi, t[7][:], ALU.mult))
            chain.mark(tt(t[8][:], t[8][:], t[9][:], ALU.subtract))
            chain.after(tt(t[10][:], t[10][:], t[11][:], ALU.add))
            chain.mark(tt(t[4][:], t[1][:], t[1][:], ALU.mult))
            chain.mark(tt(t[5][:], aim, aim, ALU.mult))
            chain.mark(tt(t[6][:], t[8][:], t[1][:], ALU.mult))
            chain.mark(tt(t[7][:], t[10][:], aim, ALU.mult))
            chain.mark(tt(t[9][:], t[8][:], aim, ALU.mult))
            chain.after(tt(t[11][:], t[10][:], t[1][:], ALU.mult))
            chain.mark(tt(t[4][:], t[4][:], t[5][:], ALU.add))
            chain.mark(tt(t[6][:], t[7][:], t[6][:], ALU.subtract))
            chain.after(tt(t[9][:], t[9][:], t[11][:], ALU.add))
            chain.after(nc.vector.reciprocal(t[4][:], t[4][:]))
            chain.after(ts(t[4][:], t[4][:], 2.0, None, ALU.mult))
            chain.mark(tt(t[6][:], t[6][:], t[4][:], ALU.mult))
            chain.after(tt(t[9][:], t[9][:], t[4][:], ALU.mult))
            a, b = t[7], t[8]
            chain.mark(nc.vector.tensor_copy(a[0:N, :], t[6][0:N, :]))
            chain.mark(nc.vector.tensor_copy(a[N:P, :], t[9][N:P, :]))
            chain.mark(nc.vector.tensor_copy(b[0:N, :], t[9][0:N, :]))
            chain.after(ts(b[N:P, :], t[6][N:P, :], -1.0, None, ALU.mult))
            chain.mark(tt(u1[:], bc(a[:], C, 2), cre[:], ALU.mult))
            chain.mark(tt(tmp_u[:], bc(b[:], C, 2), cim[:], ALU.mult))
            chain.mark(tt(u2[:], bc(b[:], C, 2), cre[:], ALU.mult))
            chain.wait()
            chain.after(tt(u1[:], u1[:], tmp_u[:], ALU.add))
            chain.after(tt(tmp_u[:], bc(a[:], C, 2), cim[:], ALU.mult))
            tt(u2[:], u2[:], tmp_u[:], ALU.subtract).then_inc(s_u, 1)
            dve.wait_ge(s_u, 1)
            first = chain.count
            with dve.Fori(0, NB // 2) as it:
                chain.loop(it, 6)
                for s in range(2):
                    hb = bass.ds((it * 2 + s) * HB, HB)
                    chain.after(tt(ph[s][:], bc(t[3][:, hb], P, 2), bc(jota[:], HB, 1), ALU.mult))
                    chain.after(ts(ph[s][:], ph[s][:], quarter[:], None, ALU.add))
                    chain.after(ts(rd[:], ph[s][:], MAGIC, MAGIC, ALU.add, ALU.subtract))
                    tt(ph[s][:], ph[s][:], rd[:], ALU.subtract).then_inc(s_ph[s], 1)
                    if s == 0:
                        dve.wait_ge(s_w[1], it + 1)
                    else:
                        dve.wait_ge(s_w[0], it + 2)
                    tt(w2[:], bc(u2[:, hb, :], KT, 2), bc(v1i[:, hb, :], C, 3), ALU.mult).then_inc(s_w2[s], 1)
                    dve.wait_ge(s_trig[s], it * 2 + 2)
                    tt(za[s][:], ph[s][:], za[s][:], ALU.mult).then_inc(s_v2[s], 1)
            chain.end(NB // 2, 6, first)

        @block.tensor
        def _(pe):
            with pe.Fori(0, NB // 2) as it:
                for s in range(2):
                    pe.wait_ge(s_v2[s], it + 1)
                    pe.wait_ge(s_w[s], it + 2)
                    for b in range(4):
                        pe.wait_ge(s_ev[b], it * 2 + s + 1)
                        for q in range(4):
                            last = nc.tensor.matmul(ps[b][:, q, :], za[s][:, 4 * b + q, :], ww[s][:, 4 * b + q, :],
                                                    start=True, stop=True)
                        last.then_inc(s_mm[s][b], 1)
    return sems


def first_norm(nc, x0t, h0_dram, xn_hi, xn_lo, ident):
    sems = []
    with ExitStack() as st:
        def sb(name, shape, dt=F32):
            return st.enter_context(nc.sbuf_tensor(name, shape, dt))

        def sem(name):
            sems.append(nc.alloc_semaphore(name))
            return sems[-1]

        two = range(2)
        stage = [sb(f"n_stage{s}", [P, KT, P]) for s in two]
        tok = [sb(f"n_tok{s}", [P, D]) for s in two]
        nrm = [sb(f"n_nrm{s}", [P, D]) for s in two]
        stats = [sb(f"n_stats{s}", [P, 2, 6]) for s in two]
        mv = [sb(f"n_mv{s}", [P, 2]) for s in two]
        std = [sb(f"n_std{s}", [P, 2]) for s in two]
        eps = sb("n_eps", [P, 1])
        pt = [st.enter_context(nc.psum_tensor(f"n_pt{s}", [P, KT, P], F32)) for s in two]
        pn = [st.enter_context(nc.psum_tensor(f"n_pn{s}", [P, KT, P], F32)) for s in two]
        s_stage, s_tr, s_tok, s_mv, s_std, s_nrm, s_trn, s_hi, s_lo, s_st, s_out = (
            [sem(f"n_{n}{s}") for s in two]
            for n in ("stage", "tr", "tok", "mv", "std", "nrm", "trn", "hi", "lo", "st", "out"))
        s_passed = sem("n_passed")
        s_dve, s_eps = sem("n_dve"), sem("n_eps")
        VIS = C // 2
        start_free(nc, [*s_tr, *s_tok, *s_lo, *s_nrm, *s_trn], 1)
        start_free(nc, [*s_out], 16)
        nc.all_engine_barrier()
        block = st.enter_context(nc.Block())

        @block.gpsimd
        def _(pool):
            with pool.Fori(0, VIS) as v:
                for s in two:
                    pool.wait_ge(s_tr[s], v + 1)
                    nc.gpsimd.tensor_copy(stage[s][:], x0t[:].rearrange("p (i c) h -> p c i h", c=C)[:, v * 2 + s, :, :]
                                          ).then_inc(s_stage[s], 1)

        @block.tensor
        def _(pe):
            def to_tokens(v, s):
                pe.wait_ge(s_stage[s], v + 1)
                pe.wait_ge(s_tok[s], v + 1)
                for i in range(KT):
                    last = nc.tensor.transpose(pt[s][:, i, :], stage[s][:, i, :], ident[:])
                last.then_inc(s_tr[s], 1)

            def to_features(v, s):
                pe.wait_ge(s_nrm[s], v + 2)
                pe.wait_ge(s_lo[s], v + 1)
                for i in range(KT):
                    last = nc.tensor.transpose(pn[s][:, i, :], nrm[s][:, i * P:(i + 1) * P], ident[:])
                last.then_inc(s_trn[s], 1)

            to_tokens(0, 0)
            with pe.Fori(0, VIS - 1) as v:
                to_tokens(v, 1)
                to_features(v, 0)
                to_tokens(v + 1, 0)
                to_features(v, 1)
            to_tokens(VIS - 1, 1)
            to_features(VIS - 1, 0)
            to_features(VIS - 1, 1)

        @block.scalar
        def _(act):
            act.wait_ge(s_eps, 1)

            def tokens(v, s):
                act.wait_ge(s_tr[s], v + 2)
                act.wait_ge(s_nrm[s], v + 1)
                act.wait_ge(s_out[s], v * 16 + 16)
                nc.scalar.activation(tok[s][:].rearrange("p (i j) -> p i j", j=P), pt[s][:], ACT.Copy).then_inc(s_tok[s], 1)
                act.wait_ge(s_mv[s], v + 1)
                nc.scalar.activation(std[s][:, 0:1], mv[s][:, 1:2], ACT.Sqrt, bias=eps[:]).then_inc(s_std[s], 1)

            def high(v, s):
                apart(act, s_passed, (s_trn[s], v + 2))
                nc.scalar.activation(xn_hi[:, :, bass.ds((v * 2 + s) * P, P)], pn[s][:], ACT.Copy).then_inc(s_hi[s], 1)

            tokens(0, 0)
            with act.Fori(0, VIS - 1) as v:
                tokens(v, 1)
                high(v, 0)
                tokens(v + 1, 0)
                high(v, 1)
            tokens(VIS - 1, 1)
            high(VIS - 1, 0)
            high(VIS - 1, 1)

        @block.sync
        def _(sp):
            with sp.Fori(0, VIS) as v:
                for s in two:
                    sp.wait_ge(s_tok[s], v + 2)
                    sp.dma_start(h0_dram[bass.ds(v * 2 + s, 1), :, :].rearrange("o h d -> (o h) d"), tok[s][:]).then_inc(s_out[s], 16)
            for s in two:
                sp.wait_ge(s_out[s], 16 * VIS + 16)

        @block.vector
        def _(dve):
            nc.vector.memset(eps[:], EPS).then_inc(s_eps, 1)
            chain = Chain(dve, s_dve)

            def normalise(v, s):
                dve.wait_ge(s_tok[s], v + 2)
                chain.mark(nc.vector.bn_stats(stats[s][:, 0, :], tok[s][:, 0:512]))
                chain.mark(nc.vector.bn_stats(stats[s][:, 1, :], tok[s][:, 512:D]))
                apart(dve, s_passed, (s_dve, chain.now()))
                nc.vector.bn_aggr(mv[s][:], stats[s][:].rearrange("p a b -> p (a b)")).then_inc(s_mv[s], 1)
                dve.wait_ge(s_std[s], v + 1)
                chain.after(nc.vector.reciprocal(std[s][:, 1:2], std[s][:, 0:1]))
                dve.wait_ge(s_trn[s], v + 1)
                nc.vector.tensor_scalar(nrm[s][:], tok[s][:], mv[s][:, 0:1], std[s][:, 1:2],
                                        ALU.subtract, ALU.mult).then_inc(s_nrm[s], 1)

            def low(v, s):
                at = bass.ds((v * 2 + s) * P, P)
                dve.wait_ge(s_hi[s], v + 1)
                nc.vector.tensor_tensor(xn_lo[:, :, at], pn[s][:], xn_hi[:, :, at], ALU.subtract).then_inc(s_lo[s], 1)

            normalise(0, 0)
            first = chain.count
            with dve.Fori(0, VIS - 1) as v:
                chain.loop(v, 6)
                normalise(v, 1)
                low(v, 0)
                normalise(v + 1, 0)
                low(v, 1)
            chain.end(VIS - 1, 6, first)
            normalise(VIS - 1, 1)
            low(VIS - 1, 0)
            low(VIS - 1, 1)
    return sems


HEADS, HD = 32, 32
HPT = P // HD
CH = 512
NCH = TOK // CH
BPC = CH // H
RMAX = bass.bass_isa.ReduceOp.max
W_TOP = 2.0 ** 13


def split_scales(chain, big, low, scale, back):
    chain.after(nc_ts(chain, low, big, 1e-30, None, ALU.max))
    chain.after(nc_ts(chain, low.bitcast(I32), low.bitcast(I32), 0x7F800000, None, ALU.bitwise_and))
    chain.after(chain.eng.reciprocal(scale, low))
    chain.after(nc_ts(chain, scale, scale, W_TOP, None, ALU.mult))
    return nc_ts(chain, back, low, 1.0 / W_TOP, None, ALU.mult)


def nc_ts(chain, *args):
    return chain.eng.tensor_scalar(*args)


def attention(nc, wqkv, bqkv, xn_hi, xn_lo, ident, mask, o_dram):
    sems = []
    with ExitStack() as st:
        def sb(name, shape, dt=F32):
            return st.enter_context(nc.sbuf_tensor(name, shape, dt))

        def ps(name, shape):
            return st.enter_context(nc.psum_tensor(name, shape, F32))

        def sem(name):
            sems.append(nc.alloc_semaphore(name))
            return sems[-1]

        two = range(2)
        raw = sb("w_raw", [P, 3, D])
        w_hi = [sb(f"w_hi{s}", [P, 3, D], F16) for s in two]
        w_lo = [sb(f"w_lo{s}", [P, 3, D], F16) for s in two]
        big, bigs, low2 = sb("w_big", [P, 3]), sb("w_bigs", [P, 3]), sb("w_pow", [P, 3])
        scale, back = sb("w_scale", [P, 3]), [sb(f"w_back{s}", [P, 3]) for s in two]
        bias = sb("b_qkv", [P, 3, KT])
        qf, kf, vf = sb("qf", [P, CH]), sb("kf", [P, CH]), sb("vf", [P, CH])
        qh, ql = sb("qh", [P, CH], F32R), sb("ql", [P, CH], F32R)
        kh, kl = (sb(n, [P, BPC, HPT, H], F32R) for n in ("kh", "kl"))
        vh, vl = (sb(n, [P, BPC, P], F32R) for n in ("vh", "vl"))
        prob = [sb(f"prob{p}", [P, 2 * HPT, H]) for p in two]
        mx, sm = ([sb(f"{n}{p}", [P, 2 * HPT]) for p in two] for n in ("mx", "sm"))
        pth, ptl = ([sb(f"{n}{p}", [P, 2, HPT * H], F32R) for p in two] for n in ("pth", "ptl"))
        ot = [sb(f"ot{s}", [P, CH]) for s in two]
        ps_a, ps_b = ps("ps_a", [P, CH]), ps("ps_b", [P, CH])
        ps_s, ps_t, ps_o = ps("ps_s", [P, 2, CH]), ps("ps_t", [P, 2, CH]), ps("ps_o", [P, 2, CH])

        s_raw, s_bias, s_big, s_bigs, s_scale, s_whi, s_wlo = (
            sem("c_" + n) for n in ("raw", "bias", "big", "bigs", "scale", "whi", "wlo"))
        s_passed = sem("c_passed")
        s_zero = sem("c_zero")
        s_pq, s_pk, s_pv, s_vt = (sem("c_" + n) for n in ("pq", "pk", "pv", "vt"))
        s_qf, s_kf, s_vf, s_ql, s_kl, s_vl = (sem("c_" + n) for n in ("qf", "kf", "vf", "ql", "kl", "vl"))
        s_score, s_mask, s_max, s_sub, s_exp, s_rc, s_prob, s_tr, s_pth, s_ptl, s_pvd, s_ox, s_od = (
            [sem(f"c_{n}{p}") for p in two]
            for n in ("score", "mask", "max", "sub", "exp", "rc", "prob", "tr", "pth", "ptl", "pvd", "ox", "od"))
        s_dve = sem("c_dve")
        TURN = 2 * NCH
        TURNS = KT // 2
        start_free(nc, [*s_od], 16)
        nc.all_engine_barrier()
        block = st.enter_context(nc.Block())

        def where(u, k):
            return u * TURN + k, (k // NCH) % 2, u * 2 + k // NCH, k % NCH

        def run(eng, first, step, last, chain=None, marks=0):
            first()
            before = chain.count if chain else 0
            with eng.Fori(0, TURNS - 1) as u:
                if chain:
                    chain.loop(u, marks)
                for k in range(1, TURN + 1):
                    step(u, k)
            if chain:
                chain.end(TURNS - 1, marks, before)
            for k in range(1, TURN):
                step(TURNS - 1, k)
            last()

        @block.sync
        def _(sp):
            sp.dma_start(bias[:], bqkv).then_inc(s_bias, 16)
            sp.dma_start(raw[:], wqkv[0, :, :, :]).then_inc(s_raw, 16)
            sp.wait_ge(s_wlo, 3)
            sp.dma_start(raw[:], wqkv[1, :, :, :]).then_inc(s_raw, 16)

            def store(u):
                for s in two:
                    for c in range(NCH):
                        n, par = u * TURN + s * NCH + c, c % 2
                        sp.wait_ge(s_ox[1], n + 1)
                        sp.dma_start(o_dram[bass.ds(u * 2 + s, 1), :, c * CH:(c + 1) * CH].rearrange("o f t -> (o f) t"),
                                     ot[par][:]).then_inc(s_od[par], 16)
                        if c == 1 and not isinstance(u, int):
                            sp.wait_ge(s_wlo, (u * 2 + s + 2) * 3)
                            sp.dma_start(raw[:], wqkv[bass.ds(u * 2 + s + 2, 1), :, :, :].rearrange("o p m n -> (o p) m n")
                                         ).then_inc(s_raw, 16)

            with sp.Fori(0, TURNS - 1) as u:
                store(u)
            store(TURNS - 1)
            for par in two:
                sp.wait_ge(s_od[par], 16 * (KT * NCH // 2) + 16)

        @block.gpsimd
        def _(pool):
            nc.gpsimd.memset(kh[:].bitcast(F32), 0.0).then_inc(s_zero, 1)
            nc.gpsimd.memset(kl[:].bitcast(F32), 0.0).then_inc(s_zero, 1)

            def reduce_big(j):
                apart(pool, s_passed, (s_big, j + 1), (s_scale, j))
                nc.gpsimd.partition_all_reduce(bigs[:], big[:], P, RMAX).then_inc(s_bigs, 1)

            def step(u, k, first=False):
                t, ws, j, c = where(u, k)
                for p in two:
                    pool.wait_ge(s_max[p], t + 1)
                    nc.gpsimd.tensor_tensor(prob[p][:], prob[p][:], bc(mx[p][:], H, 2), ALU.subtract).then_inc(s_sub[p], 1)
                for p in two:
                    pool.wait_ge(s_rc[p], t + 1)
                    nc.gpsimd.tensor_tensor(prob[p][:], prob[p][:], bc(sm[p][:], H, 2), ALU.mult).then_inc(s_prob[p], 1)
                if c == 0 and not (isinstance(u, int) and u == TURNS - 1 and k >= NCH):
                    reduce_big(j + 1)

            reduce_big(0)
            run(pool, lambda: step(0, 0), step, lambda: None)

        @block.tensor
        def _(pe):
            def project(m, out, ws, c):
                tok = slice(c * CH, (c + 1) * CH)
                for k in range(KT):
                    w = slice(k * P, (k + 1) * P)
                    nc.tensor.matmul(out[:], w_hi[ws][:, m, w], xn_hi[:, k, tok], start=(k == 0), stop=False)
                    nc.tensor.matmul(out[:], w_hi[ws][:, m, w], xn_lo[:, k, tok], start=False, stop=False)
                    last = nc.tensor.matmul(out[:], w_lo[ws][:, m, w], xn_hi[:, k, tok], start=False, stop=(k == KT - 1))
                return last

            def transposes(p):
                for b in two:
                    for a in range(HPT):
                        last = nc.tensor.transpose(ps_t[:, b, a * H:(a + 1) * H], prob[p][:, b * HPT + a, :], ident[:])
                return last

            def values(p):
                for b in two:
                    at = p * 2 + b
                    nc.tensor.matmul(ps_o[:, b, :], vh[:, at, :], pth[p][:, b, :], start=True, stop=False)
                    nc.tensor.matmul(ps_o[:, b, :], vh[:, at, :], ptl[p][:, b, :], start=False, stop=False)
                    last = nc.tensor.matmul(ps_o[:, b, :], vl[:, at, :], pth[p][:, b, :], start=False, stop=True)
                return last

            def scores(p):
                for b in two:
                    at = p * 2 + b
                    q, k = slice(at * H, (at + 1) * H), slice(0, HPT)
                    nc.tensor.matmul(ps_s[:, b, :], qh[:, q], kh[:, at, k, :], start=True, stop=False)
                    nc.tensor.matmul(ps_s[:, b, :], qh[:, q], kl[:, at, k, :], start=False, stop=False)
                    last = nc.tensor.matmul(ps_s[:, b, :], ql[:, q], kh[:, at, k, :], start=False, stop=True)
                return last

            def attend_first(t):
                pe.wait_ge(s_prob[0], t)
                transposes(0).then_inc(s_tr[0], 1)

            def attend_second(t):
                pe.wait_ge(s_prob[1], t)
                pe.wait_ge(s_ptl[0], t)
                transposes(1).then_inc(s_tr[1], 1)
                pe.wait_ge(s_vl, t)
                values(0).then_inc(s_pvd[0], 1)

            def attend_third(t):
                pe.wait_ge(s_ptl[1], t)
                pe.wait_ge(s_ox[0], t)
                values(1).then_inc(s_pvd[1], 1)

            def step(u, k, first=False):
                t, ws, j, c = where(u, k)
                if c == 0:
                    pe.wait_ge(s_wlo, 3 * (j + 1))
                pe.wait_ge(s_vf, t)
                project(0, ps_a, ws, c).then_inc(s_pq, 1)
                pe.wait_ge(s_vl, t)
                project(1, ps_b, ws, c).then_inc(s_pk, 1)
                if not first:
                    attend_first(t)
                pe.wait_ge(s_qf, t + 1)
                project(2, ps_a, ws, c).then_inc(s_pv, 1)
                if not first:
                    attend_second(t)
                pe.wait_ge(s_ql, t + 1)
                pe.wait_ge(s_kl, t + 1)
                pe.wait_ge(s_mask[1], t)
                scores(0).then_inc(s_score[0], 1)
                if not first:
                    attend_third(t)
                pe.wait_ge(s_vf, t + 1)
                pe.wait_ge(s_kf, t + 1)
                for b in range(BPC):
                    last = nc.tensor.transpose(ps_b[:, b * P:(b + 1) * P], vf[:, b * H:(b + 1) * H], ident[:])
                last.then_inc(s_vt, 1)
                pe.wait_ge(s_mask[0], t + 1)
                scores(1).then_inc(s_score[1], 1)

            def last():
                t = KT * NCH
                attend_first(t)
                attend_second(t)
                attend_third(t)

            run(pe, lambda: step(0, 0, True), step, last)

        @block.scalar
        def _(act):
            def high_weights(ws, j):
                act.wait_ge(s_scale, j + 1)
                for m in range(3):
                    nc.scalar.activation(w_hi[ws][:, m, :], raw[:, m, :], ACT.Copy, scale=scale[:, m:m + 1]).then_inc(s_whi, 1)

            def outputs(p, n_par, v, t):
                act.wait_ge(s_pvd[p], t)
                if p == 0:
                    act.wait_ge(s_od[n_par], v * 16 + 16)
                for a in range(HPT):
                    r = slice(HD * a, HD * a + HD)
                    last = nc.scalar.activation(ot[n_par][r, p * 2 * H:(p + 1) * 2 * H].rearrange("p (b q) -> p b q", q=H),
                                                ps_o[r, :, a * H:(a + 1) * H], ACT.Copy)
                last.then_inc(s_ox[p], 1)

            def attend(u, k, part):
                t = u * TURN + k
                n_par, v = (k - 1) % 2, u * (TURN // 2) + (k - 1) // 2
                if part < 2:
                    act.wait_ge(s_tr[part], t)
                    nc.scalar.activation(pth[part][:], ps_t[:], ACT.Copy).then_inc(s_pth[part], 1)
                else:
                    outputs(part - 2, n_par, v, t)

            def step(u, k, first=False):
                t, ws, j, c = where(u, k)
                apart(act, s_passed, (s_pq, t + 1), (s_ql, t))
                nc.scalar.activation(qf[:], ps_a[:], ACT.Identity, scale=back[ws][:, 0:1],
                                     bias=bias[:, 0, bass.ds(j, 1)]).then_inc(s_qf, 1)
                apart(act, s_passed, (s_pk, t + 1), (s_kl, t))
                nc.scalar.activation(kf[:], ps_b[:], ACT.Identity, scale=back[ws][:, 1:2],
                                     bias=bias[:, 1, bass.ds(j, 1)]).then_inc(s_kf, 1)
                if not first:
                    attend(u, k, 0)
                apart(act, s_passed, (s_pv, t + 1))
                nc.scalar.activation(vf[:], ps_a[:], ACT.Identity, scale=back[ws][:, 2:3],
                                     bias=bias[:, 2, bass.ds(j, 1)]).then_inc(s_vf, 1)
                if not first:
                    attend(u, k, 1)
                    attend(u, k, 2)
                    attend(u, k, 3)
                for p in two:
                    act.wait_ge(s_sub[p], t + 1)
                    nc.scalar.activation(prob[p][:], prob[p][:], ACT.Exp).then_inc(s_exp[p], 1)
                if c == 1 and not (isinstance(u, int) and u == TURNS - 1 and k >= NCH):
                    act.wait_ge(s_pv, t + 1)
                    high_weights(1 - ws, j + 1)

            act.wait_ge(s_bias, 16)
            high_weights(0, 0)
            run(act, lambda: step(0, 0, True), step, lambda: [attend(TURNS - 1, TURN, part) for part in range(4)])

        @block.vector
        def _(dve):
            chain = Chain(dve, s_dve)
            tt = nc.vector.tensor_tensor

            def find_big(j):
                dve.wait_ge(s_raw, 16 * (j + 1))
                nc.vector.tensor_reduce(big[:], raw[:], X, ALU.max, apply_absolute_value=True).then_inc(s_big, 1)

            def low_weights(ws, j):
                dve.wait_ge(s_bigs, j + 1)
                split_scales(chain, bigs[:], low2[:], scale[:], back[ws][:]).then_inc(s_scale, 1)
                for m in range(3):
                    dve.wait_ge(s_whi, 3 * j + m + 1)
                    nc.vector.scalar_tensor_tensor(w_lo[ws][:, m, :], raw[:, m, :], scale[:, m:m + 1], w_hi[ws][:, m, :],
                                                   ALU.mult, ALU.subtract).then_inc(s_wlo, 1)

            def attend(t, p):
                dve.wait_ge(s_pth[p], t)
                tt(ptl[p][:], ps_t[:], pth[p][:].bitcast(F32), ALU.subtract).then_inc(s_ptl[p], 1)

            def top(t, p):
                dve.wait_ge(s_score[p], t + 1)
                nc.vector.scalar_tensor_tensor(prob[p][:], ps_s[:].rearrange("p b (a k) -> p (b a) k", k=H), HD ** -0.5,
                                               bc(mask[:], 2 * HPT, 1), ALU.mult, ALU.add).then_inc(s_mask[p], 1)
                dve.wait_ge(s_mask[p], t + 1)
                nc.vector.tensor_reduce(mx[p][:], prob[p][:], X, ALU.max).then_inc(s_max[p], 1)

            def step(u, k, first=False):
                t, ws, j, c = where(u, k)
                dve.wait_ge(s_qf, t + 1)
                chain.after(nc.vector.tensor_copy(qh[:], qf[:]))
                tt(ql[:], qf[:], qh[:].bitcast(F32), ALU.subtract).then_inc(s_ql, 1)
                dve.wait_ge(s_kf, t + 1)
                for a in range(HPT):
                    r = slice(HD * a, HD * a + HD)
                    last = nc.vector.tensor_copy(kh[r, :, a, :], kf[r, :].rearrange("p (b k) -> p b k", k=H))
                chain.after(last)
                for a in range(HPT):
                    r = slice(HD * a, HD * a + HD)
                    last = tt(kl[r, :, a, :], kf[r, :].rearrange("p (b k) -> p b k", k=H), kh[r, :, a, :].bitcast(F32), ALU.subtract)
                last.then_inc(s_kl, 1)
                if not first:
                    attend(t, 0)
                    attend(t, 1)
                top(t, 0)
                dve.wait_ge(s_vt, t + 1)
                chain.after(nc.vector.tensor_copy(vh[:].rearrange("p b f -> p (b f)"), ps_b[:]))
                tt(vl[:].rearrange("p b f -> p (b f)"), ps_b[:], vh[:].rearrange("p b f -> p (b f)").bitcast(F32),
                   ALU.subtract).then_inc(s_vl, 1)
                top(t, 1)
                for p in two:
                    dve.wait_ge(s_exp[p], t + 1)
                    chain.after(nc.vector.tensor_reduce(sm[p][:], prob[p][:], X, ALU.add))
                    nc.vector.reciprocal(sm[p][:], sm[p][:]).then_inc(s_rc[p], 1)
                if c == 0 and not (isinstance(u, int) and u == TURNS - 1 and k >= NCH):
                    find_big(j + 1)
                if c == 1 and not (isinstance(u, int) and u == TURNS - 1 and k >= NCH):
                    low_weights(1 - ws, j + 1)

            find_big(0)
            low_weights(0, 0)
            dve.wait_ge(s_zero, 2)
            run(dve, lambda: step(0, 0, True), step, lambda: [attend(KT * NCH, p) for p in two],
                chain, TURN * 5 + 2 * 4)
    return sems


R = 32


def project_and_norm(nc, wo, bo, ga, o_dram, h0_dram, h1_dram, x2_hi, x2_lo, low, ident):
    sems = []
    with ExitStack() as st:
        def sb(name, shape, dt=F32):
            return st.enter_context(nc.sbuf_tensor(name, shape, dt))

        def sem(name):
            sems.append(nc.alloc_semaphore(name))
            return sems[-1]

        two = range(2)
        wraw = [sb(f"wo_raw{s}", [P, D]) for s in two]
        woh, wol = sb("wo_hi", [P, KT, D], F32R), sb("wo_lo", [P, KT, D], F32R)
        bob = sb("bo_rows", [P, D])
        gab = sb("gu_a", [P, KT, 2 * R])
        oraw = sb("o_raw", [P, KT, P])
        oh, ol = ([sb(f"{n}{s}", [P, KT, P], F32R) for s in two] for n in ("o_hi", "o_lo"))
        res = sb("residual", [P, D])
        h1 = sb("h1_tok", [P, D])
        nrm = sb("h1_nrm", [P, D])
        x2f = sb("x2_f32", [P, KT, P])
        stats, mv, std, eps = sb("d_stats", [P, 2, 6]), sb("d_mv", [P, 2]), sb("d_std", [P, 2]), sb("d_eps", [P, 1])
        acc = [st.enter_context(nc.psum_tensor(f"d_acc{s}", [P, 2, 512], F32)) for s in two]
        pn = st.enter_context(nc.psum_tensor("d_pn", [P, KT, P], F32))
        pl = st.enter_context(nc.psum_tensor("d_pl", [P, P], F32))
        s_passed = sem("d_passed")
        s_const, s_eps, s_dve = sem("d_const"), sem("d_eps"), sem("d_dve")
        s_wraw = [sem(f"d_wraw{s}") for s in two]
        s_woh, s_wol = sem("d_woh"), sem("d_wol")
        s_o, s_oh, s_ol, s_h0, s_res, s_acc, s_h1, s_h1out, s_mv, s_std, s_nrm, s_trn, s_hi, s_f, s_lo, s_low, s_lowout = (
            sem("d_" + n) for n in ("o", "oh", "ol", "h0", "res", "acc", "h1", "h1out", "mv", "std", "nrm", "trn", "hi",
                                    "f", "lo", "low", "lowout"))
        VIS = C // 2
        start_free(nc, [s_lo, s_lowout, s_h1, s_low], 1)
        nc.all_engine_barrier()
        block = st.enter_context(nc.Block())

        def run(eng, first, step, last, chain=None, marks=0):
            first()
            before = chain.count if chain else 0
            with eng.Fori(0, VIS - 1) as v:
                if chain:
                    chain.loop(v, marks)
                step(v * 2 + 1, 1)
                step(v * 2 + 2, 0)
            if chain:
                chain.end(VIS - 1, marks, before)
            step(C - 1, 1)
            last()

        @block.sync
        def _(sp):
            sp.dma_start(gab[:], ga).then_inc(s_const, 16)
            sp.dma_start(bob[:], bo).then_inc(s_const, 16)
            for k in range(KT):
                if k >= 2:
                    sp.wait_ge(s_wol, k - 1)
                sp.dma_start(wraw[k % 2][:], wo[:, k, :]).then_inc(s_wraw[k % 2], 16)
            with sp.Fori(0, C) as n:
                sp.wait_ge(s_h1, n + 2)
                sp.dma_start(h1_dram[bass.ds(n, 1), :, :].rearrange("o t d -> (o t) d"), h1[:]).then_inc(s_h1out, 16)
            sp.wait_ge(s_h1out, 16 * C)

        @block.gpsimd
        def _(pool):
            pool.wait_ge(s_const, 32)
            with pool.Fori(0, C) as n:
                pool.wait_ge(s_h1, n + 1)
                pool.dma_start(res[:], h0_dram[bass.ds(n, 1), :, :].rearrange("o t d -> (o t) d")).then_inc(s_h0, 16)
                pool.wait_ge(s_h0, n * 16 + 16)
                nc.gpsimd.tensor_tensor(res[:], res[:], bob[:], ALU.add).then_inc(s_res, 1)

        @block.tensor
        def _(pe):
            def half(s, b, n, first=False):
                for k in range(KT):
                    if first and b == 0:
                        pe.wait_ge(s_wol, k + 1)
                    rhs = slice(b * 512, (b + 1) * 512)
                    nc.tensor.matmul(acc[s][:, b, :], oh[s][:, k, :], woh[:, k, rhs], start=(k == 0), stop=False)
                    nc.tensor.matmul(acc[s][:, b, :], oh[s][:, k, :], wol[:, k, rhs], start=False, stop=False)
                    last = nc.tensor.matmul(acc[s][:, b, :], ol[s][:, k, :], woh[:, k, rhs], start=False, stop=(k == KT - 1))
                return last

            def to_features(n):
                pe.wait_ge(s_nrm, n)
                pe.wait_ge(s_lo, n)
                for i in range(KT):
                    last = nc.tensor.transpose(pn[:, i, :], nrm[:, i * P:(i + 1) * P], ident[:])
                last.then_inc(s_trn, 1)

            def low_rank(n):
                pe.wait_ge(s_f, n)
                pe.wait_ge(s_lowout, n)
                for k in range(KT):
                    last = nc.tensor.matmul(pl[0:2 * R, :], gab[:, k, :], x2f[:, k, :], start=(k == 0), stop=(k == KT - 1))
                last.then_inc(s_low, 1)

            def step(n, s, first=False):
                pe.wait_ge(s_ol, n + 1)
                if not first:
                    pe.wait_ge(s_h1, n)
                half(s, 0, n, first)
                if not first:
                    to_features(n)
                half(s, 1, n, first).then_inc(s_acc, 1)
                if not first:
                    low_rank(n)

            def last():
                to_features(C)
                low_rank(C)

            pe.wait_ge(s_const, 32)
            run(pe, lambda: step(0, 0, True), step, last)

        @block.scalar
        def _(act):
            def load(n):
                act.dma_start(oraw[:], o_dram.rearrange("k f t -> f k t")[:, :, bass.ds(n * H, H)]).then_inc(s_o, 16)

            def take(n):
                apart(act, s_passed, (s_trn, n))
                nc.scalar.activation(x2_hi[:, :, bass.ds((n - 1) * H, H)], pn[:], ACT.Copy).then_inc(s_hi, 1)
                act.wait_ge(s_low, n)
                nc.scalar.activation(x2f[:], pn[:], ACT.Copy).then_inc(s_f, 1)
                apart(act, s_passed, (s_low, n + 1))
                nc.scalar.activation(low[:, bass.ds((n - 1) * H, H)], pl[0:2 * R, :], ACT.Copy).then_inc(s_lowout, 1)

            def deviation(n):
                act.wait_ge(s_mv, n + 1)
                nc.scalar.activation(std[:, 0:1], mv[:, 1:2], ACT.Sqrt, bias=eps[:]).then_inc(s_std, 1)

            def split(n, s):
                act.wait_ge(s_o, n * 16 + 16)
                nc.scalar.activation(oh[s][:], oraw[:], ACT.Copy).then_inc(s_oh, 1)

            def step(n, s):
                act.wait_ge(s_ol, n + 1)
                load_n = n + 1
                load(load_n)
                act.wait_ge(s_acc, n)
                split(load_n, 1 - s)
                take(n)
                deviation(n)

            act.wait_ge(s_eps, 1)
            load(0)
            split(0, 0)
            act.wait_ge(s_ol, 1)
            load(1)
            split(1, 1)
            deviation(0)
            with act.Fori(0, VIS - 1) as v:
                step(v * 2 + 1, 1)
                step(v * 2 + 2, 0)
            take(C - 1)
            deviation(C - 1)
            take(C)

        @block.vector
        def _(dve):
            chain = Chain(dve, s_dve)
            nc.vector.memset(eps[:], EPS).then_inc(s_eps, 1)

            def low_split(n, s):
                dve.wait_ge(s_oh, n + 1)
                nc.vector.tensor_tensor(ol[s][:], oraw[:], oh[s][:].bitcast(F32), ALU.subtract).then_inc(s_ol, 1)

            def take(n):
                at = bass.ds((n - 1) * H, H)
                dve.wait_ge(s_f, n)
                nc.vector.tensor_tensor(x2_lo[:, :, at], pn[:], x2_hi[:, :, at], ALU.subtract).then_inc(s_lo, 1)

            def normalise(n, s):
                dve.wait_ge(s_acc, n + 1)
                dve.wait_ge(s_res, n + 1)
                dve.wait_ge(s_h1out, n * 16)
                nc.vector.tensor_tensor(h1[:], acc[s][:].rearrange("p b n -> p (b n)"), res[:], ALU.add).then_inc(s_h1, 1)
                dve.wait_ge(s_h1, n + 2)
                chain.mark(nc.vector.bn_stats(stats[:, 0, :], h1[:, 0:512]))
                chain.mark(nc.vector.bn_stats(stats[:, 1, :], h1[:, 512:D]))
                apart(dve, s_passed, (s_dve, chain.now()))
                nc.vector.bn_aggr(mv[:], stats[:].rearrange("p a b -> p (a b)")).then_inc(s_mv, 1)
                dve.wait_ge(s_std, n + 1)
                chain.after(nc.vector.reciprocal(std[:, 1:2], std[:, 0:1]))
                nc.vector.tensor_scalar(nrm[:], h1[:], mv[:, 0:1], std[:, 1:2], ALU.subtract, ALU.mult).then_inc(s_nrm, 1)

            def step(n, s, end=False):
                if not end:
                    low_split(n + 1, 1 - s)
                take(n)
                normalise(n, s)

            low_split(0, 0)
            for k in range(KT):
                dve.wait_ge(s_wraw[k % 2], 16 * (k // 2 + 1))
                nc.vector.tensor_copy(woh[:, k, :], wraw[k % 2][:]).then_inc(s_woh, 1)
                dve.wait_ge(s_woh, k + 1)
                nc.vector.tensor_tensor(wol[:, k, :], wraw[k % 2][:], woh[:, k, :].bitcast(F32), ALU.subtract).then_inc(s_wol, 1)
            low_split(1, 1)
            normalise(0, 0)
            first = chain.count
            with dve.Fori(0, VIS - 1) as v:
                chain.loop(v, 6)
                step(v * 2 + 1, 1)
                step(v * 2 + 2, 0)
            chain.end(VIS - 1, 6, first)
            step(C - 1, 1, True)
            take(C)
    return sems


R = 32
I = 2752
IT = -(-I // P)
Q_ZERO, Q_STEP, LR_SCALE = 7.5, 0.005, 0.02
CH = 512
NCH = TOK // CH


def gate_up(nc, qgu, sgu, bgu, da, x2_hi, x2_lo, low, hid_dram, inner_st):
    sems = []
    with ExitStack() as st:
        def sb(name, shape, dt=F32):
            return st.enter_context(nc.sbuf_tensor(name, shape, dt))

        def sem(name):
            sems.append(nc.alloc_semaphore(name))
            return sems[-1]

        two = range(2)
        qraw = [sb(f"q_raw{s}", [P, 2, D], I32) for s in two]
        q16 = [sb(f"q_f16{s}", [P, 2, D], F16) for s in two]
        braw = [sb(f"b_raw{s}", [P, 2, P]) for s in two]
        bst = [sb(f"b_stack{s}", [P, 2, P], F32R) for s in two]
        scl = sb("gu_scale", [P, 2, IT])
        lraw = sb("low_raw", [P, 2, TOK])
        lst = sb("low_stack", [P, 2, TOK], F32R)
        araw, a_st = [sb(f"a_raw{s}", [P, R]) for s in two], [sb(f"a_split{s}", [P, 2, R], F32R) for s in two]
        hs_hi, hs_lo = ([sb(f"{n}{c}", [P, CH], F32R) for c in two] for n in ("hid_hi", "hid_lo"))
        inner = sb("inner_sum", [2 * R, TOK])
        lsb = [sb(f"low_term{c}", [P, 2, CH]) for c in two]
        gsb, usb, ssb = ([sb(f"{n}{c}", [P, CH]) for c in two] for n in ("gate", "up", "silu"))
        hid = [sb(f"hid{s}", [P, TOK]) for s in two]
        ps_m = [st.enter_context(nc.psum_tensor(f"e_main{c}", [P, 2, CH], F32)) for c in two]
        ps_l = st.enter_context(nc.psum_tensor("e_low", [P, 2, CH], F32))
        ps_i = [st.enter_context(nc.psum_tensor(f"e_inner{c}", [2 * R, CH], F32)) for c in two]
        s_passed = sem("e_passed")
        s_scl, s_scl2, s_lraw, s_lst, s_dve = sem("e_scl"), sem("e_scl2"), sem("e_lraw"), sem("e_lst"), sem("e_dve")
        s_load, s_q, s_b, s_read, s_out = ([sem(f"e_{n}{s}") for s in two] for n in ("load", "q", "b", "read", "out"))
        s_main, s_gate, s_silu, s_up, s_hid, s_hi, s_lo, s_inner, s_add = (
            [sem(f"e_{n}{s}") for s in two] for n in ("main", "gate", "silu", "up", "hid", "hi", "lo", "inner", "add"))
        s_low, s_lsb, s_zero, s_moved, s_end = (sem("e_" + n) for n in ("low", "lsb", "zero", "moved", "end"))
        s_a = [sem(f"e_a{s}") for s in two]
        PER = NCH // 2
        start_free(nc, [*s_q, *s_b, *s_read, *s_up, s_lsb, *s_hid, *s_silu, *s_a, *s_add, s_lo[1]], 1)
        start_free(nc, [*s_out], 16)
        nc.all_engine_barrier()
        block = st.enter_context(nc.Block())

        @block.sync
        def _(sp):
            for m in two:
                for g in range(4):
                    sp.dma_start(lraw[R * g:R * g + R, m, :], low[R * m:R * m + R, :]).then_inc(s_lraw, 16)
            sp.dma_start(scl[:], sgu).then_inc(s_scl, 16)
            with sp.Fori(0, IT // 2) as v:
                for s in two:
                    sp.wait_ge(s_q[s], v + 1)
                    sp.wait_ge(s_b[s], v + 1)
                    sp.wait_ge(s_a[s], v + 1)
                    sp.dma_start(qraw[s][:], qgu[bass.ds(v * 2 + s, 1), :, :, :].rearrange("o p m n -> (o p) m n")).then_inc(s_load[s], 16)
                    sp.dma_start(braw[s][:], bgu[bass.ds(v * 2 + s, 1), :, :, :].rearrange("o p m n -> (o p) m n")).then_inc(s_load[s], 16)
                    sp.dma_start(araw[s][:], da[:, bass.ds(v * 2 + s, 1), :].rearrange("p o r -> p (o r)")).then_inc(s_load[s], 16)
            for m in two:
                for g in range(4):
                    for b in two:
                        sp.wait_ge(s_add[b], PER * IT + 1 + b)
                    sp.dma_start(lraw[R * g:R * g + R, m, :], inner[R * m:R * m + R, :]).then_inc(s_moved, 16)

        @block.gpsimd
        def _(pool):
            with pool.Fori(0, IT // 2) as v:
                for s in two:
                    apart(pool, s_passed, (s_load[s], v * 48 + 48), (s_read[s], v + 1))
                    nc.gpsimd.tensor_scalar(q16[s][:], qraw[s][:], Q_ZERO, None, ALU.subtract).then_inc(s_q[s], 1)

        @block.tensor
        def _(pe):
            def inner_product(b, s, n):
                pe.wait_ge(s_lo[b], n + 1)
                pe.wait_ge(s_add[b], n + 1)
                nc.tensor.matmul(ps_i[b][:], a_st[s][:, :, :], hs_hi[b][:], start=True, stop=False)
                nc.tensor.matmul(ps_i[b][:], a_st[s][:, :, :], hs_lo[b][:], start=False, stop=True).then_inc(s_inner[b], 1)

            pe.wait_ge(s_zero, 4)
            with pe.Fori(0, IT // 2) as v:
                for s in two:
                    pe.wait_ge(s_q[s], v + 2)
                    for c in range(NCH):
                        b, n = c % 2, v * 2 * PER + s * PER + c // 2
                        tok = slice(c * CH, (c + 1) * CH)
                        pe.wait_ge(s_up[b], n + 1)
                        for m in two:
                            for k in range(KT):
                                w = q16[s][:, m, k * P:(k + 1) * P]
                                nc.tensor.matmul(ps_m[b][:, m, :], w, x2_hi[:, k, tok], start=(k == 0), stop=False)
                                last = nc.tensor.matmul(ps_m[b][:, m, :], w, x2_lo[:, k, tok], start=False, stop=(k == KT - 1))
                        last.then_inc(s_main[b], 1)
                        pe.wait_ge(s_b[s], v + 2)
                        pe.wait_ge(s_lst, 1)
                        pe.wait_ge(s_lsb, (v * 2 + s) * NCH + c + 1)
                        first = nc.tensor.matmul(ps_l[:, 0, :], bst[s][:, 0, :], lst[:, 0, tok], start=True, stop=True)
                        if c == NCH - 1:
                            first.then_inc(s_read[s], 1)
                        nc.tensor.matmul(ps_l[:, 1, :], bst[s][:, 1, :], lst[:, 1, tok], start=True, stop=True).then_inc(s_low, 1)
                        if c == 1:
                            pe.wait_ge(s_a[s], v + 2)
                        inner_product(1 - b, 1 - s if c == 0 else s, n)
            inner_product(1, 1, IT * PER)

        @block.scalar
        def _(act):
            with act.Fori(0, IT // 2) as v:
                for s in two:
                    for c in range(NCH):
                        b, n = c % 2, v * 2 * PER + s * PER + c // 2
                        act.wait_ge(s_low, (v * 2 + s) * NCH + c + 1)
                        act.wait_ge(s_up[b], n + 1)
                        nc.scalar.activation(lsb[b][:], ps_l[:], ACT.Copy, scale=LR_SCALE).then_inc(s_lsb, 1)
                        act.wait_ge(s_gate[b], n + 1)
                        act.wait_ge(s_hid[b], n + 1)
                        nc.scalar.activation(ssb[b][:], gsb[b][:], ACT.Silu).then_inc(s_silu[b], 1)
                        act.wait_ge(s_hid[b], n + 2)
                        nc.scalar.activation(hs_hi[b][:], hid[s][:, c * CH:(c + 1) * CH], ACT.Copy).then_inc(s_hi[b], 1)
                    act.wait_ge(s_hid[0], v * 2 * PER + (s + 1) * PER + 1)
                    act.wait_ge(s_hid[1], v * 2 * PER + (s + 1) * PER + 1)
                    act.dma_start(hid_dram[bass.ds(v * 2 + s, 1), :, :].rearrange("o p t -> (o p) t"), hid[s][:]).then_inc(s_out[s], 16)
            for s in two:
                act.wait_ge(s_out[s], 16 * (IT // 2) + 16)

        @block.vector
        def _(dve):
            chain = Chain(dve, s_dve)
            tt = nc.vector.tensor_tensor

            def add_inner(b, c, n):
                dve.wait_ge(s_inner[b], n + 1)
                tok = slice(c * CH, (c + 1) * CH)
                tt(inner[:, tok], inner[:, tok], ps_i[b][:], ALU.add).then_inc(s_add[b], 1)

            nc.vector.memset(a_st[1][:].bitcast(F32), 0.0).then_inc(s_zero, 1)
            nc.vector.memset(hs_hi[1][:].bitcast(F32), 0.0).then_inc(s_zero, 1)
            nc.vector.memset(hs_lo[1][:].bitcast(F32), 0.0).then_inc(s_zero, 1)
            nc.vector.memset(inner[:], 0.0).then_inc(s_zero, 1)
            dve.wait_ge(s_zero, 4)
            dve.wait_ge(s_scl, 16)
            nc.vector.tensor_scalar(scl[:], scl[:], Q_STEP, None, ALU.mult).then_inc(s_scl2, 1)
            dve.wait_ge(s_scl2, 1)
            dve.wait_ge(s_lraw, 16 * 8)
            chain.after(nc.vector.tensor_copy(lst[:], lraw[:]))
            tt(lst[64:P, :, :], lraw[64:P, :, :], lst[64:P, :, :].bitcast(F32), ALU.subtract).then_inc(s_lst, 1)
            first = chain.count
            with dve.Fori(0, IT // 2) as v:
                chain.loop(v, 2 * 3)
                for s in two:
                    dve.wait_ge(s_load[s], v * 48 + 48)
                    chain.after(nc.vector.tensor_copy(bst[s][:], braw[s][:]))
                    for g in (1, 3):
                        r = slice(R * g, R * g + R)
                        last = tt(bst[s][r, :, :], braw[s][r, :, :], bst[s][r, :, :].bitcast(F32), ALU.subtract)
                        if g == 1:
                            chain.mark(last)
                    last.then_inc(s_b[s], 1)
                    chain.after(nc.vector.tensor_copy(a_st[s][:, 0, :], araw[s][:]))
                    tt(a_st[s][:, 1, :], araw[s][:], a_st[s][:, 0, :].bitcast(F32), ALU.subtract).then_inc(s_a[s], 1)
                    for c in range(NCH):
                        b, n = c % 2, v * 2 * PER + s * PER + c // 2
                        dve.wait_ge(s_main[b], n + 1)
                        dve.wait_ge(s_lsb, (v * 2 + s) * NCH + c + 2)
                        dve.wait_ge(s_silu[b], n + 1)
                        for m, out, done in ((0, gsb, s_gate), (1, usb, s_up)):
                            nc.vector.scalar_tensor_tensor(out[b][:], ps_m[b][:, m, :], scl[:, m, bass.ds(v * 2 + s, 1)], lsb[b][:, m, :],
                                                           ALU.mult, ALU.add).then_inc(done[b], 1)
                        dve.wait_ge(s_silu[b], n + 2)
                        dve.wait_ge(s_up[b], n + 2)
                        if c == 0:
                            dve.wait_ge(s_out[s], v * 16 + 16)
                        tt(hid[s][:, c * CH:(c + 1) * CH], ssb[b][:], usb[b][:], ALU.mult).then_inc(s_hid[b], 1)
                        add_inner(1 - b, (c - 1) % NCH, n)
                        dve.wait_ge(s_hi[b], n + 1)
                        tt(hs_lo[b][:], hid[s][:, c * CH:(c + 1) * CH], hs_hi[b][:].bitcast(F32), ALU.subtract).then_inc(s_lo[b], 1)
            chain.end(IT // 2, 6, first)
            add_inner(1, NCH - 1, IT * PER)
            dve.wait_ge(s_moved, 16 * 8)
            chain.after(tt(lraw[:, 0, :], lraw[:, 0, :], lraw[:, 1, :], ALU.add))
            chain.after(nc.vector.tensor_copy(inner_st[:], lraw[:, 0, :]))
            tt(inner_st[64:P, :], lraw[64:P, 0, :], inner_st[64:P, :].bitcast(F32), ALU.subtract).then_inc(s_end, 1)
            dve.wait_ge(s_end, 1)
    return sems


HALF = 512
QS = 4


def down(nc, qd, sd, db, inner_st, hid_dram, h1_dram, out):
    sems = []
    with ExitStack() as st:
        def sb(name, shape, dt=F32):
            return st.enter_context(nc.sbuf_tensor(name, shape, dt))

        def sem(name):
            sems.append(nc.alloc_semaphore(name))
            return sems[-1]

        two = range(2)
        qraw = [sb(f"f_qraw{s}", [P, D], I32) for s in range(QS)]
        qd_sb = sb("f_levels", [P, IT, D], F32R)
        braw, b_st = sb("f_braw", [P, D]), sb("f_b", [P, D], F32R)
        scl = sb("f_scale", [P, D])
        hraw = sb("f_hraw", [P, IT, P])
        hh, hl = ([sb(f"f_{n}{s}", [P, IT, P], F32R) for s in two] for n in ("hh", "hl"))
        h1 = sb("f_h1", [P, D])
        lrt = sb("f_lrt", [P, D])
        y = sb("f_y", [P, D])
        pt = sb("f_pt", [P, P], F32R)
        acc = [st.enter_context(nc.psum_tensor(f"f_acc{s}", [P, 2, HALF], F32)) for s in two]
        ps_l = st.enter_context(nc.psum_tensor("f_lr", [P, 2, HALF], F32))
        s_const, s_b, s_scl, s_dve = (sem("f_s" + n) for n in ("const", "b", "scl", "dve"))
        s_qload = [sem(f"f_sqload{s}") for s in range(QS)]
        s_q = sem("f_sq")
        s_h, s_hh, s_hl, s_acc, s_pt, s_lr, s_lrt, s_h1, s_sum, s_scaled, s_y, s_out = (
            sem("f_s" + n) for n in ("h", "hh", "hl", "acc", "pt", "lr", "lrt", "h1", "sum", "scaled", "y", "out"))
        VIS = C // 2
        start_free(nc, [s_scaled, s_lrt, s_y, s_sum], 1)
        start_free(nc, [s_out], 16)
        nc.all_engine_barrier()
        block = st.enter_context(nc.Block())

        def run(first, step, last, eng):
            first()
            with eng.Fori(0, VIS - 1) as v:
                step(v * 2 + 1, 1)
                step(v * 2 + 2, 0)
            step(C - 1, 1)
            last()

        @block.sync
        def _(sp):
            sp.dma_start(hraw[:], hid_dram.rearrange("i p t -> p i t")[:, :, 0:P]).then_inc(s_h, 16)
            for i in range(IT):
                if i >= QS:
                    sp.wait_ge(s_q, i - QS + 1)
                sp.dma_start(qraw[i % QS][:], qd[:, i, :]).then_inc(s_qload[i % QS], 16)
            with sp.Fori(0, C) as n:
                sp.wait_ge(s_y, n + 2)
                sp.dma_start(out[bass.ds(n, 1), :, :].rearrange("o t d -> (o t) d"), y[:]).then_inc(s_out, 16)
            sp.wait_ge(s_out, 16 * C + 16)

        @block.gpsimd
        def _(pool):
            pool.wait_ge(s_scl, 1)
            with pool.Fori(0, C) as n:
                pool.wait_ge(s_sum, n + 1)
                pool.dma_start(h1[:], h1_dram[bass.ds(n, 1), :, :].rearrange("o t d -> (o t) d")).then_inc(s_h1, 16)
                pool.wait_ge(s_h1, n * 16 + 16)
                pool.wait_ge(s_lrt, n + 2)
                nc.gpsimd.tensor_tensor(lrt[:], lrt[:], h1[:], ALU.add).then_inc(s_sum, 1)

        @block.tensor
        def _(pe):
            def main(s, lo, hi, first):
                for i in range(lo, hi):
                    if first:
                        pe.wait_ge(s_q, i + 1)
                    for part in (hh, hl):
                        for b in two:
                            last = nc.tensor.matmul(acc[s][:, b, :], part[s][:, i, :], qd_sb[:, i, b * HALF:(b + 1) * HALF],
                                                    start=(i == 0 and part is hh), stop=(i == IT - 1 and part is hl))
                return last

            def low_rank(n):
                pe.wait_ge(s_pt, n)
                pe.wait_ge(s_lrt, n)
                for b in two:
                    last = nc.tensor.matmul(ps_l[:, b, :], pt[:], b_st[:, b * HALF:(b + 1) * HALF], start=True, stop=True)
                last.then_inc(s_lr, 1)

            def step(n, s, first=False):
                pe.wait_ge(s_hl, n + 1)
                if not first:
                    pe.wait_ge(s_scaled, n)
                main(s, 0, IT // 2, first)
                if not first:
                    low_rank(n)
                main(s, IT // 2, IT, first).then_inc(s_acc, 1)

            def last():
                low_rank(C)

            pe.wait_ge(s_b, 1)
            run(lambda: step(0, 0, True), step, last, pe)

        @block.scalar
        def _(act):
            def split(n, s):
                act.wait_ge(s_h, n * 16 + 16)
                nc.scalar.activation(hh[s][:], hraw[:], ACT.Copy).then_inc(s_hh, 1)

            def low_terms(n):
                nc.scalar.activation(pt[:], inner_st[:, bass.ds((n - 1) * P, P)].bitcast(F32), ACT.Copy).then_inc(s_pt, 1)
                act.wait_ge(s_lr, n)
                act.wait_ge(s_y, n)
                nc.scalar.activation(lrt[:], ps_l[:].rearrange("p b n -> p (b n)"), ACT.Copy, scale=LR_SCALE).then_inc(s_lrt, 1)

            def load(n):
                act.wait_ge(s_hl, n)
                act.dma_start(hraw[:], hid_dram.rearrange("i p t -> p i t")[:, :, bass.ds(n * P, P)]).then_inc(s_h, 16)

            def step(n, s):
                load(n + 1)
                act.wait_ge(s_acc, n)
                split(n + 1, 1 - s)
                low_terms(n)

            act.dma_start(scl[:], sd).then_inc(s_const, 16)
            act.dma_start(braw[:], db).then_inc(s_const, 16)
            split(0, 0)
            load(1)
            split(1, 1)
            with act.Fori(0, VIS - 1) as v:
                step(v * 2 + 1, 1)
                step(v * 2 + 2, 0)
            low_terms(C - 1)
            low_terms(C)

        @block.vector
        def _(dve):
            chain = Chain(dve, s_dve)
            tt = nc.vector.tensor_tensor

            def low_split(n, s):
                dve.wait_ge(s_hh, n + 1)
                tt(hl[s][:], hraw[:], hh[s][:].bitcast(F32), ALU.subtract).then_inc(s_hl, 1)

            def step(n, s, end=False):
                if not end:
                    low_split(n + 1, 1 - s)
                scale_sums(n, 1 - s)

            def scale_sums(n, s):
                dve.wait_ge(s_acc, n)
                dve.wait_ge(s_out, (n - 1) * 16 + 16)
                tt(y[:], acc[s][:].rearrange("p b n -> p (b n)"), scl[:], ALU.mult).then_inc(s_scaled, 1)
                dve.wait_ge(s_scaled, n + 1)
                dve.wait_ge(s_sum, n + 1)
                tt(y[:], y[:], lrt[:], ALU.add).then_inc(s_y, 1)

            low_split(0, 0)
            dve.wait_ge(s_const, 32)
            nc.vector.tensor_scalar(scl[:], scl[:], Q_STEP, None, ALU.mult).then_inc(s_scl, 1)
            chain.after(nc.vector.tensor_copy(b_st[:], braw[:]))
            for g in (1, 3):
                r = slice(R * g, R * g + R)
                last = tt(b_st[r, :], braw[r, :], b_st[r, :].bitcast(F32), ALU.subtract)
            last.then_inc(s_b, 1)
            for i in range(IT):
                dve.wait_ge(s_qload[i % QS], 16 * (i // QS + 1))
                nc.vector.tensor_scalar(qd_sb[:, i, :], qraw[i % QS][:], Q_ZERO, None, ALU.subtract).then_inc(s_q, 1)
            low_split(1, 1)
            with dve.Fori(0, VIS - 1) as v:
                step(v * 2 + 1, 1)
                step(v * 2 + 2, 0)
            step(C - 1, 1, True)
            scale_sums(C, 1)
    return sems


def retire(nc, sems):
    nc.clear_and_free_semaphores(sems)
    nc.all_engine_barrier()


def vit_tower(nc, t, out):
    h0_dram = nc.dram_tensor("h0_tokens", (C, H, D), F32, kind="Internal").ap()
    o_dram = nc.dram_tensor("o_features", (KT, P, TOK), F32, kind="Internal").ap()
    h1_dram = nc.dram_tensor("h1_tokens", (C, H, D), F32, kind="Internal").ap()
    hid_dram = nc.dram_tensor("hidden", (IT, P, TOK), F32, kind="Internal").ap()
    with ExitStack() as whole:
        with ExitStack() as st:
            ident = st.enter_context(nc.sbuf_tensor("ident", [P, P], F32))
            mask = st.enter_context(nc.sbuf_tensor("causal_mask", [P, P], F32))
            s_const = st.enter_context(nc.semaphore("const_loaded"))
            with nc.Block() as block:
                @block.sync
                def _(sp):
                    sp.dma_start(ident[:], t["ident"]).then_inc(s_const, 16)
                    sp.dma_start(mask[:], t["mask"]).then_inc(s_const, 16)
                    sp.wait_ge(s_const, 32)
            with nc.sbuf_tensor("x0t", [P, KT * C, H], F32, side="right") as x0t:
                retire(nc, ssm_kernel(nc, t["ssm"], t["c_re"], t["c_im"], x0t))
                x_hi = st.enter_context(nc.sbuf_tensor("x_hi", [P, KT, TOK], F16))
                x_lo = st.enter_context(nc.sbuf_tensor("x_lo", [P, KT, TOK], F16))
                retire(nc, first_norm(nc, x0t, h0_dram, x_hi, x_lo, ident))
            retire(nc, attention(nc, t["w_qkv"], t["b_qkv"], x_hi, x_lo, ident, mask, o_dram))
            low = st.enter_context(nc.sbuf_tensor("low_rank", [2 * R, TOK], F32))
            retire(nc, project_and_norm(nc, t["w_o"], t["b_o"], t["gu_a"], o_dram, h0_dram, h1_dram, x_hi, x_lo, low, ident))
            inner_st = whole.enter_context(nc.sbuf_tensor("inner_stack", [P, TOK], F32R, side="right"))
            retire(nc, gate_up(nc, t["gu_q"], t["gu_scale"], t["gu_b"], t["down_a"], x_hi, x_lo, low, hid_dram, inner_st))
        down(nc, t["down_q"], t["down_scale"], t["down_b"], inner_st, hid_dram, h1_dram, out)


def layouts(v):
    import numpy as np

    def padded(a, axis):
        room = list(a.shape)
        room[axis] = IT * P - a.shape[axis]
        return np.concatenate([a, np.zeros(room, a.dtype)], axis)

    def twice(a):
        return np.concatenate([a, a], 0)

    f = {n: np.asarray(a) for n, a in v.items()}
    x, b = f["x"], f["L0_tok_B"]
    q_gu = np.stack([padded(f["L0_ffn_gate_q"], 0), padded(f["L0_ffn_up_q"], 0)])
    s_gu = np.stack([padded(f["L0_ffn_gate_scale"], 0), padded(f["L0_ffn_up_scale"], 0)])
    b_gu = np.stack([padded(f["L0_ffn_gate_B"], 1), padded(f["L0_ffn_up_B"], 1)])
    wqkv = np.stack([f["L0_attn_Wq"], f["L0_attn_Wk"], f["L0_attn_Wv"]])
    bqkv = np.stack([f["L0_attn_bq"], f["L0_attn_bk"], f["L0_attn_bv"]])
    a_gu = np.concatenate([f["L0_ffn_gate_A"], f["L0_ffn_up_A"]], 1)
    at = np.arange(P)
    out = {
        "ssm": np.stack([np.broadcast_to(f["L0_tok_log_dt"], (P, H)), twice(f["L0_tok_inv_A_real"].T),
                         twice(f["L0_tok_A_imag"].T), twice(b[..., 0].T), twice(b[..., 1].T)], 1),
        "c_re": twice(x[..., 0].transpose(2, 1, 0)),
        "c_im": twice(x[..., 1].transpose(2, 1, 0)),
        "w_qkv": wqkv.reshape(3, KT, P, KT, P).transpose(1, 4, 0, 3, 2).reshape(KT, P, 3, D),
        "b_qkv": bqkv.reshape(3, KT, P).transpose(2, 0, 1),
        "w_o": f["L0_attn_Wo"].T.reshape(KT, P, D).transpose(1, 0, 2),
        "b_o": np.broadcast_to(f["L0_attn_bo"], (P, D)),
        "gu_a": a_gu.reshape(KT, P, 2 * R).transpose(1, 0, 2),
        "gu_q": q_gu.reshape(2, IT, P, KT, P).transpose(1, 4, 0, 3, 2).reshape(IT, P, 2, D),
        "gu_scale": s_gu.reshape(2, IT, P).transpose(2, 0, 1),
        "gu_b": np.tile(b_gu.reshape(2, R, IT, P).transpose(2, 1, 0, 3), (1, 4, 1, 1)),
        "down_q": padded(f["L0_ffn_down_q"], 1).T.reshape(IT, P, D).transpose(1, 0, 2),
        "down_scale": np.broadcast_to(f["L0_ffn_down_scale"], (P, D)),
        "down_a": padded(f["L0_ffn_down_A"], 0).reshape(IT, P, R).transpose(1, 0, 2),
        "down_b": np.tile(f["L0_ffn_down_B"], (4, 1)),
        "ident": np.eye(P, dtype=np.float32),
        "mask": np.where(at[:, None] >= at[None, :], 0.0, -3e38).astype(np.float32),
    }
    return {n: np.ascontiguousarray(a) for n, a in out.items()}


def kernel(**inputs):
    import numpy as np
    import concourse.bacc as bacc
    from concourse.bass_utils import run_bass_kernel_spmd

    arrays = layouts(inputs)
    nc = bacc.Bacc("TRN2", target_bir_lowering=False, num_devices=1)
    tensors = {n: nc.dram_tensor("in_" + n, a.shape, mybir.dt.from_np(a.dtype), kind="ExternalInput").ap()
               for n, a in arrays.items()}
    out = nc.dram_tensor("out_tokens", (C, H, D), F32, kind="ExternalOutput").ap()
    vit_tower(nc, tensors, out)
    r = run_bass_kernel_spmd(nc, [{"in_" + n: a for n, a in arrays.items()}], core_ids=[0])
    return np.asarray(r.results[0]["out_tokens"])
```

```python
import math
from contextlib import ExitStack

import concourse.bass as bass
from concourse import mybir

F32 = mybir.dt.float32
F32R = mybir.dt.float32r
F16 = mybir.dt.float16
BF16 = mybir.dt.bfloat16
I32 = mybir.dt.int32
ALU = mybir.AluOpType
ACT = mybir.ActivationFunctionType
X = mybir.AxisListType.X

P = 128
C, H, N = 16, 128, 64
D = 1024
KT = D // P
TOK = C * H
MAGIC = 1.5 * 2.0 ** 23
TWO_PI = 6.2831845
EPS = 1e-5


def bc(ap, n, at):
    shape = list(ap.shape)
    shape.insert(at, n)
    return ap.unsqueeze(at).broadcast_to(shape)


def start_free(nc, sems, count):
    for sem in sems:
        nc.sync.sem_inc(sem, count)


def apart(eng, passed, *waits):
    for sem, value in waits:
        eng.wait_ge(sem, value)
    eng.sem_inc(passed, 1)


class Chain:

    def __init__(self, eng, sem):
        self.eng, self.sem, self.count, self.turn = eng, sem, 0, 0

    def loop(self, it, n):
        self.turn = it * n

    def end(self, turns, n, first):
        assert self.count - first == n, (self.count - first, n)
        self.count, self.turn = first + turns * n, 0

    def mark(self, ins):
        self.count += 1
        ins.then_inc(self.sem, 1)
        return self.count

    def now(self):
        return self.turn + self.count

    def wait(self):
        self.eng.wait_ge(self.sem, self.now())

    def after(self, ins):
        self.mark(ins)
        self.wait()


UH = 8
UNITS = H // UH
CUT = 3
TI, TJ = 8, 16
TAB = 2 * TI + TJ
LAG = 6


def ssm_and_norm(nc, ssm, cr, ci, h0_dram, xn_hi, xn_lo, ident):
    sems = []
    with ExitStack() as st:
        def sb(name, shape, dt=F32):
            return st.enter_context(nc.sbuf_tensor(name, shape, dt))

        def sem(name):
            sems.append(nc.alloc_semaphore(name))
            return sems[-1]

        two = range(2)
        par = sb("ssm_par", [P, 5, H])
        cre, cim = sb("c_re", [P, H, C]), sb("c_im", [P, H, C])
        t01 = sb("ssm_t01", [P, 2, H])
        t = [t01[:, 0, :], t01[:, 1, :]] + [sb(f"ssm_t{k}", [P, H]) for k in range(2, 12)]
        er, ek, ew = sb("exp_r", [P, 2, H]), sb("exp_k", [P, 2, H]), sb("exp_w", [P, 2, H], I32)
        steps = sb("table_steps", [P, TAB])
        half = [sb(f"half{k}", [P, 1]) for k in range(7)]
        phase, mag = sb("phase", [P, H, TAB]), sb("magnitude", [P, H, TAB])
        tab1, tab2 = sb("table1", [P, H, TAB]), sb("table2", [P, H, TAB])
        a1, a2, at = (sb(n, [P, H, TI]) for n in ("a1", "a2", "a_tmp"))
        phase_room = phase[:].rearrange("p h k -> p (h k)").rearrange("p (s n) -> p s n", n=UH * P)
        mag_room = mag[:].rearrange("p h k -> p (h k)").rearrange("p (s n) -> p s n", n=UH * P)
        w = [[phase_room[:, 2 * s + k, :] for k in two] for s in two]
        v = [mag_room[:, s, :] for s in two]
        v_second = mag_room[:, 2, :]
        xt = [sb(f"n_xt{s}", [P, KT * C, UH]) for s in two]
        tok = [sb(f"n_tok{s}", [P, D]) for s in two]
        nrm = [sb(f"n_nrm{s}", [P, D]) for s in two]
        stats = [sb(f"n_stats{s}", [P, 2, 6]) for s in two]
        mv = [sb(f"n_mv{s}", [P, 2]) for s in two]
        std = [sb(f"n_std{s}", [P, 1]) for s in two]
        rs = [sb(f"n_rs{s}", [P, 2]) for s in two]
        eps = sb("n_eps", [P, 1])
        ps = [st.enter_context(nc.psum_tensor(f"ssm_ps{s}", [P, UH, P], F32)) for s in two]
        pt = st.enter_context(nc.psum_tensor("n_pt", [P, KT, P], F32))
        pn = st.enter_context(nc.psum_tensor("n_pn", [P, KT, P], F32))

        s_in, s_c, s_const, s_dve, s_z, s_expm, s_turn0 = (sem("a_" + n) for n in ("in", "c", "const", "dve", "z", "expm", "turn0"))
        s_decay, s_mag, s_phase, s_trig, s_tab1, s_tab2, s_a, s_passed = (
            sem("a_" + n) for n in ("decay", "mag", "phase", "trig", "tab1", "tab2", "a", "passed"))
        s_v1, s_v, s_w, s_mm, s_ev, s_tr, s_tok, s_mv, s_std, s_rs, s_nrm, s_trn, s_hi, s_lo, s_out = (
            [sem(f"a_{n}{s}") for s in two]
            for n in ("v1", "v", "w", "mm", "ev", "tr", "tok", "mv", "std", "rs", "nrm", "trn", "hi", "lo", "out"))
        logdt, inva, aim, br, bi = (par[:, k, :] for k in range(5))
        VIS = UNITS // 2
        start_free(nc, [*s_v, *s_mm, *s_ev, *s_tr, *s_tok, *s_nrm, *s_trn, *s_lo], 1)
        start_free(nc, [*s_out], 16)
        nc.all_engine_barrier()
        block = st.enter_context(nc.Block())

        def four(room, n):
            return room.rearrange("p (h a b) -> p h a b", h=UH, b=n)

        def channels(n, s, start=0, end=UH):
            return bass.ds((n * 2 + s) * UH + start, end - start)

        def run(eng, stages, chain=None, marks=0):
            def iterations(n, known):
                for b in two:
                    for lag, work in stages:
                        d = b - lag
                        if not known or 0 <= 2 * n + d < UNITS:
                            work(n + d // 2, d % 2)

            for n in range(LAG // 2):
                iterations(n, True)
            before = chain.count if chain else 0
            with eng.Fori(0, VIS - LAG // 2) as n:
                if chain:
                    chain.loop(n, marks)
                iterations(n + LAG // 2, False)
            if chain:
                chain.end(VIS - LAG // 2, marks, before)
            for n in range(VIS, VIS + LAG // 2):
                iterations(n, True)

        @block.sync
        def _(sp):
            sp.dma_start(par[:], ssm).then_inc(s_in, 16)
            sp.dma_start(cre[:], cr).then_inc(s_c, 16)
            sp.dma_start(cim[:], ci).then_inc(s_c, 16)
            with sp.Fori(0, VIS) as n:
                for s in two:
                    sp.wait_ge(s_tok[s], n + 2)
                    sp.dma_start(h0_dram[:, channels(n, s), :], tok[s][:]).then_inc(s_out[s], 16)
            for s in two:
                sp.wait_ge(s_out[s], 16 * VIS + 16)

        @block.gpsimd
        def _(pool):
            for at_, count, step in ((0, TI, P), (TI, TI, TJ), (2 * TI, TJ, 1)):
                nc.gpsimd.iota(steps[:, at_:at_ + count], [[step, count]], base=0, channel_multiplier=0,
                               allow_small_or_imprecise_dtypes=True).then_inc(s_const, 1)
            pool.wait_ge(s_const, 3 + 15)
            pool.wait_ge(s_z, 1)
            nc.gpsimd.tensor_tensor(mag[:], bc(t[2][:], TAB, 2), bc(steps[:], H, 1), ALU.mult).then_inc(s_decay, 1)
            pool.wait_ge(s_trig, 5)
            pool.wait_ge(s_mag, 1)
            nc.gpsimd.tensor_tensor(tab2[:], tab2[:], mag[:], ALU.mult).then_inc(s_tab2, 1)
            pool.wait_ge(s_tab2, 1)
            pool.wait_ge(s_tab1, 1)
            pool.wait_ge(s_c, 32)

            def factors(n, s):
                pool.wait_ge(s_mm[s], n + 1)
                nc.gpsimd.tensor_tensor(four(v[s], TJ), bc(tab1[:, channels(n, s), TI:2 * TI], TJ, 3),
                                        bc(tab1[:, channels(n, s), 2 * TI:TAB], TI, 2), ALU.mult).then_inc(s_v1[s], 1)
                pool.wait_ge(s_a, 2)
                nc.gpsimd.tensor_tensor(four(w[s][0], C), bc(a1[:, channels(n, s), :], C, 3),
                                        bc(cre[:, channels(n, s), :], KT, 2), ALU.mult)
                hs = channels(n, s, 0, CUT)
                nc.gpsimd.tensor_tensor(four(w[s][1], C)[:, 0:CUT], bc(a2[:, hs, :], C, 3), bc(cim[:, hs, :], KT, 2),
                                        ALU.mult).then_inc(s_w[s], 1)

            run(pool, [(0, factors)])

        @block.tensor
        def _(pe):
            def product(n, s):
                pe.wait_ge(s_v[s], n + 2)
                pe.wait_ge(s_w[s], n * 2 + 2)
                pe.wait_ge(s_ev[s], n + 1)
                for h in range(UH):
                    cols = slice(h * P, (h + 1) * P)
                    for k in two:
                        last = nc.tensor.matmul(ps[s][:, h, :], v[s][:, cols], w[s][k][:, cols], start=(k == 0), stop=(k == 1))
                last.then_inc(s_mm[s], 1)

            def to_tokens(n, s):
                pe.wait_ge(s_ev[s], n + 2)
                pe.wait_ge(s_tok[1 - s], n + 1 + s)
                for i in range(KT):
                    last = nc.tensor.transpose(pt[:, i, :], xt[s][:, i * C:(i + 1) * C, :].rearrange("p c h -> p (c h)"), ident[:])
                last.then_inc(s_tr[s], 1)

            def to_features(n, s):
                pe.wait_ge(s_nrm[s], n + 2)
                pe.wait_ge(s_lo[1 - s], n + 1 + s)
                for i in range(KT):
                    last = nc.tensor.transpose(pn[:, i, :], nrm[s][:, i * P:(i + 1) * P], ident[:])
                last.then_inc(s_trn[s], 1)

            run(pe, [(5, to_features), (1, product), (2, to_tokens)])

        @block.scalar
        def _(act):
            act.wait_ge(s_z, 1)
            nc.scalar.activation(t[4][:], t[2][:], ACT.Exp).then_inc(s_expm, 1)
            nc.scalar.activation(t[5][:], t[2][:], ACT.Tanh, scale=0.5).then_inc(s_expm, 1)
            act.wait_ge(s_decay, 1)
            nc.scalar.activation(mag[:], mag[:], ACT.Exp).then_inc(s_mag, 1)
            act.wait_ge(s_phase, 3)
            act.wait_ge(s_const, 3 + 15)
            i, j1, j0 = slice(0, TI), slice(TI, 2 * TI), slice(2 * TI, TAB)
            quarter = half[5]
            nc.scalar.activation(tab1[:, :, 0:2 * TI], tab1[:, :, 0:2 * TI], ACT.Sin, scale=-TWO_PI, bias=quarter[:]).then_inc(s_trig, 1)
            nc.scalar.activation(tab1[:, :, j0], tab1[:, :, j0], ACT.Sin, scale=half[1][:], bias=half[3][:]).then_inc(s_trig, 1)
            nc.scalar.activation(tab2[:, :, i], phase[:, :, i], ACT.Sin, scale=TWO_PI).then_inc(s_trig, 1)
            nc.scalar.activation(tab2[:, :, j1], phase[:, :, j1], ACT.Sin, scale=half[1][:]).then_inc(s_trig, 1)
            nc.scalar.activation(tab2[:, :, j0], tab2[:, :, j0], ACT.Sin, scale=half[2][:], bias=half[4][:]).then_inc(s_trig, 1)

            def columns(n, s):
                act.wait_ge(s_mm[s], n + 2)
                act.wait_ge(s_tr[s], n + 1)
                nc.scalar.activation(xt[s][:], ps[s][:].rearrange("p h m -> p m h"), ACT.Copy).then_inc(s_ev[s], 1)

            def deviation(n, s):
                act.wait_ge(s_mv[s], n + 1)
                nc.scalar.activation(std[s][:], mv[s][:, 1:2], ACT.Sqrt, bias=eps[:]).then_inc(s_std[s], 1)

            def tokens(n, s):
                act.wait_ge(s_tr[s], n + 2)
                act.wait_ge(s_nrm[s], n + 1)
                act.wait_ge(s_out[s], n * 16 + 16)
                nc.scalar.activation(tok[s][:].rearrange("p (i j) -> p i j", j=P), pt[:], ACT.Copy).then_inc(s_tok[s], 1)

            def normalise(n, s):
                apart(act, s_passed, (s_rs[s], n + 1), (s_trn[s], n + 1))
                nc.scalar.activation(nrm[s][:], tok[s][:], ACT.Identity, scale=rs[s][:, 0:1], bias=rs[s][:, 1:2]).then_inc(s_nrm[s], 1)

            def high(n, s):
                apart(act, s_passed, (s_trn[s], n + 2))
                nc.scalar.activation(xn_hi[:].rearrange("p k (c h) -> p k c h", h=H)[:, :, :, channels(n, s)],
                                     pn[:].rearrange("p k (c h) -> p k c h", h=UH), ACT.Copy).then_inc(s_hi[s], 1)

            run(act, [(2, columns), (4, deviation), (3, tokens), (4, normalise), (5, high)])

        @block.vector
        def _(dve):
            chain = Chain(dve, s_dve)
            tt, ts = nc.vector.tensor_tensor, nc.vector.tensor_scalar
            nc.vector.memset(eps[:], EPS).then_inc(s_const, 1)
            for k, (above, below) in enumerate(((-1.0, 1.0), (-TWO_PI, TWO_PI), (TWO_PI, -TWO_PI), (math.pi / 2, 0.0),
                                                (0.0, math.pi / 2), (math.pi / 2, math.pi / 2), (1.0, -1.0))):
                nc.vector.memset(half[k][0:N, :], above).then_inc(s_const, 1)
                nc.vector.memset(half[k][N:P, :], below).then_inc(s_const, 1)
            dve.wait_ge(s_in, 16)
            chain.after(ts(er[:], par[:, 0:2, :], -87.0, 88.0, ALU.max, ALU.min))
            chain.after(ts(ek[:], er[:], 1.0 / math.log(2.0), None, ALU.mult))
            chain.after(ts(ek[:], ek[:], MAGIC, MAGIC, ALU.add, ALU.subtract))
            chain.mark(ts(ew[:], ek[:], 127.0, 2.0 ** 23, ALU.add, ALU.mult))
            chain.after(nc.vector.scalar_tensor_tensor(er[:], ek[:], -0.693359375, er[:], ALU.mult, ALU.add))
            chain.after(nc.vector.scalar_tensor_tensor(er[:], ek[:], 2.12194440e-4, er[:], ALU.mult, ALU.add))
            chain.after(ts(ek[:], er[:], 1 / math.factorial(7), None, ALU.mult))
            for k in range(6, 0, -1):
                chain.after(nc.vector.scalar_tensor_tensor(ek[:], ek[:], 1 / math.factorial(k), er[:], ALU.add, ALU.mult))
            chain.after(nc.vector.scalar_tensor_tensor(t01[:], ek[:], 1.0, ew[:].bitcast(F32), ALU.add, ALU.mult))
            chain.after(tt(t[2][:], t[1][:], t[0][:], ALU.mult))
            chain.after(ts(t[2][:], t[2][:], -1.0, None, ALU.mult))
            chain.after(tt(t[3][:], aim, t[0][:], ALU.mult))
            ts(t[3][:], t[3][:], 1.0 / (2 * math.pi), None, ALU.mult).then_inc(s_z, 1)
            dve.wait_ge(s_z, 1)
            dve.wait_ge(s_const, 3 + 15)

            chain.mark(nc.vector.tensor_copy(t[6][:], t[3][:]))
            chain.after(tt(phase[:], bc(t[3][:], TAB, 2), bc(steps[:], H, 1), ALU.mult))
            chain.after(ts(tab1[:], phase[:], MAGIC, MAGIC, ALU.add, ALU.subtract))
            tt(phase[:], phase[:], tab1[:], ALU.subtract).then_inc(s_phase, 1)
            dve.wait_ge(s_phase, 1)
            pair, j0 = slice(0, 2 * TI), slice(2 * TI, TAB)
            stt = nc.vector.scalar_tensor_tensor
            stt(tab1[:, :, pair], phase[:, :, pair], -1.0, phase[:, :, pair], ALU.mult, ALU.max).then_inc(s_phase, 1)
            chain.mark(stt(tab1[:, :, j0], phase[:, :, j0], half[0][:], phase[:, :, j0], ALU.mult, ALU.max))
            stt(tab2[:, :, j0], phase[:, :, j0], half[6][:], phase[:, :, j0], ALU.mult, ALU.max).then_inc(s_phase, 1)
            ts(t[8][:], t[6][:], MAGIC, MAGIC, ALU.add, ALU.subtract).then_inc(s_turn0, 1)
            dve.wait_ge(s_turn0, 1)
            chain.after(tt(t[6][:], t[6][:], t[8][:], ALU.subtract))
            chain.after(ts(t[6][:], t[6][:], math.pi, None, ALU.mult))
            y, y2, sin, cos = t[6], t[8], t[7], t[9]
            chain.after(tt(y2[:], y[:], y[:], ALU.mult))
            chain.mark(ts(sin[:], y2[:], 1 / math.factorial(13), None, ALU.mult))
            chain.after(ts(cos[:], y2[:], 1 / math.factorial(12), None, ALU.mult))
            for k in range(5, 0, -1):
                chain.mark(nc.vector.scalar_tensor_tensor(sin[:], sin[:], (-1) ** k / math.factorial(2 * k + 1), y2[:], ALU.add, ALU.mult))
                chain.after(nc.vector.scalar_tensor_tensor(cos[:], cos[:], (-1) ** k / math.factorial(2 * k), y2[:], ALU.add, ALU.mult))
            chain.mark(ts(cos[:], cos[:], 1.0, None, ALU.add))
            chain.after(nc.vector.scalar_tensor_tensor(sin[:], sin[:], 1.0, y[:], ALU.add, ALU.mult))
            chain.after(tt(y[:], sin[:], cos[:], ALU.mult))
            chain.after(ts(y[:], y[:], 2.0, None, ALU.mult))
            dve.wait_ge(s_expm, 2)
            chain.after(ts(t[8][:], t[4][:], 1.0, None, ALU.add))
            chain.after(tt(t[8][:], t[8][:], t[5][:], ALU.mult))
            chain.after(tt(t[7][:], t[7][:], t[7][:], ALU.mult))
            chain.after(tt(t[7][:], t[7][:], t[4][:], ALU.mult))
            chain.after(ts(t[7][:], t[7][:], -2.0, None, ALU.mult))
            chain.mark(tt(t[6][:], t[6][:], t[4][:], ALU.mult))
            chain.after(tt(t[7][:], t[7][:], t[8][:], ALU.add))
            chain.mark(tt(t[8][:], br, t[7][:], ALU.mult))
            chain.mark(tt(t[9][:], bi, t[6][:], ALU.mult))
            chain.mark(tt(t[10][:], br, t[6][:], ALU.mult))
            chain.after(tt(t[11][:], bi, t[7][:], ALU.mult))
            chain.mark(tt(t[8][:], t[8][:], t[9][:], ALU.subtract))
            chain.after(tt(t[10][:], t[10][:], t[11][:], ALU.add))
            chain.mark(tt(t[4][:], t[1][:], t[1][:], ALU.mult))
            chain.mark(tt(t[5][:], aim, aim, ALU.mult))
            chain.mark(tt(t[6][:], t[8][:], t[1][:], ALU.mult))
            chain.mark(tt(t[7][:], t[10][:], aim, ALU.mult))
            chain.mark(tt(t[9][:], t[8][:], aim, ALU.mult))
            chain.after(tt(t[11][:], t[10][:], t[1][:], ALU.mult))
            chain.mark(tt(t[4][:], t[4][:], t[5][:], ALU.add))
            chain.mark(tt(t[6][:], t[7][:], t[6][:], ALU.subtract))
            chain.after(tt(t[9][:], t[9][:], t[11][:], ALU.add))
            chain.after(nc.vector.reciprocal(t[4][:], t[4][:]))
            chain.after(ts(t[4][:], t[4][:], 2.0, None, ALU.mult))
            chain.mark(tt(t[6][:], t[6][:], t[4][:], ALU.mult))
            chain.after(tt(t[9][:], t[9][:], t[4][:], ALU.mult))
            a, b = t[7], t[8]
            chain.mark(nc.vector.tensor_copy(a[0:N, :], t[6][0:N, :]))
            chain.mark(nc.vector.tensor_copy(a[N:P, :], t[9][N:P, :]))
            chain.mark(nc.vector.tensor_copy(b[0:N, :], t[9][0:N, :]))
            chain.after(ts(b[N:P, :], t[6][N:P, :], -1.0, None, ALU.mult))
            dve.wait_ge(s_trig, 2)
            dve.wait_ge(s_mag, 1)
            tt(tab1[:], tab1[:], mag[:], ALU.mult).then_inc(s_tab1, 1)
            dve.wait_ge(s_tab1, 1)
            dve.wait_ge(s_tab2, 1)
            e_re, e_im = tab1[:, :, 0:TI], tab2[:, :, 0:TI]
            chain.mark(tt(a1[:], bc(a[:], TI, 2), e_re, ALU.mult))
            chain.mark(tt(a2[:], bc(b[:], TI, 2), e_re, ALU.mult))
            chain.after(tt(at[:], bc(b[:], TI, 2), e_im, ALU.mult))
            tt(a1[:], a1[:], at[:], ALU.add).then_inc(s_a, 1)
            dve.wait_ge(s_a, 1)
            chain.after(tt(at[:], bc(a[:], TI, 2), e_im, ALU.mult))
            tt(a2[:], a2[:], at[:], ALU.subtract).then_inc(s_a, 1)
            dve.wait_ge(s_a, 2)
            dve.wait_ge(s_c, 32)

            def factors(n, s):
                dve.wait_ge(s_mm[s], n + 1)
                hs = channels(n, s, CUT, UH)
                tt(four(w[s][1], C)[:, CUT:UH], bc(a2[:, hs, :], C, 3), bc(cim[:, hs, :], KT, 2), ALU.mult).then_inc(s_w[s], 1)
                dve.wait_ge(s_v[1 - s], n + 1 + s)
                chain.after(tt(four(v_second, TJ), bc(tab2[:, channels(n, s), TI:2 * TI], TJ, 3),
                               bc(tab2[:, channels(n, s), 2 * TI:TAB], TI, 2), ALU.mult))
                dve.wait_ge(s_v1[s], n + 1)
                tt(v[s], v[s], v_second, ALU.add).then_inc(s_v[s], 1)

            def moments(n, s):
                dve.wait_ge(s_tok[s], n + 2)
                chain.mark(nc.vector.bn_stats(stats[s][:, 0, :], tok[s][:, 0:512]))
                chain.mark(nc.vector.bn_stats(stats[s][:, 1, :], tok[s][:, 512:D]))
                apart(dve, s_passed, (s_dve, chain.now()))
                nc.vector.bn_aggr(mv[s][:], stats[s][:].rearrange("p a b -> p (a b)")).then_inc(s_mv[s], 1)

            def inverse(n, s):
                dve.wait_ge(s_std[s], n + 1)
                chain.after(nc.vector.reciprocal(rs[s][:, 0:1], std[s][:]))
                nc.vector.scalar_tensor_tensor(rs[s][:, 1:2], mv[s][:, 0:1], -1.0, rs[s][:, 0:1], ALU.mult, ALU.mult).then_inc(s_rs[s], 1)

            def low(n, s):
                dve.wait_ge(s_hi[s], n + 1)
                tt(xn_lo[:].rearrange("p k (c h) -> p k c h", h=H)[:, :, :, channels(n, s)], pn[:].rearrange("p k (c h) -> p k c h", h=UH),
                   xn_hi[:].rearrange("p k (c h) -> p k c h", h=H)[:, :, :, channels(n, s)], ALU.subtract).then_inc(s_lo[s], 1)

            run(dve, [(4, inverse), (0, factors), (3, moments), (5, low)], chain, 2 * 4)
    return sems


HEADS, HD = 32, 32
HPT = P // HD
CH = 512
NCH = TOK // CH
BPC = CH // H
RMAX = bass.bass_isa.ReduceOp.max
W_TOP = 2.0 ** 13


def split_scales(chain, big, low, scale, back):
    chain.after(nc_ts(chain, low, big, 1e-30, None, ALU.max))
    chain.after(nc_ts(chain, low.bitcast(I32), low.bitcast(I32), 0x7F800000, None, ALU.bitwise_and))
    chain.after(chain.eng.reciprocal(scale, low))
    chain.after(nc_ts(chain, scale, scale, W_TOP, None, ALU.mult))
    return nc_ts(chain, back, low, 1.0 / W_TOP, None, ALU.mult)


def nc_ts(chain, *args):
    return chain.eng.tensor_scalar(*args)


def attention(nc, wqkv, bqkv, xn_hi, xn_lo, ident, mask, o_dram):
    sems = []
    with ExitStack() as st:
        def sb(name, shape, dt=F32):
            return st.enter_context(nc.sbuf_tensor(name, shape, dt))

        def ps(name, shape):
            return st.enter_context(nc.psum_tensor(name, shape, F32))

        def sem(name):
            sems.append(nc.alloc_semaphore(name))
            return sems[-1]

        two = range(2)
        raw = sb("w_raw", [P, 3, D])
        w_hi = [sb(f"w_hi{s}", [P, 3, D], F16) for s in two]
        w_lo = [sb(f"w_lo{s}", [P, 3, D], F16) for s in two]
        big, bigs, low2 = sb("w_big", [P, 3]), sb("w_bigs", [P, 3]), sb("w_pow", [P, 3])
        scale, back = sb("w_scale", [P, 3]), [sb(f"w_back{s}", [P, 3]) for s in two]
        bias = sb("b_qkv", [P, 3, KT])
        qf, kf, vf = sb("qf", [P, CH]), sb("kf", [P, CH]), sb("vf", [P, CH])
        qh, ql = sb("qh", [P, CH], F32R), sb("ql", [P, CH], F32R)
        kh, kl = (sb(n, [P, BPC, HPT, H], F32R) for n in ("kh", "kl"))
        vh, vl = (sb(n, [P, BPC, P], F32R) for n in ("vh", "vl"))
        prob = [sb(f"prob{p}", [P, 2 * HPT, H]) for p in two]
        mx, sm = ([sb(f"{n}{p}", [P, 2 * HPT]) for p in two] for n in ("mx", "sm"))
        pth, ptl = ([sb(f"{n}{p}", [P, 2, HPT * H], F32R) for p in two] for n in ("pth", "ptl"))
        ot = [sb(f"ot{s}", [P, CH]) for s in two]
        ps_a, ps_b = ps("ps_a", [P, CH]), ps("ps_b", [P, CH])
        ps_s, ps_t, ps_o = ps("ps_s", [P, 2, CH]), ps("ps_t", [P, 2, CH]), ps("ps_o", [P, 2, CH])

        s_raw, s_bias, s_big, s_bigs, s_scale, s_whi, s_wlo = (
            sem("c_" + n) for n in ("raw", "bias", "big", "bigs", "scale", "whi", "wlo"))
        s_passed = sem("c_passed")
        s_zero = sem("c_zero")
        s_pq, s_pk, s_pv, s_vt = (sem("c_" + n) for n in ("pq", "pk", "pv", "vt"))
        s_qf, s_kf, s_vf, s_ql, s_kl, s_vl = (sem("c_" + n) for n in ("qf", "kf", "vf", "ql", "kl", "vl"))
        s_score, s_mask, s_max, s_sub, s_exp, s_rc, s_prob, s_tr, s_pth, s_ptl, s_pvd, s_ox, s_od = (
            [sem(f"c_{n}{p}") for p in two]
            for n in ("score", "mask", "max", "sub", "exp", "rc", "prob", "tr", "pth", "ptl", "pvd", "ox", "od"))
        s_dve = sem("c_dve")
        TURN = 2 * NCH
        TURNS = KT // 2
        start_free(nc, [*s_od], 16)
        nc.all_engine_barrier()
        block = st.enter_context(nc.Block())

        def where(u, k):
            return u * TURN + k, (k // NCH) % 2, u * 2 + k // NCH, k % NCH

        def run(eng, first, step, last, chain=None, marks=0):
            first()
            before = chain.count if chain else 0
            with eng.Fori(0, TURNS - 1) as u:
                if chain:
                    chain.loop(u, marks)
                for k in range(1, TURN + 1):
                    step(u, k)
            if chain:
                chain.end(TURNS - 1, marks, before)
            for k in range(1, TURN):
                step(TURNS - 1, k)
            last()

        @block.sync
        def _(sp):
            sp.dma_start(bias[:], bqkv).then_inc(s_bias, 16)
            sp.dma_start(raw[:], wqkv[0, :, :, :]).then_inc(s_raw, 16)
            sp.wait_ge(s_wlo, 3)
            sp.dma_start(raw[:], wqkv[1, :, :, :]).then_inc(s_raw, 16)

            def store(u):
                for s in two:
                    for c in range(NCH):
                        n, par = u * TURN + s * NCH + c, c % 2
                        sp.wait_ge(s_ox[1], n + 1)
                        sp.dma_start(o_dram[bass.ds(u * 2 + s, 1), :, c * CH:(c + 1) * CH].rearrange("o f t -> (o f) t"),
                                     ot[par][:]).then_inc(s_od[par], 16)
                        if c == 1 and not isinstance(u, int):
                            sp.wait_ge(s_wlo, (u * 2 + s + 2) * 3)
                            sp.dma_start(raw[:], wqkv[bass.ds(u * 2 + s + 2, 1), :, :, :].rearrange("o p m n -> (o p) m n")
                                         ).then_inc(s_raw, 16)

            with sp.Fori(0, TURNS - 1) as u:
                store(u)
            store(TURNS - 1)
            for par in two:
                sp.wait_ge(s_od[par], 16 * (KT * NCH // 2) + 16)

        @block.gpsimd
        def _(pool):
            nc.gpsimd.memset(kh[:].bitcast(F32), 0.0).then_inc(s_zero, 1)
            nc.gpsimd.memset(kl[:].bitcast(F32), 0.0).then_inc(s_zero, 1)

            def reduce_big(j):
                apart(pool, s_passed, (s_big, j + 1), (s_scale, j))
                nc.gpsimd.partition_all_reduce(bigs[:], big[:], P, RMAX).then_inc(s_bigs, 1)

            def step(u, k, first=False):
                t, ws, j, c = where(u, k)
                for p in two:
                    pool.wait_ge(s_max[p], t + 1)
                    nc.gpsimd.tensor_tensor(prob[p][:], prob[p][:], bc(mx[p][:], H, 2), ALU.subtract).then_inc(s_sub[p], 1)
                for p in two:
                    pool.wait_ge(s_rc[p], t + 1)
                    nc.gpsimd.tensor_tensor(prob[p][:], prob[p][:], bc(sm[p][:], H, 2), ALU.mult).then_inc(s_prob[p], 1)
                if c == 0 and not (isinstance(u, int) and u == TURNS - 1 and k >= NCH):
                    reduce_big(j + 1)

            reduce_big(0)
            run(pool, lambda: step(0, 0), step, lambda: None)

        @block.tensor
        def _(pe):
            def project(m, out, ws, c):
                tok = slice(c * CH, (c + 1) * CH)
                for k in range(KT):
                    w = slice(k * P, (k + 1) * P)
                    nc.tensor.matmul(out[:], w_hi[ws][:, m, w], xn_hi[:, k, tok], start=(k == 0), stop=False)
                    nc.tensor.matmul(out[:], w_hi[ws][:, m, w], xn_lo[:, k, tok], start=False, stop=False)
                    last = nc.tensor.matmul(out[:], w_lo[ws][:, m, w], xn_hi[:, k, tok], start=False, stop=(k == KT - 1))
                return last

            def transposes(p):
                for b in two:
                    for a in range(HPT):
                        last = nc.tensor.transpose(ps_t[:, b, a * H:(a + 1) * H], prob[p][:, b * HPT + a, :], ident[:])
                return last

            def values(p):
                for b in two:
                    at = p * 2 + b
                    nc.tensor.matmul(ps_o[:, b, :], vh[:, at, :], pth[p][:, b, :], start=True, stop=False)
                    nc.tensor.matmul(ps_o[:, b, :], vh[:, at, :], ptl[p][:, b, :], start=False, stop=False)
                    last = nc.tensor.matmul(ps_o[:, b, :], vl[:, at, :], pth[p][:, b, :], start=False, stop=True)
                return last

            def scores(p):
                for b in two:
                    at = p * 2 + b
                    q, k = slice(at * H, (at + 1) * H), slice(0, HPT)
                    nc.tensor.matmul(ps_s[:, b, :], qh[:, q], kh[:, at, k, :], start=True, stop=False)
                    nc.tensor.matmul(ps_s[:, b, :], qh[:, q], kl[:, at, k, :], start=False, stop=False)
                    last = nc.tensor.matmul(ps_s[:, b, :], ql[:, q], kh[:, at, k, :], start=False, stop=True)
                return last

            def attend_first(t):
                pe.wait_ge(s_prob[0], t)
                transposes(0).then_inc(s_tr[0], 1)

            def attend_second(t):
                pe.wait_ge(s_prob[1], t)
                pe.wait_ge(s_ptl[0], t)
                transposes(1).then_inc(s_tr[1], 1)
                pe.wait_ge(s_vl, t)
                values(0).then_inc(s_pvd[0], 1)

            def attend_third(t):
                pe.wait_ge(s_ptl[1], t)
                pe.wait_ge(s_ox[0], t)
                values(1).then_inc(s_pvd[1], 1)

            def step(u, k, first=False):
                t, ws, j, c = where(u, k)
                if c == 0:
                    pe.wait_ge(s_wlo, 3 * (j + 1))
                pe.wait_ge(s_vf, t)
                project(0, ps_a, ws, c).then_inc(s_pq, 1)
                pe.wait_ge(s_vl, t)
                project(1, ps_b, ws, c).then_inc(s_pk, 1)
                if not first:
                    attend_first(t)
                pe.wait_ge(s_qf, t + 1)
                project(2, ps_a, ws, c).then_inc(s_pv, 1)
                if not first:
                    attend_second(t)
                pe.wait_ge(s_ql, t + 1)
                pe.wait_ge(s_kl, t + 1)
                pe.wait_ge(s_mask[1], t)
                scores(0).then_inc(s_score[0], 1)
                if not first:
                    attend_third(t)
                pe.wait_ge(s_vf, t + 1)
                pe.wait_ge(s_kf, t + 1)
                for b in range(BPC):
                    last = nc.tensor.transpose(ps_b[:, b * P:(b + 1) * P], vf[:, b * H:(b + 1) * H], ident[:])
                last.then_inc(s_vt, 1)
                pe.wait_ge(s_mask[0], t + 1)
                scores(1).then_inc(s_score[1], 1)

            def last():
                t = KT * NCH
                attend_first(t)
                attend_second(t)
                attend_third(t)

            run(pe, lambda: step(0, 0, True), step, last)

        @block.scalar
        def _(act):
            def high_weights(ws, j):
                act.wait_ge(s_scale, j + 1)
                for m in range(3):
                    nc.scalar.activation(w_hi[ws][:, m, :], raw[:, m, :], ACT.Copy, scale=scale[:, m:m + 1]).then_inc(s_whi, 1)

            def outputs(p, n_par, v, t):
                act.wait_ge(s_pvd[p], t)
                if p == 0:
                    act.wait_ge(s_od[n_par], v * 16 + 16)
                for a in range(HPT):
                    r = slice(HD * a, HD * a + HD)
                    last = nc.scalar.activation(ot[n_par][r, p * 2 * H:(p + 1) * 2 * H].rearrange("p (b q) -> p b q", q=H),
                                                ps_o[r, :, a * H:(a + 1) * H], ACT.Copy)
                last.then_inc(s_ox[p], 1)

            def attend(u, k, part):
                t = u * TURN + k
                n_par, v = (k - 1) % 2, u * (TURN // 2) + (k - 1) // 2
                if part < 2:
                    act.wait_ge(s_tr[part], t)
                    nc.scalar.activation(pth[part][:], ps_t[:], ACT.Copy).then_inc(s_pth[part], 1)
                else:
                    outputs(part - 2, n_par, v, t)

            def step(u, k, first=False):
                t, ws, j, c = where(u, k)
                apart(act, s_passed, (s_pq, t + 1), (s_ql, t))
                nc.scalar.activation(qf[:], ps_a[:], ACT.Identity, scale=back[ws][:, 0:1],
                                     bias=bias[:, 0, bass.ds(j, 1)]).then_inc(s_qf, 1)
                apart(act, s_passed, (s_pk, t + 1), (s_kl, t))
                nc.scalar.activation(kf[:], ps_b[:], ACT.Identity, scale=back[ws][:, 1:2],
                                     bias=bias[:, 1, bass.ds(j, 1)]).then_inc(s_kf, 1)
                if not first:
                    attend(u, k, 0)
                apart(act, s_passed, (s_pv, t + 1))
                nc.scalar.activation(vf[:], ps_a[:], ACT.Identity, scale=back[ws][:, 2:3],
                                     bias=bias[:, 2, bass.ds(j, 1)]).then_inc(s_vf, 1)
                if not first:
                    attend(u, k, 1)
                    attend(u, k, 2)
                    attend(u, k, 3)
                for p in two:
                    act.wait_ge(s_sub[p], t + 1)
                    nc.scalar.activation(prob[p][:], prob[p][:], ACT.Exp).then_inc(s_exp[p], 1)
                if c == 1 and not (isinstance(u, int) and u == TURNS - 1 and k >= NCH):
                    act.wait_ge(s_pv, t + 1)
                    high_weights(1 - ws, j + 1)

            act.wait_ge(s_bias, 16)
            high_weights(0, 0)
            run(act, lambda: step(0, 0, True), step, lambda: [attend(TURNS - 1, TURN, part) for part in range(4)])

        @block.vector
        def _(dve):
            chain = Chain(dve, s_dve)
            tt = nc.vector.tensor_tensor

            def find_big(j):
                dve.wait_ge(s_raw, 16 * (j + 1))
                nc.vector.tensor_reduce(big[:], raw[:], X, ALU.max, apply_absolute_value=True).then_inc(s_big, 1)

            def low_weights(ws, j):
                dve.wait_ge(s_bigs, j + 1)
                split_scales(chain, bigs[:], low2[:], scale[:], back[ws][:]).then_inc(s_scale, 1)
                for m in range(3):
                    dve.wait_ge(s_whi, 3 * j + m + 1)
                    nc.vector.scalar_tensor_tensor(w_lo[ws][:, m, :], raw[:, m, :], scale[:, m:m + 1], w_hi[ws][:, m, :],
                                                   ALU.mult, ALU.subtract).then_inc(s_wlo, 1)

            def attend(t, p):
                dve.wait_ge(s_pth[p], t)
                tt(ptl[p][:], ps_t[:], pth[p][:].bitcast(F32), ALU.subtract).then_inc(s_ptl[p], 1)

            def top(t, p):
                dve.wait_ge(s_score[p], t + 1)
                nc.vector.scalar_tensor_tensor(prob[p][:], ps_s[:].rearrange("p b (a k) -> p (b a) k", k=H), HD ** -0.5,
                                               bc(mask[:], 2 * HPT, 1), ALU.mult, ALU.add).then_inc(s_mask[p], 1)
                dve.wait_ge(s_mask[p], t + 1)
                nc.vector.tensor_reduce(mx[p][:], prob[p][:], X, ALU.max).then_inc(s_max[p], 1)

            def step(u, k, first=False):
                t, ws, j, c = where(u, k)
                dve.wait_ge(s_qf, t + 1)
                chain.after(nc.vector.tensor_copy(qh[:], qf[:]))
                tt(ql[:], qf[:], qh[:].bitcast(F32), ALU.subtract).then_inc(s_ql, 1)
                dve.wait_ge(s_kf, t + 1)
                for a in range(HPT):
                    r = slice(HD * a, HD * a + HD)
                    last = nc.vector.tensor_copy(kh[r, :, a, :], kf[r, :].rearrange("p (b k) -> p b k", k=H))
                chain.after(last)
                for a in range(HPT):
                    r = slice(HD * a, HD * a + HD)
                    last = tt(kl[r, :, a, :], kf[r, :].rearrange("p (b k) -> p b k", k=H), kh[r, :, a, :].bitcast(F32), ALU.subtract)
                last.then_inc(s_kl, 1)
                if not first:
                    attend(t, 0)
                    attend(t, 1)
                top(t, 0)
                dve.wait_ge(s_vt, t + 1)
                chain.after(nc.vector.tensor_copy(vh[:].rearrange("p b f -> p (b f)"), ps_b[:]))
                tt(vl[:].rearrange("p b f -> p (b f)"), ps_b[:], vh[:].rearrange("p b f -> p (b f)").bitcast(F32),
                   ALU.subtract).then_inc(s_vl, 1)
                top(t, 1)
                for p in two:
                    dve.wait_ge(s_exp[p], t + 1)
                    chain.after(nc.vector.tensor_reduce(sm[p][:], prob[p][:], X, ALU.add))
                    nc.vector.reciprocal(sm[p][:], sm[p][:]).then_inc(s_rc[p], 1)
                if c == 0 and not (isinstance(u, int) and u == TURNS - 1 and k >= NCH):
                    find_big(j + 1)
                if c == 1 and not (isinstance(u, int) and u == TURNS - 1 and k >= NCH):
                    low_weights(1 - ws, j + 1)

            find_big(0)
            low_weights(0, 0)
            dve.wait_ge(s_zero, 2)
            run(dve, lambda: step(0, 0, True), step, lambda: [attend(KT * NCH, p) for p in two],
                chain, TURN * 5 + 2 * 4)
    return sems


R = 32


def project_and_norm(nc, wo, bo, ga, o_dram, h0_dram, h1_dram, x2_hi, x2_lo, low, ident):
    sems = []
    with ExitStack() as st:
        def sb(name, shape, dt=F32):
            return st.enter_context(nc.sbuf_tensor(name, shape, dt))

        def sem(name):
            sems.append(nc.alloc_semaphore(name))
            return sems[-1]

        two = range(2)
        wraw = [sb(f"wo_raw{s}", [P, D]) for s in two]
        woh, wol = sb("wo_hi", [P, KT, D], F32R), sb("wo_lo", [P, KT, D], F32R)
        bob = sb("bo_rows", [P, D])
        gab = sb("gu_a", [P, KT, 2 * R])
        oraw = sb("o_raw", [P, KT, P])
        oh, ol = ([sb(f"{n}{s}", [P, KT, P], F32R) for s in two] for n in ("o_hi", "o_lo"))
        res = sb("residual", [P, D])
        h1 = sb("h1_tok", [P, D])
        nrm = sb("h1_nrm", [P, D])
        x2f = sb("x2_f32", [P, KT, P])
        stats, mv, std, eps = sb("d_stats", [P, 2, 6]), sb("d_mv", [P, 2]), sb("d_std", [P, 2]), sb("d_eps", [P, 1])
        acc = [st.enter_context(nc.psum_tensor(f"d_acc{s}", [P, 2, 512], F32)) for s in two]
        pn = st.enter_context(nc.psum_tensor("d_pn", [P, KT, P], F32))
        pl = st.enter_context(nc.psum_tensor("d_pl", [P, P], F32))
        s_passed = sem("d_passed")
        s_const, s_eps, s_dve = sem("d_const"), sem("d_eps"), sem("d_dve")
        s_wraw = [sem(f"d_wraw{s}") for s in two]
        s_woh, s_wol = sem("d_woh"), sem("d_wol")
        s_o, s_oh, s_ol, s_h0, s_res, s_acc, s_h1, s_h1out, s_mv, s_std, s_nrm, s_trn, s_hi, s_f, s_lo, s_low, s_lowout = (
            sem("d_" + n) for n in ("o", "oh", "ol", "h0", "res", "acc", "h1", "h1out", "mv", "std", "nrm", "trn", "hi",
                                    "f", "lo", "low", "lowout"))
        VIS = C // 2
        start_free(nc, [s_lo, s_lowout, s_h1, s_low], 1)
        nc.all_engine_barrier()
        block = st.enter_context(nc.Block())

        def run(eng, first, step, last, chain=None, marks=0):
            first()
            before = chain.count if chain else 0
            with eng.Fori(0, VIS - 1) as v:
                if chain:
                    chain.loop(v, marks)
                step(v * 2 + 1, 1)
                step(v * 2 + 2, 0)
            if chain:
                chain.end(VIS - 1, marks, before)
            step(C - 1, 1)
            last()

        @block.sync
        def _(sp):
            sp.dma_start(gab[:], ga).then_inc(s_const, 16)
            sp.dma_start(bob[:], bo).then_inc(s_const, 16)
            for k in range(KT):
                if k >= 2:
                    sp.wait_ge(s_wol, k - 1)
                sp.dma_start(wraw[k % 2][:], wo[:, k, :]).then_inc(s_wraw[k % 2], 16)
            with sp.Fori(0, C) as n:
                sp.wait_ge(s_h1, n + 2)
                sp.dma_start(h1_dram[bass.ds(n, 1), :, :].rearrange("o t d -> (o t) d"), h1[:]).then_inc(s_h1out, 16)
            sp.wait_ge(s_h1out, 16 * C)

        @block.gpsimd
        def _(pool):
            pool.wait_ge(s_const, 32)
            with pool.Fori(0, C) as n:
                pool.wait_ge(s_h1, n + 1)
                pool.dma_start(res[:], h0_dram[bass.ds(n, 1), :, :].rearrange("o t d -> (o t) d")).then_inc(s_h0, 16)
                pool.wait_ge(s_h0, n * 16 + 16)
                nc.gpsimd.tensor_tensor(res[:], res[:], bob[:], ALU.add).then_inc(s_res, 1)

        @block.tensor
        def _(pe):
            def half(s, b, n, first=False):
                for k in range(KT):
                    if first and b == 0:
                        pe.wait_ge(s_wol, k + 1)
                    rhs = slice(b * 512, (b + 1) * 512)
                    nc.tensor.matmul(acc[s][:, b, :], oh[s][:, k, :], woh[:, k, rhs], start=(k == 0), stop=False)
                    nc.tensor.matmul(acc[s][:, b, :], oh[s][:, k, :], wol[:, k, rhs], start=False, stop=False)
                    last = nc.tensor.matmul(acc[s][:, b, :], ol[s][:, k, :], woh[:, k, rhs], start=False, stop=(k == KT - 1))
                return last

            def to_features(n):
                pe.wait_ge(s_nrm, n)
                pe.wait_ge(s_lo, n)
                for i in range(KT):
                    last = nc.tensor.transpose(pn[:, i, :], nrm[:, i * P:(i + 1) * P], ident[:])
                last.then_inc(s_trn, 1)

            def low_rank(n):
                pe.wait_ge(s_f, n)
                pe.wait_ge(s_lowout, n)
                for k in range(KT):
                    last = nc.tensor.matmul(pl[0:2 * R, :], gab[:, k, :], x2f[:, k, :], start=(k == 0), stop=(k == KT - 1))
                last.then_inc(s_low, 1)

            def step(n, s, first=False):
                pe.wait_ge(s_ol, n + 1)
                if not first:
                    pe.wait_ge(s_h1, n)
                half(s, 0, n, first)
                if not first:
                    to_features(n)
                half(s, 1, n, first).then_inc(s_acc, 1)
                if not first:
                    low_rank(n)

            def last():
                to_features(C)
                low_rank(C)

            pe.wait_ge(s_const, 32)
            run(pe, lambda: step(0, 0, True), step, last)

        @block.scalar
        def _(act):
            def load(n):
                act.dma_start(oraw[:], o_dram.rearrange("k f t -> f k t")[:, :, bass.ds(n * H, H)]).then_inc(s_o, 16)

            def take(n):
                apart(act, s_passed, (s_trn, n))
                nc.scalar.activation(x2_hi[:, :, bass.ds((n - 1) * H, H)], pn[:], ACT.Copy).then_inc(s_hi, 1)
                act.wait_ge(s_low, n)
                nc.scalar.activation(x2f[:], pn[:], ACT.Copy).then_inc(s_f, 1)
                apart(act, s_passed, (s_low, n + 1))
                nc.scalar.activation(low[:, bass.ds((n - 1) * H, H)], pl[0:2 * R, :], ACT.Copy).then_inc(s_lowout, 1)

            def deviation(n):
                act.wait_ge(s_mv, n + 1)
                nc.scalar.activation(std[:, 0:1], mv[:, 1:2], ACT.Sqrt, bias=eps[:]).then_inc(s_std, 1)

            def split(n, s):
                act.wait_ge(s_o, n * 16 + 16)
                nc.scalar.activation(oh[s][:], oraw[:], ACT.Copy).then_inc(s_oh, 1)

            def step(n, s):
                act.wait_ge(s_ol, n + 1)
                load_n = n + 1
                load(load_n)
                act.wait_ge(s_acc, n)
                split(load_n, 1 - s)
                take(n)
                deviation(n)

            act.wait_ge(s_eps, 1)
            load(0)
            split(0, 0)
            act.wait_ge(s_ol, 1)
            load(1)
            split(1, 1)
            deviation(0)
            with act.Fori(0, VIS - 1) as v:
                step(v * 2 + 1, 1)
                step(v * 2 + 2, 0)
            take(C - 1)
            deviation(C - 1)
            take(C)

        @block.vector
        def _(dve):
            chain = Chain(dve, s_dve)
            nc.vector.memset(eps[:], EPS).then_inc(s_eps, 1)

            def low_split(n, s):
                dve.wait_ge(s_oh, n + 1)
                nc.vector.tensor_tensor(ol[s][:], oraw[:], oh[s][:].bitcast(F32), ALU.subtract).then_inc(s_ol, 1)

            def take(n):
                at = bass.ds((n - 1) * H, H)
                dve.wait_ge(s_f, n)
                nc.vector.tensor_tensor(x2_lo[:, :, at], pn[:], x2_hi[:, :, at], ALU.subtract).then_inc(s_lo, 1)

            def normalise(n, s):
                dve.wait_ge(s_acc, n + 1)
                dve.wait_ge(s_res, n + 1)
                dve.wait_ge(s_h1out, n * 16)
                nc.vector.tensor_tensor(h1[:], acc[s][:].rearrange("p b n -> p (b n)"), res[:], ALU.add).then_inc(s_h1, 1)
                dve.wait_ge(s_h1, n + 2)
                chain.mark(nc.vector.bn_stats(stats[:, 0, :], h1[:, 0:512]))
                chain.mark(nc.vector.bn_stats(stats[:, 1, :], h1[:, 512:D]))
                apart(dve, s_passed, (s_dve, chain.now()))
                nc.vector.bn_aggr(mv[:], stats[:].rearrange("p a b -> p (a b)")).then_inc(s_mv, 1)
                dve.wait_ge(s_std, n + 1)
                chain.after(nc.vector.reciprocal(std[:, 1:2], std[:, 0:1]))
                nc.vector.tensor_scalar(nrm[:], h1[:], mv[:, 0:1], std[:, 1:2], ALU.subtract, ALU.mult).then_inc(s_nrm, 1)

            def step(n, s, end=False):
                if not end:
                    low_split(n + 1, 1 - s)
                take(n)
                normalise(n, s)

            low_split(0, 0)
            for k in range(KT):
                dve.wait_ge(s_wraw[k % 2], 16 * (k // 2 + 1))
                nc.vector.tensor_copy(woh[:, k, :], wraw[k % 2][:]).then_inc(s_woh, 1)
                dve.wait_ge(s_woh, k + 1)
                nc.vector.tensor_tensor(wol[:, k, :], wraw[k % 2][:], woh[:, k, :].bitcast(F32), ALU.subtract).then_inc(s_wol, 1)
            low_split(1, 1)
            normalise(0, 0)
            first = chain.count
            with dve.Fori(0, VIS - 1) as v:
                chain.loop(v, 6)
                step(v * 2 + 1, 1)
                step(v * 2 + 2, 0)
            chain.end(VIS - 1, 6, first)
            step(C - 1, 1, True)
            take(C)
    return sems


R = 32
I = 2752
IT = -(-I // P)
Q_ZERO, Q_STEP, LR_SCALE = 7.5, 0.005, 0.02
CH = 512
NCH = TOK // CH


def gate_up(nc, qgu, sgu, bgu, da, x2_hi, x2_lo, low, hid_dram, inner_st):
    sems = []
    with ExitStack() as st:
        def sb(name, shape, dt=F32):
            return st.enter_context(nc.sbuf_tensor(name, shape, dt))

        def sem(name):
            sems.append(nc.alloc_semaphore(name))
            return sems[-1]

        two = range(2)
        qraw = [sb(f"q_raw{s}", [P, 2, D], I32) for s in two]
        q16 = [sb(f"q_f16{s}", [P, 2, D], F16) for s in two]
        braw = [sb(f"b_raw{s}", [P, 2, P]) for s in two]
        bst = [sb(f"b_stack{s}", [P, 2, P], F32R) for s in two]
        scl = sb("gu_scale", [P, 2, IT])
        lraw = sb("low_raw", [P, 2, TOK])
        lst = sb("low_stack", [P, 2, TOK], F32R)
        araw, a_st = [sb(f"a_raw{s}", [P, R]) for s in two], [sb(f"a_split{s}", [P, 2, R], F32R) for s in two]
        hs_hi, hs_lo = ([sb(f"{n}{c}", [P, CH], F32R) for c in two] for n in ("hid_hi", "hid_lo"))
        inner = sb("inner_sum", [2 * R, TOK])
        lsb = [sb(f"low_term{c}", [P, 2, CH]) for c in two]
        gsb, usb, ssb = ([sb(f"{n}{c}", [P, CH]) for c in two] for n in ("gate", "up", "silu"))
        hid = [sb(f"hid{s}", [P, TOK]) for s in two]
        ps_m = [st.enter_context(nc.psum_tensor(f"e_main{c}", [P, 2, CH], F32)) for c in two]
        ps_l = st.enter_context(nc.psum_tensor("e_low", [P, 2, CH], F32))
        ps_i = [st.enter_context(nc.psum_tensor(f"e_inner{c}", [2 * R, CH], F32)) for c in two]
        s_passed = sem("e_passed")
        s_scl, s_scl2, s_lraw, s_lst, s_dve = sem("e_scl"), sem("e_scl2"), sem("e_lraw"), sem("e_lst"), sem("e_dve")
        s_load, s_q, s_b, s_read, s_out = ([sem(f"e_{n}{s}") for s in two] for n in ("load", "q", "b", "read", "out"))
        s_main, s_gate, s_silu, s_up, s_hid, s_hi, s_lo, s_inner, s_add = (
            [sem(f"e_{n}{s}") for s in two] for n in ("main", "gate", "silu", "up", "hid", "hi", "lo", "inner", "add"))
        s_low, s_lsb, s_zero, s_moved, s_end = (sem("e_" + n) for n in ("low", "lsb", "zero", "moved", "end"))
        s_a = [sem(f"e_a{s}") for s in two]
        PER = NCH // 2
        start_free(nc, [*s_q, *s_b, *s_read, *s_up, s_lsb, *s_hid, *s_silu, *s_a, *s_add, s_lo[1]], 1)
        start_free(nc, [*s_out], 16)
        nc.all_engine_barrier()
        block = st.enter_context(nc.Block())

        @block.sync
        def _(sp):
            for m in two:
                for g in range(4):
                    sp.dma_start(lraw[R * g:R * g + R, m, :], low[R * m:R * m + R, :]).then_inc(s_lraw, 16)
            sp.dma_start(scl[:], sgu).then_inc(s_scl, 16)
            with sp.Fori(0, IT // 2) as v:
                for s in two:
                    sp.wait_ge(s_q[s], v + 1)
                    sp.wait_ge(s_b[s], v + 1)
                    sp.wait_ge(s_a[s], v + 1)
                    sp.dma_start(qraw[s][:], qgu[bass.ds(v * 2 + s, 1), :, :, :].rearrange("o p m n -> (o p) m n")).then_inc(s_load[s], 16)
                    sp.dma_start(braw[s][:], bgu[bass.ds(v * 2 + s, 1), :, :, :].rearrange("o p m n -> (o p) m n")).then_inc(s_load[s], 16)
                    sp.dma_start(araw[s][:], da[:, bass.ds(v * 2 + s, 1), :].rearrange("p o r -> p (o r)")).then_inc(s_load[s], 16)
            for m in two:
                for g in range(4):
                    for b in two:
                        sp.wait_ge(s_add[b], PER * IT + 1 + b)
                    sp.dma_start(lraw[R * g:R * g + R, m, :], inner[R * m:R * m + R, :]).then_inc(s_moved, 16)

        @block.gpsimd
        def _(pool):
            with pool.Fori(0, IT // 2) as v:
                for s in two:
                    apart(pool, s_passed, (s_load[s], v * 48 + 48), (s_read[s], v + 1))
                    nc.gpsimd.tensor_scalar(q16[s][:], qraw[s][:], Q_ZERO, None, ALU.subtract).then_inc(s_q[s], 1)

        @block.tensor
        def _(pe):
            def inner_product(b, s, n):
                pe.wait_ge(s_lo[b], n + 1)
                pe.wait_ge(s_add[b], n + 1)
                nc.tensor.matmul(ps_i[b][:], a_st[s][:, :, :], hs_hi[b][:], start=True, stop=False)
                nc.tensor.matmul(ps_i[b][:], a_st[s][:, :, :], hs_lo[b][:], start=False, stop=True).then_inc(s_inner[b], 1)

            pe.wait_ge(s_zero, 4)
            with pe.Fori(0, IT // 2) as v:
                for s in two:
                    pe.wait_ge(s_q[s], v + 2)
                    for c in range(NCH):
                        b, n = c % 2, v * 2 * PER + s * PER + c // 2
                        tok = slice(c * CH, (c + 1) * CH)
                        pe.wait_ge(s_up[b], n + 1)
                        for m in two:
                            for k in range(KT):
                                w = q16[s][:, m, k * P:(k + 1) * P]
                                nc.tensor.matmul(ps_m[b][:, m, :], w, x2_hi[:, k, tok], start=(k == 0), stop=False)
                                last = nc.tensor.matmul(ps_m[b][:, m, :], w, x2_lo[:, k, tok], start=False, stop=(k == KT - 1))
                        last.then_inc(s_main[b], 1)
                        pe.wait_ge(s_b[s], v + 2)
                        pe.wait_ge(s_lst, 1)
                        pe.wait_ge(s_lsb, (v * 2 + s) * NCH + c + 1)
                        first = nc.tensor.matmul(ps_l[:, 0, :], bst[s][:, 0, :], lst[:, 0, tok], start=True, stop=True)
                        if c == NCH - 1:
                            first.then_inc(s_read[s], 1)
                        nc.tensor.matmul(ps_l[:, 1, :], bst[s][:, 1, :], lst[:, 1, tok], start=True, stop=True).then_inc(s_low, 1)
                        if c == 1:
                            pe.wait_ge(s_a[s], v + 2)
                        inner_product(1 - b, 1 - s if c == 0 else s, n)
            inner_product(1, 1, IT * PER)

        @block.scalar
        def _(act):
            with act.Fori(0, IT // 2) as v:
                for s in two:
                    for c in range(NCH):
                        b, n = c % 2, v * 2 * PER + s * PER + c // 2
                        act.wait_ge(s_low, (v * 2 + s) * NCH + c + 1)
                        act.wait_ge(s_up[b], n + 1)
                        nc.scalar.activation(lsb[b][:], ps_l[:], ACT.Copy, scale=LR_SCALE).then_inc(s_lsb, 1)
                        act.wait_ge(s_gate[b], n + 1)
                        act.wait_ge(s_hid[b], n + 1)
                        nc.scalar.activation(ssb[b][:], gsb[b][:], ACT.Silu).then_inc(s_silu[b], 1)
                        act.wait_ge(s_hid[b], n + 2)
                        nc.scalar.activation(hs_hi[b][:], hid[s][:, c * CH:(c + 1) * CH], ACT.Copy).then_inc(s_hi[b], 1)
                    act.wait_ge(s_hid[0], v * 2 * PER + (s + 1) * PER + 1)
                    act.wait_ge(s_hid[1], v * 2 * PER + (s + 1) * PER + 1)
                    act.dma_start(hid_dram[bass.ds(v * 2 + s, 1), :, :].rearrange("o p t -> (o p) t"), hid[s][:]).then_inc(s_out[s], 16)
            for s in two:
                act.wait_ge(s_out[s], 16 * (IT // 2) + 16)

        @block.vector
        def _(dve):
            chain = Chain(dve, s_dve)
            tt = nc.vector.tensor_tensor

            def add_inner(b, c, n):
                dve.wait_ge(s_inner[b], n + 1)
                tok = slice(c * CH, (c + 1) * CH)
                tt(inner[:, tok], inner[:, tok], ps_i[b][:], ALU.add).then_inc(s_add[b], 1)

            nc.vector.memset(a_st[1][:].bitcast(F32), 0.0).then_inc(s_zero, 1)
            nc.vector.memset(hs_hi[1][:].bitcast(F32), 0.0).then_inc(s_zero, 1)
            nc.vector.memset(hs_lo[1][:].bitcast(F32), 0.0).then_inc(s_zero, 1)
            nc.vector.memset(inner[:], 0.0).then_inc(s_zero, 1)
            dve.wait_ge(s_zero, 4)
            dve.wait_ge(s_scl, 16)
            nc.vector.tensor_scalar(scl[:], scl[:], Q_STEP, None, ALU.mult).then_inc(s_scl2, 1)
            dve.wait_ge(s_scl2, 1)
            dve.wait_ge(s_lraw, 16 * 8)
            chain.after(nc.vector.tensor_copy(lst[:], lraw[:]))
            tt(lst[64:P, :, :], lraw[64:P, :, :], lst[64:P, :, :].bitcast(F32), ALU.subtract).then_inc(s_lst, 1)
            first = chain.count
            with dve.Fori(0, IT // 2) as v:
                chain.loop(v, 2 * 3)
                for s in two:
                    dve.wait_ge(s_load[s], v * 48 + 48)
                    chain.after(nc.vector.tensor_copy(bst[s][:], braw[s][:]))
                    for g in (1, 3):
                        r = slice(R * g, R * g + R)
                        last = tt(bst[s][r, :, :], braw[s][r, :, :], bst[s][r, :, :].bitcast(F32), ALU.subtract)
                        if g == 1:
                            chain.mark(last)
                    last.then_inc(s_b[s], 1)
                    chain.after(nc.vector.tensor_copy(a_st[s][:, 0, :], araw[s][:]))
                    tt(a_st[s][:, 1, :], araw[s][:], a_st[s][:, 0, :].bitcast(F32), ALU.subtract).then_inc(s_a[s], 1)
                    for c in range(NCH):
                        b, n = c % 2, v * 2 * PER + s * PER + c // 2
                        dve.wait_ge(s_main[b], n + 1)
                        dve.wait_ge(s_lsb, (v * 2 + s) * NCH + c + 2)
                        dve.wait_ge(s_silu[b], n + 1)
                        for m, out, done in ((0, gsb, s_gate), (1, usb, s_up)):
                            nc.vector.scalar_tensor_tensor(out[b][:], ps_m[b][:, m, :], scl[:, m, bass.ds(v * 2 + s, 1)], lsb[b][:, m, :],
                                                           ALU.mult, ALU.add).then_inc(done[b], 1)
                        dve.wait_ge(s_silu[b], n + 2)
                        dve.wait_ge(s_up[b], n + 2)
                        if c == 0:
                            dve.wait_ge(s_out[s], v * 16 + 16)
                        tt(hid[s][:, c * CH:(c + 1) * CH], ssb[b][:], usb[b][:], ALU.mult).then_inc(s_hid[b], 1)
                        add_inner(1 - b, (c - 1) % NCH, n)
                        dve.wait_ge(s_hi[b], n + 1)
                        tt(hs_lo[b][:], hid[s][:, c * CH:(c + 1) * CH], hs_hi[b][:].bitcast(F32), ALU.subtract).then_inc(s_lo[b], 1)
            chain.end(IT // 2, 6, first)
            add_inner(1, NCH - 1, IT * PER)
            dve.wait_ge(s_moved, 16 * 8)
            chain.after(tt(lraw[:, 0, :], lraw[:, 0, :], lraw[:, 1, :], ALU.add))
            chain.after(nc.vector.tensor_copy(inner_st[:], lraw[:, 0, :]))
            tt(inner_st[64:P, :], lraw[64:P, 0, :], inner_st[64:P, :].bitcast(F32), ALU.subtract).then_inc(s_end, 1)
            dve.wait_ge(s_end, 1)
    return sems


HALF = 512
QS = 4


def down(nc, qd, sd, db, inner_st, hid_dram, h1_dram, out):
    sems = []
    with ExitStack() as st:
        def sb(name, shape, dt=F32):
            return st.enter_context(nc.sbuf_tensor(name, shape, dt))

        def sem(name):
            sems.append(nc.alloc_semaphore(name))
            return sems[-1]

        two = range(2)
        qraw = [sb(f"f_qraw{s}", [P, D], I32) for s in range(QS)]
        qd_sb = sb("f_levels", [P, IT, D], F32R)
        braw, b_st = sb("f_braw", [P, D]), sb("f_b", [P, D], F32R)
        scl = sb("f_scale", [P, D])
        hraw = sb("f_hraw", [P, IT, P])
        hh, hl = ([sb(f"f_{n}{s}", [P, IT, P], F32R) for s in two] for n in ("hh", "hl"))
        h1 = sb("f_h1", [P, D])
        lrt = sb("f_lrt", [P, D])
        y = sb("f_y", [P, D])
        pt = sb("f_pt", [P, P], F32R)
        acc = [st.enter_context(nc.psum_tensor(f"f_acc{s}", [P, 2, HALF], F32)) for s in two]
        ps_l = st.enter_context(nc.psum_tensor("f_lr", [P, 2, HALF], F32))
        s_const, s_b, s_scl, s_dve = (sem("f_s" + n) for n in ("const", "b", "scl", "dve"))
        s_qload = [sem(f"f_sqload{s}") for s in range(QS)]
        s_q = sem("f_sq")
        s_h, s_hh, s_hl, s_acc, s_pt, s_lr, s_lrt, s_h1, s_sum, s_scaled, s_y, s_out = (
            sem("f_s" + n) for n in ("h", "hh", "hl", "acc", "pt", "lr", "lrt", "h1", "sum", "scaled", "y", "out"))
        VIS = C // 2
        start_free(nc, [s_scaled, s_lrt, s_y, s_sum], 1)
        start_free(nc, [s_out], 16)
        nc.all_engine_barrier()
        block = st.enter_context(nc.Block())

        def run(first, step, last, eng):
            first()
            with eng.Fori(0, VIS - 1) as v:
                step(v * 2 + 1, 1)
                step(v * 2 + 2, 0)
            step(C - 1, 1)
            last()

        @block.sync
        def _(sp):
            sp.dma_start(hraw[:], hid_dram.rearrange("i p t -> p i t")[:, :, 0:P]).then_inc(s_h, 16)
            for i in range(IT):
                if i >= QS:
                    sp.wait_ge(s_q, i - QS + 1)
                sp.dma_start(qraw[i % QS][:], qd[:, i, :]).then_inc(s_qload[i % QS], 16)
            with sp.Fori(0, C) as n:
                sp.wait_ge(s_y, n + 2)
                sp.dma_start(out[bass.ds(n, 1), :, :].rearrange("o t d -> (o t) d"), y[:]).then_inc(s_out, 16)
            sp.wait_ge(s_out, 16 * C + 16)

        @block.gpsimd
        def _(pool):
            pool.wait_ge(s_scl, 1)
            with pool.Fori(0, C) as n:
                pool.wait_ge(s_sum, n + 1)
                pool.dma_start(h1[:], h1_dram[bass.ds(n, 1), :, :].rearrange("o t d -> (o t) d")).then_inc(s_h1, 16)
                pool.wait_ge(s_h1, n * 16 + 16)
                pool.wait_ge(s_lrt, n + 2)
                nc.gpsimd.tensor_tensor(lrt[:], lrt[:], h1[:], ALU.add).then_inc(s_sum, 1)

        @block.tensor
        def _(pe):
            def main(s, lo, hi, first):
                for i in range(lo, hi):
                    if first:
                        pe.wait_ge(s_q, i + 1)
                    for part in (hh, hl):
                        for b in two:
                            last = nc.tensor.matmul(acc[s][:, b, :], part[s][:, i, :], qd_sb[:, i, b * HALF:(b + 1) * HALF],
                                                    start=(i == 0 and part is hh), stop=(i == IT - 1 and part is hl))
                return last

            def low_rank(n):
                pe.wait_ge(s_pt, n)
                pe.wait_ge(s_lrt, n)
                for b in two:
                    last = nc.tensor.matmul(ps_l[:, b, :], pt[:], b_st[:, b * HALF:(b + 1) * HALF], start=True, stop=True)
                last.then_inc(s_lr, 1)

            def step(n, s, first=False):
                pe.wait_ge(s_hl, n + 1)
                if not first:
                    pe.wait_ge(s_scaled, n)
                main(s, 0, IT // 2, first)
                if not first:
                    low_rank(n)
                main(s, IT // 2, IT, first).then_inc(s_acc, 1)

            def last():
                low_rank(C)

            pe.wait_ge(s_b, 1)
            run(lambda: step(0, 0, True), step, last, pe)

        @block.scalar
        def _(act):
            def split(n, s):
                act.wait_ge(s_h, n * 16 + 16)
                nc.scalar.activation(hh[s][:], hraw[:], ACT.Copy).then_inc(s_hh, 1)

            def low_terms(n):
                nc.scalar.activation(pt[:], inner_st[:, bass.ds((n - 1) * P, P)].bitcast(F32), ACT.Copy).then_inc(s_pt, 1)
                act.wait_ge(s_lr, n)
                act.wait_ge(s_y, n)
                nc.scalar.activation(lrt[:], ps_l[:].rearrange("p b n -> p (b n)"), ACT.Copy, scale=LR_SCALE).then_inc(s_lrt, 1)

            def load(n):
                act.wait_ge(s_hl, n)
                act.dma_start(hraw[:], hid_dram.rearrange("i p t -> p i t")[:, :, bass.ds(n * P, P)]).then_inc(s_h, 16)

            def step(n, s):
                load(n + 1)
                act.wait_ge(s_acc, n)
                split(n + 1, 1 - s)
                low_terms(n)

            act.dma_start(scl[:], sd).then_inc(s_const, 16)
            act.dma_start(braw[:], db).then_inc(s_const, 16)
            split(0, 0)
            load(1)
            split(1, 1)
            with act.Fori(0, VIS - 1) as v:
                step(v * 2 + 1, 1)
                step(v * 2 + 2, 0)
            low_terms(C - 1)
            low_terms(C)

        @block.vector
        def _(dve):
            chain = Chain(dve, s_dve)
            tt = nc.vector.tensor_tensor

            def low_split(n, s):
                dve.wait_ge(s_hh, n + 1)
                tt(hl[s][:], hraw[:], hh[s][:].bitcast(F32), ALU.subtract).then_inc(s_hl, 1)

            def step(n, s, end=False):
                if not end:
                    low_split(n + 1, 1 - s)
                scale_sums(n, 1 - s)

            def scale_sums(n, s):
                dve.wait_ge(s_acc, n)
                dve.wait_ge(s_out, (n - 1) * 16 + 16)
                tt(y[:], acc[s][:].rearrange("p b n -> p (b n)"), scl[:], ALU.mult).then_inc(s_scaled, 1)
                dve.wait_ge(s_scaled, n + 1)
                dve.wait_ge(s_sum, n + 1)
                tt(y[:], y[:], lrt[:], ALU.add).then_inc(s_y, 1)

            low_split(0, 0)
            dve.wait_ge(s_const, 32)
            nc.vector.tensor_scalar(scl[:], scl[:], Q_STEP, None, ALU.mult).then_inc(s_scl, 1)
            chain.after(nc.vector.tensor_copy(b_st[:], braw[:]))
            for g in (1, 3):
                r = slice(R * g, R * g + R)
                last = tt(b_st[r, :], braw[r, :], b_st[r, :].bitcast(F32), ALU.subtract)
            last.then_inc(s_b, 1)
            for i in range(IT):
                dve.wait_ge(s_qload[i % QS], 16 * (i // QS + 1))
                nc.vector.tensor_scalar(qd_sb[:, i, :], qraw[i % QS][:], Q_ZERO, None, ALU.subtract).then_inc(s_q, 1)
            low_split(1, 1)
            with dve.Fori(0, VIS - 1) as v:
                step(v * 2 + 1, 1)
                step(v * 2 + 2, 0)
            step(C - 1, 1, True)
            scale_sums(C, 1)
    return sems


def retire(nc, sems):
    nc.clear_and_free_semaphores(sems)
    nc.all_engine_barrier()


def vit_tower(nc, t, out):
    h0_dram = nc.dram_tensor("h0_tokens", (C, H, D), F32, kind="Internal").ap()
    o_dram = nc.dram_tensor("o_features", (KT, P, TOK), F32, kind="Internal").ap()
    h1_dram = nc.dram_tensor("h1_tokens", (C, H, D), F32, kind="Internal").ap()
    hid_dram = nc.dram_tensor("hidden", (IT, P, TOK), F32, kind="Internal").ap()
    with ExitStack() as whole:
        with ExitStack() as st:
            ident = st.enter_context(nc.sbuf_tensor("ident", [P, P], F32))
            mask = st.enter_context(nc.sbuf_tensor("causal_mask", [P, P], F32))
            s_const = st.enter_context(nc.semaphore("const_loaded"))
            with nc.Block() as block:
                @block.sync
                def _(sp):
                    sp.dma_start(ident[:], t["ident"]).then_inc(s_const, 16)
                    sp.dma_start(mask[:], t["mask"]).then_inc(s_const, 16)
                    sp.wait_ge(s_const, 32)
            x_hi = st.enter_context(nc.sbuf_tensor("x_hi", [P, KT, TOK], F16))
            x_lo = st.enter_context(nc.sbuf_tensor("x_lo", [P, KT, TOK], F16))
            retire(nc, ssm_and_norm(nc, t["ssm"], t["c_re"], t["c_im"], h0_dram, x_hi, x_lo, ident))
            retire(nc, attention(nc, t["w_qkv"], t["b_qkv"], x_hi, x_lo, ident, mask, o_dram))
            low = st.enter_context(nc.sbuf_tensor("low_rank", [2 * R, TOK], F32))
            retire(nc, project_and_norm(nc, t["w_o"], t["b_o"], t["gu_a"], o_dram, h0_dram, h1_dram, x_hi, x_lo, low, ident))
            inner_st = whole.enter_context(nc.sbuf_tensor("inner_stack", [P, TOK], F32R, side="right"))
            retire(nc, gate_up(nc, t["gu_q"], t["gu_scale"], t["gu_b"], t["down_a"], x_hi, x_lo, low, hid_dram, inner_st))
        down(nc, t["down_q"], t["down_scale"], t["down_b"], inner_st, hid_dram, h1_dram, out)


def layouts(v):
    import numpy as np

    def padded(a, axis):
        room = list(a.shape)
        room[axis] = IT * P - a.shape[axis]
        return np.concatenate([a, np.zeros(room, a.dtype)], axis)

    def twice(a):
        return np.concatenate([a, a], 0)

    f = {n: np.asarray(a) for n, a in v.items()}
    x, b = f["x"], f["L0_tok_B"]
    q_gu = np.stack([padded(f["L0_ffn_gate_q"], 0), padded(f["L0_ffn_up_q"], 0)])
    s_gu = np.stack([padded(f["L0_ffn_gate_scale"], 0), padded(f["L0_ffn_up_scale"], 0)])
    b_gu = np.stack([padded(f["L0_ffn_gate_B"], 1), padded(f["L0_ffn_up_B"], 1)])
    wqkv = np.stack([f["L0_attn_Wq"], f["L0_attn_Wk"], f["L0_attn_Wv"]])
    bqkv = np.stack([f["L0_attn_bq"], f["L0_attn_bk"], f["L0_attn_bv"]])
    a_gu = np.concatenate([f["L0_ffn_gate_A"], f["L0_ffn_up_A"]], 1)
    at = np.arange(P)
    out = {
        "ssm": np.stack([np.broadcast_to(f["L0_tok_log_dt"], (P, H)), twice(f["L0_tok_inv_A_real"].T),
                         twice(f["L0_tok_A_imag"].T), twice(b[..., 0].T), twice(b[..., 1].T)], 1),
        "c_re": twice(x[..., 0].transpose(2, 1, 0)),
        "c_im": twice(x[..., 1].transpose(2, 1, 0)),
        "w_qkv": wqkv.reshape(3, KT, P, KT, P).transpose(1, 4, 0, 3, 2).reshape(KT, P, 3, D),
        "b_qkv": bqkv.reshape(3, KT, P).transpose(2, 0, 1),
        "w_o": f["L0_attn_Wo"].T.reshape(KT, P, D).transpose(1, 0, 2),
        "b_o": np.broadcast_to(f["L0_attn_bo"], (P, D)),
        "gu_a": a_gu.reshape(KT, P, 2 * R).transpose(1, 0, 2),
        "gu_q": q_gu.reshape(2, IT, P, KT, P).transpose(1, 4, 0, 3, 2).reshape(IT, P, 2, D),
        "gu_scale": s_gu.reshape(2, IT, P).transpose(2, 0, 1),
        "gu_b": np.tile(b_gu.reshape(2, R, IT, P).transpose(2, 1, 0, 3), (1, 4, 1, 1)),
        "down_q": padded(f["L0_ffn_down_q"], 1).T.reshape(IT, P, D).transpose(1, 0, 2),
        "down_scale": np.broadcast_to(f["L0_ffn_down_scale"], (P, D)),
        "down_a": padded(f["L0_ffn_down_A"], 0).reshape(IT, P, R).transpose(1, 0, 2),
        "down_b": np.tile(f["L0_ffn_down_B"], (4, 1)),
        "ident": np.eye(P, dtype=np.float32),
        "mask": np.where(at[:, None] >= at[None, :], 0.0, -3e38).astype(np.float32),
    }
    return {n: np.ascontiguousarray(a) for n, a in out.items()}


def kernel(**inputs):
    import numpy as np
    import concourse.bacc as bacc
    from concourse.bass_utils import run_bass_kernel_spmd

    arrays = layouts(inputs)
    nc = bacc.Bacc("TRN2", target_bir_lowering=False, num_devices=1)
    tensors = {n: nc.dram_tensor("in_" + n, a.shape, mybir.dt.from_np(a.dtype), kind="ExternalInput").ap()
               for n, a in arrays.items()}
    out = nc.dram_tensor("out_tokens", (C, H, D), F32, kind="ExternalOutput").ap()
    vit_tower(nc, tensors, out)
    r = run_bass_kernel_spmd(nc, [{"in_" + n: a for n, a in arrays.items()}], core_ids=[0])
    return np.asarray(r.results[0]["out_tokens"])
```

```python
import math
from contextlib import ExitStack

import concourse.bass as bass
from concourse import mybir

F32 = mybir.dt.float32
F32R = mybir.dt.float32r
F16 = mybir.dt.float16
BF16 = mybir.dt.bfloat16
I32 = mybir.dt.int32
ALU = mybir.AluOpType
ACT = mybir.ActivationFunctionType
X = mybir.AxisListType.X

P = 128
C, H, N = 16, 128, 64
D = 1024
KT = D // P
TOK = C * H
MAGIC = 1.5 * 2.0 ** 23
TWO_PI = 6.2831845
EPS = 1e-5


def bc(ap, n, at):
    shape = list(ap.shape)
    shape.insert(at, n)
    return ap.unsqueeze(at).broadcast_to(shape)


def start_free(nc, sems, count):
    for sem in sems:
        nc.sync.sem_inc(sem, count)


def apart(eng, passed, *waits):
    for sem, value in waits:
        eng.wait_ge(sem, value)
    eng.sem_inc(passed, 1)


class Chain:

    def __init__(self, eng, sem):
        self.eng, self.sem, self.count, self.turn = eng, sem, 0, 0

    def loop(self, it, n):
        self.turn = it * n

    def end(self, turns, n, first):
        assert self.count - first == n, (self.count - first, n)
        self.count, self.turn = first + turns * n, 0

    def mark(self, ins):
        self.count += 1
        ins.then_inc(self.sem, 1)
        return self.count

    def now(self):
        return self.turn + self.count

    def wait(self):
        self.eng.wait_ge(self.sem, self.now())

    def after(self, ins):
        self.mark(ins)
        self.wait()


UH = 8
UNITS = H // UH
CUT = 3
TI, TJ = 8, 16
TAB = 2 * TI + TJ
LAG = 6


def ssm_and_norm(nc, ssm, cr, ci, h0_dram, xn_hi, xn_lo, ident, w_first, raw, s_raw):
    sems = []
    with ExitStack() as st:
        def sb(name, shape, dt=F32):
            return st.enter_context(nc.sbuf_tensor(name, shape, dt))

        def sem(name):
            sems.append(nc.alloc_semaphore(name))
            return sems[-1]

        two = range(2)
        par = sb("ssm_par", [P, 5, H])
        cre, cim = sb("c_re", [P, H, C]), sb("c_im", [P, H, C])
        t01 = sb("ssm_t01", [P, 2, H])
        t = [t01[:, 0, :], t01[:, 1, :]] + [sb(f"ssm_t{k}", [P, H]) for k in range(2, 12)]
        er, ek, ew = sb("exp_r", [P, 2, H]), sb("exp_k", [P, 2, H]), sb("exp_w", [P, 2, H], I32)
        steps = sb("table_steps", [P, TAB])
        half = [sb(f"half{k}", [P, 1]) for k in range(7)]
        phase, mag = sb("phase", [P, H, TAB]), sb("magnitude", [P, H, TAB])
        tab1, tab2 = sb("table1", [P, H, TAB]), sb("table2", [P, H, TAB])
        a1, a2, at = (sb(n, [P, H, TI]) for n in ("a1", "a2", "a_tmp"))
        phase_room = phase[:].rearrange("p h k -> p (h k)").rearrange("p (s n) -> p s n", n=UH * P)
        mag_room = mag[:].rearrange("p h k -> p (h k)").rearrange("p (s n) -> p s n", n=UH * P)
        w = [[phase_room[:, 2 * s + k, :] for k in two] for s in two]
        v = [mag_room[:, s, :] for s in two]
        v_second = mag_room[:, 2, :]
        xt = [sb(f"n_xt{s}", [P, KT * C, UH]) for s in two]
        tok = [sb(f"n_tok{s}", [P, D]) for s in two]
        nrm = [sb(f"n_nrm{s}", [P, D]) for s in two]
        stats = [sb(f"n_stats{s}", [P, 2, 6]) for s in two]
        mv = [sb(f"n_mv{s}", [P, 2]) for s in two]
        std = [sb(f"n_std{s}", [P, 1]) for s in two]
        rs = [sb(f"n_rs{s}", [P, 2]) for s in two]
        eps = sb("n_eps", [P, 1])
        ps = [st.enter_context(nc.psum_tensor(f"ssm_ps{s}", [P, UH, P], F32)) for s in two]
        pt = st.enter_context(nc.psum_tensor("n_pt", [P, KT, P], F32))
        pn = st.enter_context(nc.psum_tensor("n_pn", [P, KT, P], F32))

        s_in, s_c, s_const, s_dve, s_z, s_expm, s_turn0 = (sem("a_" + n) for n in ("in", "c", "const", "dve", "z", "expm", "turn0"))
        s_decay, s_mag, s_phase, s_trig, s_tab1, s_tab2, s_a, s_passed = (
            sem("a_" + n) for n in ("decay", "mag", "phase", "trig", "tab1", "tab2", "a", "passed"))
        s_v1, s_v, s_w, s_mm, s_ev, s_tr, s_tok, s_mv, s_std, s_rs, s_nrm, s_trn, s_hi, s_lo, s_out = (
            [sem(f"a_{n}{s}") for s in two]
            for n in ("v1", "v", "w", "mm", "ev", "tr", "tok", "mv", "std", "rs", "nrm", "trn", "hi", "lo", "out"))
        logdt, inva, aim, br, bi = (par[:, k, :] for k in range(5))
        VIS = UNITS // 2
        start_free(nc, [*s_v, *s_mm, *s_ev, *s_tr, *s_tok, *s_nrm, *s_trn, *s_lo], 1)
        start_free(nc, [*s_out], 16)
        nc.all_engine_barrier()
        block = st.enter_context(nc.Block())

        def four(room, n):
            return room.rearrange("p (h a b) -> p h a b", h=UH, b=n)

        def channels(n, s, start=0, end=UH):
            return bass.ds((n * 2 + s) * UH + start, end - start)

        def run(eng, stages, chain=None, marks=0):
            def iterations(n, known):
                for b in two:
                    for lag, work in stages:
                        d = b - lag
                        if not known or 0 <= 2 * n + d < UNITS:
                            work(n + d // 2, d % 2)

            for n in range(LAG // 2):
                iterations(n, True)
            before = chain.count if chain else 0
            with eng.Fori(0, VIS - LAG // 2) as n:
                if chain:
                    chain.loop(n, marks)
                iterations(n + LAG // 2, False)
            if chain:
                chain.end(VIS - LAG // 2, marks, before)
            for n in range(VIS, VIS + LAG // 2):
                iterations(n, True)

        @block.sync
        def _(sp):
            sp.dma_start(par[:], ssm).then_inc(s_in, 16)
            sp.dma_start(cre[:], cr).then_inc(s_c, 16)
            sp.dma_start(cim[:], ci).then_inc(s_c, 16)
            sp.dma_start(raw[:], w_first).then_inc(s_raw, 16)
            with sp.Fori(0, VIS) as n:
                for s in two:
                    sp.wait_ge(s_tok[s], n + 2)
                    sp.dma_start(h0_dram[:, channels(n, s), :], tok[s][:]).then_inc(s_out[s], 16)
            for s in two:
                sp.wait_ge(s_out[s], 16 * VIS + 16)

        @block.gpsimd
        def _(pool):
            for at_, count, step in ((0, TI, P), (TI, TI, TJ), (2 * TI, TJ, 1)):
                nc.gpsimd.iota(steps[:, at_:at_ + count], [[step, count]], base=0, channel_multiplier=0,
                               allow_small_or_imprecise_dtypes=True).then_inc(s_const, 1)
            pool.wait_ge(s_const, 3 + 15)
            pool.wait_ge(s_z, 1)
            nc.gpsimd.tensor_tensor(mag[:], bc(t[2][:], TAB, 2), bc(steps[:], H, 1), ALU.mult).then_inc(s_decay, 1)
            pool.wait_ge(s_trig, 5)
            pool.wait_ge(s_mag, 1)
            nc.gpsimd.tensor_tensor(tab2[:], tab2[:], mag[:], ALU.mult).then_inc(s_tab2, 1)
            pool.wait_ge(s_tab2, 1)
            pool.wait_ge(s_tab1, 1)
            pool.wait_ge(s_c, 32)

            def factors(n, s):
                pool.wait_ge(s_mm[s], n + 1)
                nc.gpsimd.tensor_tensor(four(v[s], TJ), bc(tab1[:, channels(n, s), TI:2 * TI], TJ, 3),
                                        bc(tab1[:, channels(n, s), 2 * TI:TAB], TI, 2), ALU.mult).then_inc(s_v1[s], 1)
                pool.wait_ge(s_a, 2)
                nc.gpsimd.tensor_tensor(four(w[s][0], C), bc(a1[:, channels(n, s), :], C, 3),
                                        bc(cre[:, channels(n, s), :], KT, 2), ALU.mult)
                hs = channels(n, s, 0, CUT)
                nc.gpsimd.tensor_tensor(four(w[s][1], C)[:, 0:CUT], bc(a2[:, hs, :], C, 3), bc(cim[:, hs, :], KT, 2),
                                        ALU.mult).then_inc(s_w[s], 1)

            run(pool, [(0, factors)])

        @block.tensor
        def _(pe):
            def product(n, s):
                pe.wait_ge(s_v[s], n + 2)
                pe.wait_ge(s_w[s], n * 2 + 2)
                pe.wait_ge(s_ev[s], n + 1)
                for h in range(UH):
                    cols = slice(h * P, (h + 1) * P)
                    for k in two:
                        last = nc.tensor.matmul(ps[s][:, h, :], v[s][:, cols], w[s][k][:, cols], start=(k == 0), stop=(k == 1))
                last.then_inc(s_mm[s], 1)

            def to_tokens(n, s):
                pe.wait_ge(s_ev[s], n + 2)
                pe.wait_ge(s_tok[1 - s], n + 1 + s)
                for i in range(KT):
                    last = nc.tensor.transpose(pt[:, i, :], xt[s][:, i * C:(i + 1) * C, :].rearrange("p c h -> p (c h)"), ident[:])
                last.then_inc(s_tr[s], 1)

            def to_features(n, s):
                pe.wait_ge(s_nrm[s], n + 2)
                pe.wait_ge(s_lo[1 - s], n + 1 + s)
                for i in range(KT):
                    last = nc.tensor.transpose(pn[:, i, :], nrm[s][:, i * P:(i + 1) * P], ident[:])
                last.then_inc(s_trn[s], 1)

            run(pe, [(5, to_features), (1, product), (2, to_tokens)])

        @block.scalar
        def _(act):
            act.wait_ge(s_z, 1)
            nc.scalar.activation(t[4][:], t[2][:], ACT.Exp).then_inc(s_expm, 1)
            nc.scalar.activation(t[5][:], t[2][:], ACT.Tanh, scale=0.5).then_inc(s_expm, 1)
            act.wait_ge(s_decay, 1)
            nc.scalar.activation(mag[:], mag[:], ACT.Exp).then_inc(s_mag, 1)
            act.wait_ge(s_phase, 3)
            act.wait_ge(s_const, 3 + 15)
            i, j1, j0 = slice(0, TI), slice(TI, 2 * TI), slice(2 * TI, TAB)
            quarter = half[5]
            nc.scalar.activation(tab1[:, :, 0:2 * TI], tab1[:, :, 0:2 * TI], ACT.Sin, scale=-TWO_PI, bias=quarter[:]).then_inc(s_trig, 1)
            nc.scalar.activation(tab1[:, :, j0], tab1[:, :, j0], ACT.Sin, scale=half[1][:], bias=half[3][:]).then_inc(s_trig, 1)
            nc.scalar.activation(tab2[:, :, i], phase[:, :, i], ACT.Sin, scale=TWO_PI).then_inc(s_trig, 1)
            nc.scalar.activation(tab2[:, :, j1], phase[:, :, j1], ACT.Sin, scale=half[1][:]).then_inc(s_trig, 1)
            nc.scalar.activation(tab2[:, :, j0], tab2[:, :, j0], ACT.Sin, scale=half[2][:], bias=half[4][:]).then_inc(s_trig, 1)

            def columns(n, s):
                act.wait_ge(s_mm[s], n + 2)
                act.wait_ge(s_tr[s], n + 1)
                nc.scalar.activation(xt[s][:], ps[s][:].rearrange("p h m -> p m h"), ACT.Copy).then_inc(s_ev[s], 1)

            def deviation(n, s):
                act.wait_ge(s_mv[s], n + 1)
                nc.scalar.activation(std[s][:], mv[s][:, 1:2], ACT.Sqrt, bias=eps[:]).then_inc(s_std[s], 1)

            def tokens(n, s):
                act.wait_ge(s_tr[s], n + 2)
                act.wait_ge(s_nrm[s], n + 1)
                act.wait_ge(s_out[s], n * 16 + 16)
                nc.scalar.activation(tok[s][:].rearrange("p (i j) -> p i j", j=P), pt[:], ACT.Copy).then_inc(s_tok[s], 1)

            def normalise(n, s):
                apart(act, s_passed, (s_rs[s], n + 1), (s_trn[s], n + 1))
                nc.scalar.activation(nrm[s][:], tok[s][:], ACT.Identity, scale=rs[s][:, 0:1], bias=rs[s][:, 1:2]).then_inc(s_nrm[s], 1)

            def high(n, s):
                apart(act, s_passed, (s_trn[s], n + 2))
                nc.scalar.activation(xn_hi[:].rearrange("p k (c h) -> p k c h", h=H)[:, :, :, channels(n, s)],
                                     pn[:].rearrange("p k (c h) -> p k c h", h=UH), ACT.Copy).then_inc(s_hi[s], 1)

            run(act, [(2, columns), (4, deviation), (3, tokens), (4, normalise), (5, high)])

        @block.vector
        def _(dve):
            chain = Chain(dve, s_dve)
            tt, ts = nc.vector.tensor_tensor, nc.vector.tensor_scalar
            nc.vector.memset(eps[:], EPS).then_inc(s_const, 1)
            for k, (above, below) in enumerate(((-1.0, 1.0), (-TWO_PI, TWO_PI), (TWO_PI, -TWO_PI), (math.pi / 2, 0.0),
                                                (0.0, math.pi / 2), (math.pi / 2, math.pi / 2), (1.0, -1.0))):
                nc.vector.memset(half[k][0:N, :], above).then_inc(s_const, 1)
                nc.vector.memset(half[k][N:P, :], below).then_inc(s_const, 1)
            dve.wait_ge(s_in, 16)
            chain.after(ts(er[:], par[:, 0:2, :], -87.0, 88.0, ALU.max, ALU.min))
            chain.after(ts(ek[:], er[:], 1.0 / math.log(2.0), None, ALU.mult))
            chain.after(ts(ek[:], ek[:], MAGIC, MAGIC, ALU.add, ALU.subtract))
            chain.mark(ts(ew[:], ek[:], 127.0, 2.0 ** 23, ALU.add, ALU.mult))
            chain.after(nc.vector.scalar_tensor_tensor(er[:], ek[:], -0.693359375, er[:], ALU.mult, ALU.add))
            chain.after(nc.vector.scalar_tensor_tensor(er[:], ek[:], 2.12194440e-4, er[:], ALU.mult, ALU.add))
            chain.after(ts(ek[:], er[:], 1 / math.factorial(7), None, ALU.mult))
            for k in range(6, 0, -1):
                chain.after(nc.vector.scalar_tensor_tensor(ek[:], ek[:], 1 / math.factorial(k), er[:], ALU.add, ALU.mult))
            chain.after(nc.vector.scalar_tensor_tensor(t01[:], ek[:], 1.0, ew[:].bitcast(F32), ALU.add, ALU.mult))
            chain.after(tt(t[2][:], t[1][:], t[0][:], ALU.mult))
            chain.after(ts(t[2][:], t[2][:], -1.0, None, ALU.mult))
            chain.after(tt(t[3][:], aim, t[0][:], ALU.mult))
            ts(t[3][:], t[3][:], 1.0 / (2 * math.pi), None, ALU.mult).then_inc(s_z, 1)
            dve.wait_ge(s_z, 1)
            dve.wait_ge(s_const, 3 + 15)

            chain.mark(nc.vector.tensor_copy(t[6][:], t[3][:]))
            chain.after(tt(phase[:], bc(t[3][:], TAB, 2), bc(steps[:], H, 1), ALU.mult))
            chain.after(ts(tab1[:], phase[:], MAGIC, MAGIC, ALU.add, ALU.subtract))
            tt(phase[:], phase[:], tab1[:], ALU.subtract).then_inc(s_phase, 1)
            dve.wait_ge(s_phase, 1)
            pair, j0 = slice(0, 2 * TI), slice(2 * TI, TAB)
            stt = nc.vector.scalar_tensor_tensor
            stt(tab1[:, :, pair], phase[:, :, pair], -1.0, phase[:, :, pair], ALU.mult, ALU.max).then_inc(s_phase, 1)
            chain.mark(stt(tab1[:, :, j0], phase[:, :, j0], half[0][:], phase[:, :, j0], ALU.mult, ALU.max))
            stt(tab2[:, :, j0], phase[:, :, j0], half[6][:], phase[:, :, j0], ALU.mult, ALU.max).then_inc(s_phase, 1)
            ts(t[8][:], t[6][:], MAGIC, MAGIC, ALU.add, ALU.subtract).then_inc(s_turn0, 1)
            dve.wait_ge(s_turn0, 1)
            chain.after(tt(t[6][:], t[6][:], t[8][:], ALU.subtract))
            chain.after(ts(t[6][:], t[6][:], math.pi, None, ALU.mult))
            y, y2, sin, cos = t[6], t[8], t[7], t[9]
            chain.after(tt(y2[:], y[:], y[:], ALU.mult))
            chain.mark(ts(sin[:], y2[:], 1 / math.factorial(13), None, ALU.mult))
            chain.after(ts(cos[:], y2[:], 1 / math.factorial(12), None, ALU.mult))
            for k in range(5, 0, -1):
                chain.mark(nc.vector.scalar_tensor_tensor(sin[:], sin[:], (-1) ** k / math.factorial(2 * k + 1), y2[:], ALU.add, ALU.mult))
                chain.after(nc.vector.scalar_tensor_tensor(cos[:], cos[:], (-1) ** k / math.factorial(2 * k), y2[:], ALU.add, ALU.mult))
            chain.mark(ts(cos[:], cos[:], 1.0, None, ALU.add))
            chain.after(nc.vector.scalar_tensor_tensor(sin[:], sin[:], 1.0, y[:], ALU.add, ALU.mult))
            chain.after(tt(y[:], sin[:], cos[:], ALU.mult))
            chain.after(ts(y[:], y[:], 2.0, None, ALU.mult))
            dve.wait_ge(s_expm, 2)
            chain.after(ts(t[8][:], t[4][:], 1.0, None, ALU.add))
            chain.after(tt(t[8][:], t[8][:], t[5][:], ALU.mult))
            chain.after(tt(t[7][:], t[7][:], t[7][:], ALU.mult))
            chain.after(tt(t[7][:], t[7][:], t[4][:], ALU.mult))
            chain.after(ts(t[7][:], t[7][:], -2.0, None, ALU.mult))
            chain.mark(tt(t[6][:], t[6][:], t[4][:], ALU.mult))
            chain.after(tt(t[7][:], t[7][:], t[8][:], ALU.add))
            chain.mark(tt(t[8][:], br, t[7][:], ALU.mult))
            chain.mark(tt(t[9][:], bi, t[6][:], ALU.mult))
            chain.mark(tt(t[10][:], br, t[6][:], ALU.mult))
            chain.after(tt(t[11][:], bi, t[7][:], ALU.mult))
            chain.mark(tt(t[8][:], t[8][:], t[9][:], ALU.subtract))
            chain.after(tt(t[10][:], t[10][:], t[11][:], ALU.add))
            chain.mark(tt(t[4][:], t[1][:], t[1][:], ALU.mult))
            chain.mark(tt(t[5][:], aim, aim, ALU.mult))
            chain.mark(tt(t[6][:], t[8][:], t[1][:], ALU.mult))
            chain.mark(tt(t[7][:], t[10][:], aim, ALU.mult))
            chain.mark(tt(t[9][:], t[8][:], aim, ALU.mult))
            chain.after(tt(t[11][:], t[10][:], t[1][:], ALU.mult))
            chain.mark(tt(t[4][:], t[4][:], t[5][:], ALU.add))
            chain.mark(tt(t[6][:], t[7][:], t[6][:], ALU.subtract))
            chain.after(tt(t[9][:], t[9][:], t[11][:], ALU.add))
            chain.after(nc.vector.reciprocal(t[4][:], t[4][:]))
            chain.after(ts(t[4][:], t[4][:], 2.0, None, ALU.mult))
            chain.mark(tt(t[6][:], t[6][:], t[4][:], ALU.mult))
            chain.after(tt(t[9][:], t[9][:], t[4][:], ALU.mult))
            a, b = t[7], t[8]
            chain.mark(nc.vector.tensor_copy(a[0:N, :], t[6][0:N, :]))
            chain.mark(nc.vector.tensor_copy(a[N:P, :], t[9][N:P, :]))
            chain.mark(nc.vector.tensor_copy(b[0:N, :], t[9][0:N, :]))
            chain.after(ts(b[N:P, :], t[6][N:P, :], -1.0, None, ALU.mult))
            dve.wait_ge(s_trig, 2)
            dve.wait_ge(s_mag, 1)
            tt(tab1[:], tab1[:], mag[:], ALU.mult).then_inc(s_tab1, 1)
            dve.wait_ge(s_tab1, 1)
            dve.wait_ge(s_tab2, 1)
            e_re, e_im = tab1[:, :, 0:TI], tab2[:, :, 0:TI]
            chain.mark(tt(a1[:], bc(a[:], TI, 2), e_re, ALU.mult))
            chain.mark(tt(a2[:], bc(b[:], TI, 2), e_re, ALU.mult))
            chain.after(tt(at[:], bc(b[:], TI, 2), e_im, ALU.mult))
            tt(a1[:], a1[:], at[:], ALU.add).then_inc(s_a, 1)
            dve.wait_ge(s_a, 1)
            chain.after(tt(at[:], bc(a[:], TI, 2), e_im, ALU.mult))
            tt(a2[:], a2[:], at[:], ALU.subtract).then_inc(s_a, 1)
            dve.wait_ge(s_a, 2)
            dve.wait_ge(s_c, 32)

            def factors(n, s):
                dve.wait_ge(s_mm[s], n + 1)
                hs = channels(n, s, CUT, UH)
                tt(four(w[s][1], C)[:, CUT:UH], bc(a2[:, hs, :], C, 3), bc(cim[:, hs, :], KT, 2), ALU.mult).then_inc(s_w[s], 1)
                dve.wait_ge(s_v[1 - s], n + 1 + s)
                chain.after(tt(four(v_second, TJ), bc(tab2[:, channels(n, s), TI:2 * TI], TJ, 3),
                               bc(tab2[:, channels(n, s), 2 * TI:TAB], TI, 2), ALU.mult))
                dve.wait_ge(s_v1[s], n + 1)
                tt(v[s], v[s], v_second, ALU.add).then_inc(s_v[s], 1)

            def moments(n, s):
                dve.wait_ge(s_tok[s], n + 2)
                chain.mark(nc.vector.bn_stats(stats[s][:, 0, :], tok[s][:, 0:512]))
                chain.mark(nc.vector.bn_stats(stats[s][:, 1, :], tok[s][:, 512:D]))
                apart(dve, s_passed, (s_dve, chain.now()))
                nc.vector.bn_aggr(mv[s][:], stats[s][:].rearrange("p a b -> p (a b)")).then_inc(s_mv[s], 1)

            def inverse(n, s):
                dve.wait_ge(s_std[s], n + 1)
                chain.after(nc.vector.reciprocal(rs[s][:, 0:1], std[s][:]))
                nc.vector.scalar_tensor_tensor(rs[s][:, 1:2], mv[s][:, 0:1], -1.0, rs[s][:, 0:1], ALU.mult, ALU.mult).then_inc(s_rs[s], 1)

            def low(n, s):
                dve.wait_ge(s_hi[s], n + 1)
                tt(xn_lo[:].rearrange("p k (c h) -> p k c h", h=H)[:, :, :, channels(n, s)], pn[:].rearrange("p k (c h) -> p k c h", h=UH),
                   xn_hi[:].rearrange("p k (c h) -> p k c h", h=H)[:, :, :, channels(n, s)], ALU.subtract).then_inc(s_lo[s], 1)

            run(dve, [(4, inverse), (0, factors), (3, moments), (5, low)], chain, 2 * 4)
    return sems


HEADS, HD = 32, 32
HPT = P // HD
CH = 512
NCH = TOK // CH
BPC = CH // H
RMAX = bass.bass_isa.ReduceOp.max
W_TOP = 2.0 ** 13


def split_scales(chain, big, low, scale, back):
    chain.after(nc_ts(chain, low, big, 1e-30, None, ALU.max))
    chain.after(nc_ts(chain, low.bitcast(I32), low.bitcast(I32), 0x7F800000, None, ALU.bitwise_and))
    chain.after(chain.eng.reciprocal(scale, low))
    chain.after(nc_ts(chain, scale, scale, W_TOP, None, ALU.mult))
    return nc_ts(chain, back, low, 1.0 / W_TOP, None, ALU.mult)


def nc_ts(chain, *args):
    return chain.eng.tensor_scalar(*args)


def attention(nc, wqkv, bqkv, raw, s_raw, xn_hi, xn_lo, ident, mask, o_dram):
    sems = []
    with ExitStack() as st:
        def sb(name, shape, dt=F32):
            return st.enter_context(nc.sbuf_tensor(name, shape, dt))

        def ps(name, shape):
            return st.enter_context(nc.psum_tensor(name, shape, F32))

        def sem(name):
            sems.append(nc.alloc_semaphore(name))
            return sems[-1]

        two = range(2)
        w_hi = [sb(f"w_hi{s}", [P, 3, D], F16) for s in two]
        w_lo = [sb(f"w_lo{s}", [P, 3, D], F16) for s in two]
        big, bigs, low2 = sb("w_big", [P, 3]), sb("w_bigs", [P, 3]), sb("w_pow", [P, 3])
        scale, back = sb("w_scale", [P, 3]), [sb(f"w_back{s}", [P, 3]) for s in two]
        bias = sb("b_qkv", [P, 3, KT])
        qf, kf, vf = sb("qf", [P, CH]), sb("kf", [P, CH]), sb("vf", [P, CH])
        qh, ql = sb("qh", [P, CH], F32R), sb("ql", [P, CH], F32R)
        kh, kl = (sb(n, [P, BPC, HPT, H], F32R) for n in ("kh", "kl"))
        vh, vl = (sb(n, [P, BPC, P], F32R) for n in ("vh", "vl"))
        prob = [sb(f"prob{p}", [P, 2 * HPT, H]) for p in two]
        mx, sm = ([sb(f"{n}{p}", [P, 2 * HPT]) for p in two] for n in ("mx", "sm"))
        pth, ptl = ([sb(f"{n}{p}", [P, 2, HPT * H], F32R) for p in two] for n in ("pth", "ptl"))
        ot = [sb(f"ot{s}", [P, CH]) for s in two]
        ps_a, ps_b = ps("ps_a", [P, CH]), ps("ps_b", [P, CH])
        ps_s, ps_t, ps_o = ps("ps_s", [P, 2, CH]), ps("ps_t", [P, 2, CH]), ps("ps_o", [P, 2, CH])

        s_bias, s_big, s_bigs, s_scale, s_whi, s_wlo = (
            sem("c_" + n) for n in ("bias", "big", "bigs", "scale", "whi", "wlo"))
        s_passed = sem("c_passed")
        s_zero = sem("c_zero")
        s_pq, s_pk, s_pv, s_vt = (sem("c_" + n) for n in ("pq", "pk", "pv", "vt"))
        s_qf, s_kf, s_vf, s_ql, s_kl, s_vl = (sem("c_" + n) for n in ("qf", "kf", "vf", "ql", "kl", "vl"))
        s_score, s_mask, s_max, s_sub, s_exp, s_rc, s_prob, s_tr, s_pth, s_ptl, s_pvd, s_ox, s_od = (
            [sem(f"c_{n}{p}") for p in two]
            for n in ("score", "mask", "max", "sub", "exp", "rc", "prob", "tr", "pth", "ptl", "pvd", "ox", "od"))
        s_dve = sem("c_dve")
        TURN = 2 * NCH
        TURNS = KT // 2
        start_free(nc, [*s_od], 16)
        nc.all_engine_barrier()
        block = st.enter_context(nc.Block())

        def where(u, k):
            return u * TURN + k, (k // NCH) % 2, u * 2 + k // NCH, k % NCH

        def run(eng, first, step, last, chain=None, marks=0):
            first()
            before = chain.count if chain else 0
            with eng.Fori(0, TURNS - 1) as u:
                if chain:
                    chain.loop(u, marks)
                for k in range(1, TURN + 1):
                    step(u, k)
            if chain:
                chain.end(TURNS - 1, marks, before)
            for k in range(1, TURN):
                step(TURNS - 1, k)
            last()

        @block.sync
        def _(sp):
            sp.dma_start(bias[:], bqkv).then_inc(s_bias, 16)
            sp.wait_ge(s_wlo, 3)
            sp.dma_start(raw[:], wqkv[1, :, :, :]).then_inc(s_raw, 16)

            def store(u):
                for s in two:
                    for c in range(NCH):
                        n, par = u * TURN + s * NCH + c, c % 2
                        sp.wait_ge(s_ox[1], n + 1)
                        sp.dma_start(o_dram[bass.ds(u * 2 + s, 1), :, c * CH:(c + 1) * CH].rearrange("o f t -> (o f) t"),
                                     ot[par][:]).then_inc(s_od[par], 16)
                        if c == NCH - 1 and not isinstance(u, int):
                            sp.wait_ge(s_wlo, (u * 2 + s + 2) * 3)
                            sp.dma_start(raw[:], wqkv[bass.ds(u * 2 + s + 2, 1), :, :, :].rearrange("o p m n -> (o p) m n")
                                         ).then_inc(s_raw, 16)

            with sp.Fori(0, TURNS - 1) as u:
                store(u)
            store(TURNS - 1)
            for par in two:
                sp.wait_ge(s_od[par], 16 * (KT * NCH // 2) + 16)

        @block.gpsimd
        def _(pool):
            nc.gpsimd.memset(kh[:].bitcast(F32), 0.0).then_inc(s_zero, 1)
            nc.gpsimd.memset(kl[:].bitcast(F32), 0.0).then_inc(s_zero, 1)

            def reduce_big(j):
                apart(pool, s_passed, (s_big, j + 1), (s_scale, j))
                nc.gpsimd.partition_all_reduce(bigs[:], big[:], P, RMAX).then_inc(s_bigs, 1)

            def step(u, k, first=False):
                t, ws, j, c = where(u, k)
                for p in two:
                    pool.wait_ge(s_max[p], t + 1)
                    nc.gpsimd.tensor_tensor(prob[p][:], prob[p][:], bc(mx[p][:], H, 2), ALU.subtract).then_inc(s_sub[p], 1)
                for p in two:
                    pool.wait_ge(s_rc[p], t + 1)
                    nc.gpsimd.tensor_tensor(prob[p][:], prob[p][:], bc(sm[p][:], H, 2), ALU.mult).then_inc(s_prob[p], 1)
                if c == 0 and not (isinstance(u, int) and u == TURNS - 1 and k >= NCH):
                    reduce_big(j + 1)

            reduce_big(0)
            run(pool, lambda: step(0, 0), step, lambda: None)

        @block.tensor
        def _(pe):
            def project(m, out, ws, c):
                tok = slice(c * CH, (c + 1) * CH)
                for k in range(KT):
                    w = slice(k * P, (k + 1) * P)
                    nc.tensor.matmul(out[:], w_hi[ws][:, m, w], xn_hi[:, k, tok], start=(k == 0), stop=False)
                    nc.tensor.matmul(out[:], w_hi[ws][:, m, w], xn_lo[:, k, tok], start=False, stop=False)
                    last = nc.tensor.matmul(out[:], w_lo[ws][:, m, w], xn_hi[:, k, tok], start=False, stop=(k == KT - 1))
                return last

            def transposes(p):
                for b in two:
                    for a in range(HPT):
                        last = nc.tensor.transpose(ps_t[:, b, a * H:(a + 1) * H], prob[p][:, b * HPT + a, :], ident[:])
                return last

            def values(p):
                for b in two:
                    at = p * 2 + b
                    nc.tensor.matmul(ps_o[:, b, :], vh[:, at, :], pth[p][:, b, :], start=True, stop=False)
                    nc.tensor.matmul(ps_o[:, b, :], vh[:, at, :], ptl[p][:, b, :], start=False, stop=False)
                    last = nc.tensor.matmul(ps_o[:, b, :], vl[:, at, :], pth[p][:, b, :], start=False, stop=True)
                return last

            def scores(p):
                for b in two:
                    at = p * 2 + b
                    q, k = slice(at * H, (at + 1) * H), slice(0, HPT)
                    nc.tensor.matmul(ps_s[:, b, :], qh[:, q], kh[:, at, k, :], start=True, stop=False)
                    nc.tensor.matmul(ps_s[:, b, :], qh[:, q], kl[:, at, k, :], start=False, stop=False)
                    last = nc.tensor.matmul(ps_s[:, b, :], ql[:, q], kh[:, at, k, :], start=False, stop=True)
                return last

            def attend_first(t):
                pe.wait_ge(s_prob[0], t)
                transposes(0).then_inc(s_tr[0], 1)

            def attend_second(t):
                pe.wait_ge(s_prob[1], t)
                pe.wait_ge(s_ptl[0], t)
                transposes(1).then_inc(s_tr[1], 1)
                pe.wait_ge(s_vl, t)
                values(0).then_inc(s_pvd[0], 1)

            def attend_third(t):
                pe.wait_ge(s_ptl[1], t)
                pe.wait_ge(s_ox[0], t)
                values(1).then_inc(s_pvd[1], 1)

            def step(u, k, first=False):
                t, ws, j, c = where(u, k)
                if c == 0:
                    pe.wait_ge(s_wlo, 3 * j + 1)
                pe.wait_ge(s_vf, t)
                project(0, ps_a, ws, c).then_inc(s_pq, 1)
                if c == 0:
                    pe.wait_ge(s_wlo, 3 * j + 2)
                pe.wait_ge(s_vl, t)
                project(1, ps_b, ws, c).then_inc(s_pk, 1)
                if not first:
                    attend_first(t)
                if c == 0:
                    pe.wait_ge(s_wlo, 3 * j + 3)
                pe.wait_ge(s_qf, t + 1)
                project(2, ps_a, ws, c).then_inc(s_pv, 1)
                if not first:
                    attend_second(t)
                pe.wait_ge(s_ql, t + 1)
                pe.wait_ge(s_kl, t + 1)
                pe.wait_ge(s_mask[1], t)
                scores(0).then_inc(s_score[0], 1)
                if not first:
                    attend_third(t)
                pe.wait_ge(s_vf, t + 1)
                pe.wait_ge(s_kf, t + 1)
                for b in range(BPC):
                    last = nc.tensor.transpose(ps_b[:, b * P:(b + 1) * P], vf[:, b * H:(b + 1) * H], ident[:])
                last.then_inc(s_vt, 1)
                pe.wait_ge(s_mask[0], t + 1)
                scores(1).then_inc(s_score[1], 1)

            def last():
                t = KT * NCH
                attend_first(t)
                attend_second(t)
                attend_third(t)

            run(pe, lambda: step(0, 0, True), step, last)

        @block.scalar
        def _(act):
            def high_weights(ws, j, m):
                act.wait_ge(s_scale, j + 1)
                nc.scalar.activation(w_hi[ws][:, m, :], raw[:, m, :], ACT.Copy, scale=scale[:, m:m + 1]).then_inc(s_whi, 1)

            def outputs(p, n_par, v, t):
                act.wait_ge(s_pvd[p], t)
                if p == 0:
                    act.wait_ge(s_od[n_par], v * 16 + 16)
                for a in range(HPT):
                    r = slice(HD * a, HD * a + HD)
                    last = nc.scalar.activation(ot[n_par][r, p * 2 * H:(p + 1) * 2 * H].rearrange("p (b q) -> p b q", q=H),
                                                ps_o[r, :, a * H:(a + 1) * H], ACT.Copy)
                last.then_inc(s_ox[p], 1)

            def attend(u, k, part):
                t = u * TURN + k
                n_par, v = (k - 1) % 2, u * (TURN // 2) + (k - 1) // 2
                if part < 2:
                    act.wait_ge(s_tr[part], t)
                    nc.scalar.activation(pth[part][:], ps_t[:], ACT.Copy).then_inc(s_pth[part], 1)
                else:
                    outputs(part - 2, n_par, v, t)

            def step(u, k, first=False):
                t, ws, j, c = where(u, k)
                apart(act, s_passed, (s_pq, t + 1), (s_ql, t))
                nc.scalar.activation(qf[:], ps_a[:], ACT.Identity, scale=back[ws][:, 0:1],
                                     bias=bias[:, 0, bass.ds(j, 1)]).then_inc(s_qf, 1)
                apart(act, s_passed, (s_pk, t + 1), (s_kl, t))
                nc.scalar.activation(kf[:], ps_b[:], ACT.Identity, scale=back[ws][:, 1:2],
                                     bias=bias[:, 1, bass.ds(j, 1)]).then_inc(s_kf, 1)
                if not first:
                    attend(u, k, 0)
                apart(act, s_passed, (s_pv, t + 1))
                nc.scalar.activation(vf[:], ps_a[:], ACT.Identity, scale=back[ws][:, 2:3],
                                     bias=bias[:, 2, bass.ds(j, 1)]).then_inc(s_vf, 1)
                if not first:
                    attend(u, k, 1)
                    attend(u, k, 2)
                    attend(u, k, 3)
                for p in two:
                    act.wait_ge(s_sub[p], t + 1)
                    nc.scalar.activation(prob[p][:], prob[p][:], ACT.Exp).then_inc(s_exp[p], 1)
                if c >= 1 and not (isinstance(u, int) and u == TURNS - 1 and k >= NCH):
                    act.wait_ge(s_pv, t + 1)
                    high_weights(1 - ws, j + 1, c - 1)

            act.wait_ge(s_bias, 16)
            for m in range(3):
                high_weights(0, 0, m)
            run(act, lambda: step(0, 0, True), step, lambda: [attend(TURNS - 1, TURN, part) for part in range(4)])

        @block.vector
        def _(dve):
            chain = Chain(dve, s_dve)
            tt = nc.vector.tensor_tensor

            def find_big(j):
                dve.wait_ge(s_raw, 16 * (j + 1))
                nc.vector.tensor_reduce(big[:], raw[:], X, ALU.max, apply_absolute_value=True).then_inc(s_big, 1)

            def find_scales(ws, j):
                dve.wait_ge(s_bigs, j + 1)
                split_scales(chain, bigs[:], low2[:], scale[:], back[ws][:]).then_inc(s_scale, 1)

            def low_weights(ws, j, m):
                dve.wait_ge(s_whi, 3 * j + m + 1)
                nc.vector.scalar_tensor_tensor(w_lo[ws][:, m, :], raw[:, m, :], scale[:, m:m + 1], w_hi[ws][:, m, :],
                                               ALU.mult, ALU.subtract).then_inc(s_wlo, 1)

            def attend(t, p):
                dve.wait_ge(s_pth[p], t)
                tt(ptl[p][:], ps_t[:], pth[p][:].bitcast(F32), ALU.subtract).then_inc(s_ptl[p], 1)

            def top(t, p):
                dve.wait_ge(s_score[p], t + 1)
                nc.vector.scalar_tensor_tensor(prob[p][:], ps_s[:].rearrange("p b (a k) -> p (b a) k", k=H), HD ** -0.5,
                                               bc(mask[:], 2 * HPT, 1), ALU.mult, ALU.add).then_inc(s_mask[p], 1)
                dve.wait_ge(s_mask[p], t + 1)
                nc.vector.tensor_reduce(mx[p][:], prob[p][:], X, ALU.max).then_inc(s_max[p], 1)

            def step(u, k, first=False):
                t, ws, j, c = where(u, k)
                dve.wait_ge(s_qf, t + 1)
                chain.after(nc.vector.tensor_copy(qh[:], qf[:]))
                tt(ql[:], qf[:], qh[:].bitcast(F32), ALU.subtract).then_inc(s_ql, 1)
                dve.wait_ge(s_kf, t + 1)
                for a in range(HPT):
                    r = slice(HD * a, HD * a + HD)
                    last = nc.vector.tensor_copy(kh[r, :, a, :], kf[r, :].rearrange("p (b k) -> p b k", k=H))
                chain.after(last)
                if not first:
                    attend(t, 0)
                for a in range(HPT):
                    r = slice(HD * a, HD * a + HD)
                    last = tt(kl[r, :, a, :], kf[r, :].rearrange("p (b k) -> p b k", k=H), kh[r, :, a, :].bitcast(F32), ALU.subtract)
                last.then_inc(s_kl, 1)
                if not first:
                    attend(t, 1)
                top(t, 0)
                dve.wait_ge(s_vt, t + 1)
                chain.after(nc.vector.tensor_copy(vh[:].rearrange("p b f -> p (b f)"), ps_b[:]))
                tt(vl[:].rearrange("p b f -> p (b f)"), ps_b[:], vh[:].rearrange("p b f -> p (b f)").bitcast(F32),
                   ALU.subtract).then_inc(s_vl, 1)
                top(t, 1)
                for p in two:
                    dve.wait_ge(s_exp[p], t + 1)
                    chain.after(nc.vector.tensor_reduce(sm[p][:], prob[p][:], X, ALU.add))
                    nc.vector.reciprocal(sm[p][:], sm[p][:]).then_inc(s_rc[p], 1)
                if c == 0 and not (isinstance(u, int) and u == TURNS - 1 and k >= NCH):
                    find_big(j + 1)
                if c == 1 and not (isinstance(u, int) and u == TURNS - 1 and k >= NCH):
                    find_scales(1 - ws, j + 1)
                if c >= 1 and not (isinstance(u, int) and u == TURNS - 1 and k >= NCH):
                    low_weights(1 - ws, j + 1, c - 1)

            find_big(0)
            find_scales(0, 0)
            for m in range(3):
                low_weights(0, 0, m)
            dve.wait_ge(s_zero, 2)
            run(dve, lambda: step(0, 0, True), step, lambda: [attend(KT * NCH, p) for p in two],
                chain, TURN * 5 + 2 * 4)
    return sems


R = 32
BEHIND_D = 6


def project_and_norm(nc, wo, bo, ga, o_dram, h0_dram, h1_dram, x2_hi, x2_lo, low, ident):
    sems = []
    with ExitStack() as st:
        def sb(name, shape, dt=F32):
            return st.enter_context(nc.sbuf_tensor(name, shape, dt))

        def sem(name):
            sems.append(nc.alloc_semaphore(name))
            return sems[-1]

        two = range(2)
        wraw = [sb(f"wo_raw{s}", [P, D]) for s in two]
        woh, wol = sb("wo_hi", [P, KT, D], F32R), sb("wo_lo", [P, KT, D], F32R)
        bob = sb("bo_rows", [P, D])
        gab = sb("gu_a", [P, KT, 2 * R])
        oraw = sb("o_raw", [P, KT, P])
        oh, ol = ([sb(f"{n}{s}", [P, KT, P], F32R) for s in two] for n in ("o_hi", "o_lo"))
        res = sb("residual", [P, D])
        h1 = sb("h1_tok", [P, D])
        nrm = sb("h1_nrm", [P, D])
        x2f = sb("x2_f32", [P, KT, P])
        stats, mv, std, eps = sb("d_stats", [P, 2, 6]), sb("d_mv", [P, 2]), sb("d_std", [P, 2]), sb("d_eps", [P, 1])
        acc = [st.enter_context(nc.psum_tensor(f"d_acc{s}", [P, 2, 512], F32)) for s in two]
        pn = st.enter_context(nc.psum_tensor("d_pn", [P, KT, P], F32))
        pl = st.enter_context(nc.psum_tensor("d_pl", [P, P], F32))
        s_passed = sem("d_passed")
        s_const, s_eps, s_dve = sem("d_const"), sem("d_eps"), sem("d_dve")
        s_wraw = [sem(f"d_wraw{s}") for s in two]
        s_woh, s_wol = sem("d_woh"), sem("d_wol")
        s_o, s_oh, s_ol, s_h0, s_res, s_acc, s_h1, s_h1out, s_mv, s_std, s_nrm, s_trn, s_hi, s_f, s_lo, s_low, s_lowout = (
            sem("d_" + n) for n in ("o", "oh", "ol", "h0", "res", "acc", "h1", "h1out", "mv", "std", "nrm", "trn", "hi",
                                    "f", "lo", "low", "lowout"))
        VIS = C // 2
        start_free(nc, [s_lo, s_lowout, s_h1, s_low], 1)
        nc.all_engine_barrier()
        block = st.enter_context(nc.Block())

        @block.sync
        def _(sp):
            sp.dma_start(gab[:], ga).then_inc(s_const, 16)
            sp.dma_start(bob[:], bo).then_inc(s_const, 16)
            for k in range(KT):
                if k >= 2:
                    sp.wait_ge(s_wol, k - 1)
                sp.dma_start(wraw[k % 2][:], wo[:, k, :]).then_inc(s_wraw[k % 2], 16)
            with sp.Fori(0, C) as n:
                sp.wait_ge(s_h1, n + 2)
                sp.dma_start(h1_dram[bass.ds(n, 1), :, :].rearrange("o t d -> (o t) d"), h1[:]).then_inc(s_h1out, 16)
            sp.wait_ge(s_h1out, 16 * C)

        @block.gpsimd
        def _(pool):
            pool.wait_ge(s_const, 32)
            with pool.Fori(0, C) as n:
                pool.wait_ge(s_h1, n + 1)
                pool.dma_start(res[:], h0_dram[bass.ds(n, 1), :, :].rearrange("o t d -> (o t) d")).then_inc(s_h0, 16)
                pool.wait_ge(s_h0, n * 16 + 16)
                nc.gpsimd.tensor_tensor(res[:], res[:], bob[:], ALU.add).then_inc(s_res, 1)

        @block.tensor
        def _(pe):
            def products(s, b, k):
                rhs = slice(b * 512, (b + 1) * 512)
                nc.tensor.matmul(acc[s][:, b, :], oh[s][:, k, :], woh[:, k, rhs], start=(k == 0), stop=False)
                nc.tensor.matmul(acc[s][:, b, :], oh[s][:, k, :], wol[:, k, rhs], start=False, stop=False)
                return nc.tensor.matmul(acc[s][:, b, :], ol[s][:, k, :], woh[:, k, rhs], start=False, stop=(k == KT - 1))

            def half(s, b):
                for k in range(KT):
                    last = products(s, b, k)
                return last

            def to_features(n):
                pe.wait_ge(s_nrm, n)
                pe.wait_ge(s_lo, n)
                for i in range(KT):
                    last = nc.tensor.transpose(pn[:, i, :], nrm[:, i * P:(i + 1) * P], ident[:])
                last.then_inc(s_trn, 1)

            def low_rank(n):
                pe.wait_ge(s_f, n)
                pe.wait_ge(s_lowout, n)
                for k in range(KT):
                    last = nc.tensor.matmul(pl[0:2 * R, :], gab[:, k, :], x2f[:, k, :], start=(k == 0), stop=(k == KT - 1))
                last.then_inc(s_low, 1)

            def first_two():
                pe.wait_ge(s_ol, 1)
                for k in range(KT + BEHIND_D):
                    if k < KT:
                        pe.wait_ge(s_wol, k + 1)
                        products(0, 0, k)
                        last = products(0, 1, k)
                        if k == KT - 1:
                            last.then_inc(s_acc, 1)
                    if k == BEHIND_D:
                        pe.wait_ge(s_ol, 2)
                    if k >= BEHIND_D:
                        products(1, 0, k - BEHIND_D)
                        last = products(1, 1, k - BEHIND_D)
                    if k == KT + BEHIND_D - 3:
                        to_features(1)
                last.then_inc(s_acc, 1)
                low_rank(1)

            def step(n, s):
                pe.wait_ge(s_ol, n + 1)
                pe.wait_ge(s_h1, n)
                half(s, 0)
                to_features(n)
                half(s, 1).then_inc(s_acc, 1)
                low_rank(n)

            pe.wait_ge(s_const, 32)
            first_two()
            with pe.Fori(0, VIS - 1) as v:
                step(v * 2 + 2, 0)
                step(v * 2 + 3, 1)
            to_features(C)
            low_rank(C)

        @block.scalar
        def _(act):
            def high_weights(start, end):
                for k in range(start, end):
                    act.wait_ge(s_wraw[k % 2], 16 * (k // 2 + 1))
                    nc.scalar.activation(woh[:, k, :], wraw[k % 2][:], ACT.Copy).then_inc(s_woh, 1)

            def load(n):
                act.dma_start(oraw[:], o_dram.rearrange("k f t -> f k t")[:, :, bass.ds(n * H, H)]).then_inc(s_o, 16)

            def take(n):
                apart(act, s_passed, (s_trn, n))
                nc.scalar.activation(x2_hi[:, :, bass.ds((n - 1) * H, H)], pn[:], ACT.Copy).then_inc(s_hi, 1)
                act.wait_ge(s_low, n)
                nc.scalar.activation(x2f[:], pn[:], ACT.Copy).then_inc(s_f, 1)
                apart(act, s_passed, (s_low, n + 1))
                nc.scalar.activation(low[:, bass.ds((n - 1) * H, H)], pl[0:2 * R, :], ACT.Copy).then_inc(s_lowout, 1)

            def deviation(n):
                act.wait_ge(s_mv, n + 1)
                nc.scalar.activation(std[:, 0:1], mv[:, 1:2], ACT.Sqrt, bias=eps[:]).then_inc(s_std, 1)

            def split(n, s):
                act.wait_ge(s_o, n * 16 + 16)
                nc.scalar.activation(oh[s][:], oraw[:], ACT.Copy).then_inc(s_oh, 1)

            def step(n, s):
                act.wait_ge(s_ol, n + 1)
                load_n = n + 1
                load(load_n)
                act.wait_ge(s_acc, n)
                split(load_n, 1 - s)
                take(n)
                deviation(n)

            act.wait_ge(s_eps, 1)
            load(0)
            high_weights(0, 1)
            split(0, 0)
            high_weights(1, 2)
            act.wait_ge(s_ol, 1)
            load(1)
            high_weights(2, 5)
            split(1, 1)
            high_weights(5, KT)
            deviation(0)
            with act.Fori(0, VIS - 1) as v:
                step(v * 2 + 1, 1)
                step(v * 2 + 2, 0)
            take(C - 1)
            deviation(C - 1)
            take(C)

        @block.vector
        def _(dve):
            chain = Chain(dve, s_dve)
            nc.vector.memset(eps[:], EPS).then_inc(s_eps, 1)

            def low_split(n, s):
                dve.wait_ge(s_oh, n + 1)
                nc.vector.tensor_tensor(ol[s][:], oraw[:], oh[s][:].bitcast(F32), ALU.subtract).then_inc(s_ol, 1)

            def take(n):
                at = bass.ds((n - 1) * H, H)
                dve.wait_ge(s_f, n)
                nc.vector.tensor_tensor(x2_lo[:, :, at], pn[:], x2_hi[:, :, at], ALU.subtract).then_inc(s_lo, 1)

            def normalise(n, s):
                dve.wait_ge(s_acc, n + 1)
                dve.wait_ge(s_res, n + 1)
                dve.wait_ge(s_h1out, n * 16)
                nc.vector.tensor_tensor(h1[:], acc[s][:].rearrange("p b n -> p (b n)"), res[:], ALU.add).then_inc(s_h1, 1)
                dve.wait_ge(s_h1, n + 2)
                chain.mark(nc.vector.bn_stats(stats[:, 0, :], h1[:, 0:512]))
                chain.mark(nc.vector.bn_stats(stats[:, 1, :], h1[:, 512:D]))
                apart(dve, s_passed, (s_dve, chain.now()))
                nc.vector.bn_aggr(mv[:], stats[:].rearrange("p a b -> p (a b)")).then_inc(s_mv, 1)
                dve.wait_ge(s_std, n + 1)
                chain.after(nc.vector.reciprocal(std[:, 1:2], std[:, 0:1]))
                nc.vector.tensor_scalar(nrm[:], h1[:], mv[:, 0:1], std[:, 1:2], ALU.subtract, ALU.mult).then_inc(s_nrm, 1)

            def step(n, s, end=False):
                if not end:
                    low_split(n + 1, 1 - s)
                take(n)
                normalise(n, s)

            low_split(0, 0)
            for k in range(KT):
                dve.wait_ge(s_woh, k + 1)
                nc.vector.tensor_tensor(wol[:, k, :], wraw[k % 2][:], woh[:, k, :].bitcast(F32), ALU.subtract).then_inc(s_wol, 1)
                if k == 4:
                    low_split(1, 1)
            normalise(0, 0)
            first = chain.count
            with dve.Fori(0, VIS - 1) as v:
                chain.loop(v, 6)
                step(v * 2 + 1, 1)
                step(v * 2 + 2, 0)
            chain.end(VIS - 1, 6, first)
            step(C - 1, 1, True)
            take(C)
    return sems


R = 32
I = 2752
IT = -(-I // P)
Q_ZERO, Q_STEP, LR_SCALE = 7.5, 0.005, 0.02
CH = 512
NCH = TOK // CH


def gate_up(nc, qgu, sgu, bgu, da, spread_by, qd, x2_hi, x2_lo, low, hid_dram, inner_st, ring, s_ring):
    sems = []
    with ExitStack() as st:
        def sb(name, shape, dt=F32):
            return st.enter_context(nc.sbuf_tensor(name, shape, dt))

        def sem(name):
            sems.append(nc.alloc_semaphore(name))
            return sems[-1]

        two = range(2)
        qraw = [sb(f"q_raw{s}", [P, 2, D], I32) for s in two]
        q16 = [sb(f"q_f16{s}", [P, 2, D], F16) for s in two]
        braw = [sb(f"b_raw{s}", [P, 2, P]) for s in two]
        bst = [sb(f"b_stack{s}", [P, 2, P], F32R) for s in two]
        scl = sb("gu_scale", [P, 2, IT])
        sel_raw, sel = sb("spread_raw", [2 * R, 6, P]), sb("spread_by", [2 * R, 6, P], F32R)
        lst = sb("low_stack", [P, 2, TOK], F32R)
        araw, a_st = [sb(f"a_raw{s}", [P, R]) for s in two], [sb(f"a_split{s}", [P, 2, R], F32R) for s in two]
        hs_hi, hs_lo = ([sb(f"{n}{c}", [P, CH], F32R) for c in two] for n in ("hid_hi", "hid_lo"))
        inner = sb("inner_sum", [2 * R, TOK])
        lsb = [sb(f"low_term{c}", [P, 2, CH]) for c in two]
        gsb, usb, ssb = ([sb(f"{n}{c}", [P, CH]) for c in two] for n in ("gate", "up", "silu"))
        hid = [sb(f"hid{s}", [P, TOK]) for s in two]
        ps_m = [st.enter_context(nc.psum_tensor(f"e_main{c}", [P, 2, CH], F32)) for c in two]
        ps_l = st.enter_context(nc.psum_tensor("e_low", [P, 2, CH], F32))
        ps_i = [st.enter_context(nc.psum_tensor(f"e_inner{c}", [P, CH], F32)) for c in two]
        s_passed = sem("e_passed")
        s_scl, s_scl2, s_sel, s_sel2, s_spread, s_part_hi, s_part_lo, s_lst, s_ist, s_dve = (
            sem("e_" + n) for n in ("scl", "scl2", "sel", "sel2", "spread", "part_hi", "part_lo", "lst", "ist", "dve"))
        s_load, s_q, s_b, s_read, s_out = ([sem(f"e_{n}{s}") for s in two] for n in ("load", "q", "b", "read", "out"))
        s_main, s_gate, s_silu, s_up, s_hid, s_hi, s_lo, s_inner, s_add = (
            [sem(f"e_{n}{s}") for s in two] for n in ("main", "gate", "silu", "up", "hid", "hi", "lo", "inner", "add"))
        s_low, s_lsb, s_zero = (sem("e_" + n) for n in ("low", "lsb", "zero"))
        s_a = [sem(f"e_a{s}") for s in two]
        PER = NCH // 2
        start_free(nc, [*s_q, *s_b, *s_read, *s_up, s_lsb, *s_hid, *s_silu, *s_a, *s_add, s_lo[1]], 1)
        start_free(nc, [*s_out], 16)
        nc.all_engine_barrier()
        block = st.enter_context(nc.Block())

        first_banks = [(ps_m[0][:, 0, :], ps_m[0][:, 1, :]), (ps_m[1][:, 0, :], ps_m[1][:, 1, :]),
                       (ps_l[:, 0, :], ps_l[:, 1, :]), (ps_i[0][:], ps_i[1][:])]
        last_banks = [ps_m[0][:, 0, :], ps_m[0][:, 1, :], ps_m[1][:, 0, :], ps_m[1][:, 1, :]]

        @block.sync
        def _(sp):
            sp.dma_start(sel_raw[:], spread_by).then_inc(s_sel, 16)
            with sp.Fori(0, IT // 2) as v:
                for s in two:
                    sp.wait_ge(s_q[s], v + 1)
                    sp.wait_ge(s_b[s], v + 1)
                    sp.wait_ge(s_a[s], v + 1)
                    sp.dma_start(qraw[s][:], qgu[bass.ds(v * 2 + s, 1), :, :, :].rearrange("o p m n -> (o p) m n")).then_inc(s_load[s], 16)
                    sp.dma_start(braw[s][:], bgu[bass.ds(v * 2 + s, 1), :, :, :].rearrange("o p m n -> (o p) m n")).then_inc(s_load[s], 16)
                    sp.dma_start(araw[s][:], da[:, bass.ds(v * 2 + s, 1), :].rearrange("p o r -> p (o r)")).then_inc(s_load[s], 16)
            for i, slot in enumerate(ring):
                sp.dma_start(slot[:], qd[:, i, :]).then_inc(s_ring[i], 16)

        @block.gpsimd
        def _(pool):
            pool.wait_ge(s_load[1], 48)
            nc.gpsimd.tensor_scalar(q16[1][:], qraw[1][:], Q_ZERO, None, ALU.subtract).then_inc(s_q[1], 1)
            with pool.Fori(1, IT // 2) as v:
                for s in two:
                    apart(pool, s_passed, (s_load[s], v * 48 + 48), (s_read[s], v + 1))
                    nc.gpsimd.tensor_scalar(q16[s][:], qraw[s][:], Q_ZERO, None, ALU.subtract).then_inc(s_q[s], 1)

        @block.tensor
        def _(pe):
            def inner_product(b, s, n):
                pe.wait_ge(s_lo[b], n + 1)
                pe.wait_ge(s_add[b], n + 1)
                nc.tensor.matmul(ps_i[b][0:2 * R, :], a_st[s][:, :, :], hs_hi[b][:], start=True, stop=False)
                nc.tensor.matmul(ps_i[b][0:2 * R, :], a_st[s][:, :, :], hs_lo[b][:], start=False, stop=True).then_inc(s_inner[b], 1)

            pe.wait_ge(s_sel2, 1)
            for c in range(NCH):
                pe.wait_ge(s_part_lo, c + 1)
                for m in two:
                    nc.tensor.matmul(first_banks[c][m], sel[:, m, :], hs_hi[c % 2][0:2 * R, :], start=True, stop=False)
                    last = nc.tensor.matmul(first_banks[c][m], sel[:, 2 + m, :], hs_lo[c % 2][0:2 * R, :], start=False, stop=True)
                last.then_inc(s_spread, 1)
            pe.wait_ge(s_lst, 4)
            with pe.Fori(0, IT // 2) as v:
                for s in two:
                    pe.wait_ge(s_q[s], v + 2)
                    for c in range(NCH):
                        b, n = c % 2, v * 2 * PER + s * PER + c // 2
                        tok = slice(c * CH, (c + 1) * CH)
                        pe.wait_ge(s_up[b], n + 1)
                        for m in two:
                            for k in range(KT):
                                w = q16[s][:, m, k * P:(k + 1) * P]
                                nc.tensor.matmul(ps_m[b][:, m, :], w, x2_hi[:, k, tok], start=(k == 0), stop=False)
                                last = nc.tensor.matmul(ps_m[b][:, m, :], w, x2_lo[:, k, tok], start=False, stop=(k == KT - 1))
                        last.then_inc(s_main[b], 1)
                        pe.wait_ge(s_b[s], v + 2)
                        pe.wait_ge(s_lst, 2 * NCH)
                        pe.wait_ge(s_lsb, (v * 2 + s) * NCH + c + 1)
                        first = nc.tensor.matmul(ps_l[:, 0, :], bst[s][:, 0, :], lst[:, 0, tok], start=True, stop=True)
                        if c == NCH - 1:
                            first.then_inc(s_read[s], 1)
                        nc.tensor.matmul(ps_l[:, 1, :], bst[s][:, 1, :], lst[:, 1, tok], start=True, stop=True).then_inc(s_low, 1)
                        if c == 1:
                            pe.wait_ge(s_a[s], v + 2)
                        inner_product(1 - b, 1 - s if c == 0 else s, n)
            inner_product(1, 1, IT * PER)
            for b in two:
                pe.wait_ge(s_up[b], PER * IT + 1)
            for c in range(NCH):
                pe.wait_ge(s_part_lo, NCH + c + 1)
                nc.tensor.matmul(last_banks[c], sel[:, 4, :], hs_hi[c % 2][0:2 * R, :], start=True, stop=False)
                nc.tensor.matmul(last_banks[c], sel[:, 5, :], hs_lo[c % 2][0:2 * R, :], start=False, stop=True).then_inc(s_spread, 1)

        @block.scalar
        def _(act):
            act.dma_start(scl[:], sgu).then_inc(s_scl, 16)

            def part(source, c, before):
                if c >= 2:
                    act.wait_ge(s_spread, before + c - 1)
                nc.scalar.activation(hs_hi[c % 2][0:2 * R, :], source[:, c * CH:(c + 1) * CH], ACT.Copy).then_inc(s_part_hi, 1)

            act.wait_ge(s_zero, 4)
            part(low, 0, 0)
            for c in range(NCH):
                if c + 1 < NCH:
                    part(low, c + 1, 0)
                act.wait_ge(s_spread, c + 1)
                nc.scalar.activation(lst[:, 0, c * CH:(c + 1) * CH], first_banks[c][0], ACT.Copy).then_inc(s_lst, 1)
            with act.Fori(0, IT // 2) as v:
                for s in two:
                    for c in range(NCH):
                        b, n = c % 2, v * 2 * PER + s * PER + c // 2
                        act.wait_ge(s_low, (v * 2 + s) * NCH + c + 1)
                        act.wait_ge(s_up[b], n + 1)
                        nc.scalar.activation(lsb[b][:], ps_l[:], ACT.Copy, scale=LR_SCALE).then_inc(s_lsb, 1)
                        act.wait_ge(s_gate[b], n + 1)
                        act.wait_ge(s_hid[b], n + 1)
                        nc.scalar.activation(ssb[b][:], gsb[b][:], ACT.Silu).then_inc(s_silu[b], 1)
                        act.wait_ge(s_hid[b], n + 2)
                        nc.scalar.activation(hs_hi[b][:], hid[s][:, c * CH:(c + 1) * CH], ACT.Copy).then_inc(s_hi[b], 1)
                    act.wait_ge(s_hid[0], v * 2 * PER + (s + 1) * PER + 1)
                    act.wait_ge(s_hid[1], v * 2 * PER + (s + 1) * PER + 1)
                    act.dma_start(hid_dram[bass.ds(v * 2 + s, 1), :, :].rearrange("o p t -> (o p) t"), hid[s][:]).then_inc(s_out[s], 16)
            for b in two:
                act.wait_ge(s_add[b], PER * IT + 1 + b)
            part(inner, 0, NCH)
            for c in range(NCH):
                if c + 1 < NCH:
                    part(inner, c + 1, NCH)
                act.wait_ge(s_spread, NCH + c + 1)
                nc.scalar.activation(inner_st[:, c * CH:(c + 1) * CH], last_banks[c], ACT.Copy).then_inc(s_ist, 1)
            for s in two:
                act.wait_ge(s_out[s], 16 * (IT // 2) + 16)

        @block.vector
        def _(dve):
            chain = Chain(dve, s_dve)
            tt = nc.vector.tensor_tensor

            def add_inner(b, c, n):
                dve.wait_ge(s_inner[b], n + 1)
                tok = slice(c * CH, (c + 1) * CH)
                tt(inner[:, tok], inner[:, tok], ps_i[b][0:2 * R, :], ALU.add).then_inc(s_add[b], 1)

            nc.vector.memset(a_st[1][:].bitcast(F32), 0.0).then_inc(s_zero, 1)
            nc.vector.memset(hs_hi[1][:].bitcast(F32), 0.0).then_inc(s_zero, 1)
            nc.vector.memset(hs_lo[1][:].bitcast(F32), 0.0).then_inc(s_zero, 1)
            nc.vector.memset(inner[:], 0.0).then_inc(s_zero, 1)
            dve.wait_ge(s_zero, 4)
            dve.wait_ge(s_scl, 16)
            nc.vector.tensor_scalar(scl[:], scl[:], Q_STEP, None, ALU.mult).then_inc(s_scl2, 1)
            dve.wait_ge(s_scl2, 1)

            def part(source, c, before):
                dve.wait_ge(s_part_hi, before + c + 1)
                if c >= 2:
                    dve.wait_ge(s_spread, before + c - 1)
                tt(hs_lo[c % 2][0:2 * R, :], source[:, c * CH:(c + 1) * CH], hs_hi[c % 2][0:2 * R, :].bitcast(F32),
                   ALU.subtract).then_inc(s_part_lo, 1)

            dve.wait_ge(s_sel, 16)
            nc.vector.tensor_copy(sel[:], sel_raw[:]).then_inc(s_sel2, 1)
            part(low, 0, 0)
            for c in range(NCH):
                if c + 1 < NCH:
                    part(low, c + 1, 0)
                if c == 1:
                    dve.wait_ge(s_load[0], 48)
                    nc.vector.tensor_scalar(q16[0][:], qraw[0][:], Q_ZERO, None, ALU.subtract).then_inc(s_q[0], 1)
                dve.wait_ge(s_spread, c + 1)
                nc.vector.tensor_copy(lst[:, 1, c * CH:(c + 1) * CH], first_banks[c][1]).then_inc(s_lst, 1)
            first = chain.count
            with dve.Fori(0, IT // 2) as v:
                chain.loop(v, 2 * 3)
                for s in two:
                    dve.wait_ge(s_load[s], v * 48 + 48)
                    chain.after(nc.vector.tensor_copy(bst[s][:], braw[s][:]))
                    for g in (1, 3):
                        r = slice(R * g, R * g + R)
                        last = tt(bst[s][r, :, :], braw[s][r, :, :], bst[s][r, :, :].bitcast(F32), ALU.subtract)
                        if g == 1:
                            chain.mark(last)
                    last.then_inc(s_b[s], 1)
                    chain.after(nc.vector.tensor_copy(a_st[s][:, 0, :], araw[s][:]))
                    tt(a_st[s][:, 1, :], araw[s][:], a_st[s][:, 0, :].bitcast(F32), ALU.subtract).then_inc(s_a[s], 1)
                    for c in range(NCH):
                        b, n = c % 2, v * 2 * PER + s * PER + c // 2
                        dve.wait_ge(s_main[b], n + 1)
                        dve.wait_ge(s_lsb, (v * 2 + s) * NCH + c + 2)
                        dve.wait_ge(s_silu[b], n + 1)
                        for m, out, done in ((0, gsb, s_gate), (1, usb, s_up)):
                            nc.vector.scalar_tensor_tensor(out[b][:], ps_m[b][:, m, :], scl[:, m, bass.ds(v * 2 + s, 1)], lsb[b][:, m, :],
                                                           ALU.mult, ALU.add).then_inc(done[b], 1)
                        dve.wait_ge(s_silu[b], n + 2)
                        dve.wait_ge(s_up[b], n + 2)
                        if c == 0:
                            dve.wait_ge(s_out[s], v * 16 + 16)
                        tt(hid[s][:, c * CH:(c + 1) * CH], ssb[b][:], usb[b][:], ALU.mult).then_inc(s_hid[b], 1)
                        add_inner(1 - b, (c - 1) % NCH, n)
                        dve.wait_ge(s_hi[b], n + 1)
                        tt(hs_lo[b][:], hid[s][:, c * CH:(c + 1) * CH], hs_hi[b][:].bitcast(F32), ALU.subtract).then_inc(s_lo[b], 1)
            chain.end(IT // 2, 6, first)
            add_inner(1, NCH - 1, IT * PER)
            for c in range(NCH):
                part(inner, c, NCH)
            dve.wait_ge(s_part_lo, 2 * NCH)
            dve.wait_ge(s_ist, NCH)
    return sems


HALF = 512
BEHIND_F = 16
QS = 5


def down(nc, qd, sd, db, inner_st, hid_dram, h1_dram, out, qraw, s_qload):
    sems = []
    with ExitStack() as st:
        def sb(name, shape, dt=F32):
            return st.enter_context(nc.sbuf_tensor(name, shape, dt))

        def sem(name):
            sems.append(nc.alloc_semaphore(name))
            return sems[-1]

        two = range(2)
        qd_sb = sb("f_levels", [P, IT, D], F32R)
        braw, b_st = sb("f_braw", [P, D]), sb("f_b", [P, D], F32R)
        scl = sb("f_scale", [P, D])
        hraw = sb("f_hraw", [P, IT, P])
        hh, hl = ([sb(f"f_{n}{s}", [P, IT, P], F32R) for s in two] for n in ("hh", "hl"))
        h1 = sb("f_h1", [P, D])
        lrt = sb("f_lrt", [P, D])
        y = sb("f_y", [P, D])
        pt = sb("f_pt", [P, P], F32R)
        acc = [st.enter_context(nc.psum_tensor(f"f_acc{s}", [P, 2, HALF], F32)) for s in two]
        ps_l = st.enter_context(nc.psum_tensor("f_lr", [P, 2, HALF], F32))
        s_const, s_b, s_scl, s_dve = (sem("f_s" + n) for n in ("const", "b", "scl", "dve"))
        s_q = sem("f_sq")
        s_h, s_hh, s_hl, s_acc, s_pt, s_lr, s_lrt, s_h1, s_sum, s_scaled, s_y, s_out = (
            sem("f_s" + n) for n in ("h", "hh", "hl", "acc", "pt", "lr", "lrt", "h1", "sum", "scaled", "y", "out"))
        VIS = C // 2
        start_free(nc, [s_scaled, s_lrt, s_y, s_sum], 1)
        start_free(nc, [s_out], 16)
        nc.all_engine_barrier()
        block = st.enter_context(nc.Block())

        @block.sync
        def _(sp):
            sp.dma_start(hraw[:], hid_dram.rearrange("i p t -> p i t")[:, :, 0:P]).then_inc(s_h, 16)
            for i in range(QS, IT):
                sp.wait_ge(s_q, i - QS + 1)
                sp.dma_start(qraw[i % QS][:], qd[:, i, :]).then_inc(s_qload[i % QS], 16)
            with sp.Fori(0, C) as n:
                sp.wait_ge(s_y, n + 2)
                sp.dma_start(out[bass.ds(n, 1), :, :].rearrange("o t d -> (o t) d"), y[:]).then_inc(s_out, 16)
            sp.wait_ge(s_out, 16 * C + 16)

        @block.gpsimd
        def _(pool):
            pool.wait_ge(s_scl, 1)
            with pool.Fori(0, C) as n:
                pool.wait_ge(s_sum, n + 1)
                pool.dma_start(h1[:], h1_dram[bass.ds(n, 1), :, :].rearrange("o t d -> (o t) d")).then_inc(s_h1, 16)
                pool.wait_ge(s_h1, n * 16 + 16)
                pool.wait_ge(s_lrt, n + 2)
                nc.gpsimd.tensor_tensor(lrt[:], lrt[:], h1[:], ALU.add).then_inc(s_sum, 1)

        @block.tensor
        def _(pe):
            def main(s, lo, hi):
                for i in range(lo, hi):
                    for part in (hh, hl):
                        for b in two:
                            last = nc.tensor.matmul(acc[s][:, b, :], part[s][:, i, :], qd_sb[:, i, b * HALF:(b + 1) * HALF],
                                                    start=(i == 0 and part is hh), stop=(i == IT - 1 and part is hl))
                return last

            def low_rank(n):
                pe.wait_ge(s_pt, n)
                pe.wait_ge(s_lrt, n)
                for b in two:
                    last = nc.tensor.matmul(ps_l[:, b, :], pt[:], b_st[:, b * HALF:(b + 1) * HALF], start=True, stop=True)
                last.then_inc(s_lr, 1)

            def first_two():
                pe.wait_ge(s_hl, 1)
                for i in range(IT + BEHIND_F):
                    if i < IT:
                        pe.wait_ge(s_q, i + 1)
                        last = main(0, i, i + 1)
                        if i == IT - 1:
                            last.then_inc(s_acc, 1)
                    if i == BEHIND_F:
                        pe.wait_ge(s_hl, 2)
                    if i >= BEHIND_F:
                        last = main(1, i - BEHIND_F, i - BEHIND_F + 1)
                    if i == IT + BEHIND_F - 2:
                        pe.wait_ge(s_b, 1)
                        low_rank(1)
                last.then_inc(s_acc, 1)

            def step(n, s):
                pe.wait_ge(s_hl, n + 1)
                pe.wait_ge(s_scaled, n)
                main(s, 0, IT // 2)
                low_rank(n)
                main(s, IT // 2, IT).then_inc(s_acc, 1)

            first_two()
            with pe.Fori(0, VIS - 1) as v:
                step(v * 2 + 2, 0)
                step(v * 2 + 3, 1)
            low_rank(C)

        @block.scalar
        def _(act):
            def split(n, s):
                act.wait_ge(s_h, n * 16 + 16)
                nc.scalar.activation(hh[s][:], hraw[:], ACT.Copy).then_inc(s_hh, 1)

            def low_terms(n):
                nc.scalar.activation(pt[:], inner_st[:, bass.ds((n - 1) * P, P)].bitcast(F32), ACT.Copy).then_inc(s_pt, 1)
                act.wait_ge(s_lr, n)
                act.wait_ge(s_y, n)
                nc.scalar.activation(lrt[:], ps_l[:].rearrange("p b n -> p (b n)"), ACT.Copy, scale=LR_SCALE).then_inc(s_lrt, 1)

            def load(n):
                act.wait_ge(s_hl, n)
                act.dma_start(hraw[:], hid_dram.rearrange("i p t -> p i t")[:, :, bass.ds(n * P, P)]).then_inc(s_h, 16)

            def step(n, s):
                load(n + 1)
                act.wait_ge(s_acc, n)
                split(n + 1, 1 - s)
                low_terms(n)

            act.dma_start(scl[:], sd).then_inc(s_const, 16)
            act.dma_start(braw[:], db).then_inc(s_const, 16)
            split(0, 0)
            load(1)
            split(1, 1)
            with act.Fori(0, VIS - 1) as v:
                step(v * 2 + 1, 1)
                step(v * 2 + 2, 0)
            low_terms(C - 1)
            low_terms(C)

        @block.vector
        def _(dve):
            chain = Chain(dve, s_dve)
            tt = nc.vector.tensor_tensor

            def low_split(n, s):
                dve.wait_ge(s_hh, n + 1)
                tt(hl[s][:], hraw[:], hh[s][:].bitcast(F32), ALU.subtract).then_inc(s_hl, 1)

            def step(n, s, end=False):
                if not end:
                    low_split(n + 1, 1 - s)
                scale_sums(n, 1 - s)

            def scale_sums(n, s):
                dve.wait_ge(s_acc, n)
                dve.wait_ge(s_out, (n - 1) * 16 + 16)
                tt(y[:], acc[s][:].rearrange("p b n -> p (b n)"), scl[:], ALU.mult).then_inc(s_scaled, 1)
                dve.wait_ge(s_scaled, n + 1)
                dve.wait_ge(s_sum, n + 1)
                tt(y[:], y[:], lrt[:], ALU.add).then_inc(s_y, 1)

            def levels(start, end):
                for i in range(start, end):
                    dve.wait_ge(s_qload[i % QS], 16 * (i // QS + 1))
                    nc.vector.tensor_scalar(qd_sb[:, i, :], qraw[i % QS][:], Q_ZERO, None, ALU.subtract).then_inc(s_q, 1)

            levels(0, QS)
            low_split(0, 0)
            dve.wait_ge(s_const, 32)
            nc.vector.tensor_scalar(scl[:], scl[:], Q_STEP, None, ALU.mult).then_inc(s_scl, 1)
            chain.after(nc.vector.tensor_copy(b_st[:], braw[:]))
            for g in (1, 3):
                r = slice(R * g, R * g + R)
                last = tt(b_st[r, :], braw[r, :], b_st[r, :].bitcast(F32), ALU.subtract)
            last.then_inc(s_b, 1)
            levels(QS, 14)
            low_split(1, 1)
            levels(14, IT)
            with dve.Fori(0, VIS - 1) as v:
                step(v * 2 + 1, 1)
                step(v * 2 + 2, 0)
            step(C - 1, 1, True)
            scale_sums(C, 1)
    return sems


def retire(nc, sems):
    nc.clear_and_free_semaphores(sems)
    nc.all_engine_barrier()


def vit_tower(nc, t, out):
    h0_dram = nc.dram_tensor("h0_tokens", (C, H, D), F32, kind="Internal").ap()
    o_dram = nc.dram_tensor("o_features", (KT, P, TOK), F32, kind="Internal").ap()
    h1_dram = nc.dram_tensor("h1_tokens", (C, H, D), F32, kind="Internal").ap()
    hid_dram = nc.dram_tensor("hidden", (IT, P, TOK), F32, kind="Internal").ap()
    with ExitStack() as whole:
        s_ring = [nc.alloc_semaphore(f"down_levels{i}") for i in range(QS)]
        with ExitStack() as st:
            ident = st.enter_context(nc.sbuf_tensor("ident", [P, P], F32))
            mask = st.enter_context(nc.sbuf_tensor("causal_mask", [P, P], F32))
            s_const = st.enter_context(nc.semaphore("const_loaded"))
            s_raw = nc.alloc_semaphore("qkv_weights")
            with nc.sbuf_tensor("w_raw", [P, 3, D], F32, side="right") as raw:
                with nc.Block() as block:
                    @block.sync
                    def _(sp):
                        sp.dma_start(ident[:], t["ident"]).then_inc(s_const, 16)
                        sp.dma_start(mask[:], t["mask"]).then_inc(s_const, 16)
                        sp.wait_ge(s_const, 32)
                x_hi = st.enter_context(nc.sbuf_tensor("x_hi", [P, KT, TOK], F16))
                x_lo = st.enter_context(nc.sbuf_tensor("x_lo", [P, KT, TOK], F16))
                retire(nc, ssm_and_norm(nc, t["ssm"], t["c_re"], t["c_im"], h0_dram, x_hi, x_lo, ident,
                                        t["w_qkv"][0, :, :, :], raw, s_raw))
                retire(nc, attention(nc, t["w_qkv"], t["b_qkv"], raw, s_raw, x_hi, x_lo, ident, mask, o_dram))
            low = st.enter_context(nc.sbuf_tensor("low_rank", [2 * R, TOK], F32))
            retire(nc, project_and_norm(nc, t["w_o"], t["b_o"], t["gu_a"], o_dram, h0_dram, h1_dram, x_hi, x_lo, low, ident))
            inner_st = whole.enter_context(nc.sbuf_tensor("inner_stack", [P, TOK], F32R, side="right"))
            ring = [whole.enter_context(nc.sbuf_tensor(f"down_raw{i}", [P, D], I32, side="right")) for i in range(QS)]
            retire(nc, gate_up(nc, t["gu_q"], t["gu_scale"], t["gu_b"], t["down_a"], t["spread_by"], t["down_q"], x_hi, x_lo, low,
                               hid_dram, inner_st, ring, s_ring))
        down(nc, t["down_q"], t["down_scale"], t["down_b"], inner_st, hid_dram, h1_dram, out, ring, s_ring)


def layouts(v):
    import numpy as np

    def padded(a, axis):
        room = list(a.shape)
        room[axis] = IT * P - a.shape[axis]
        return np.concatenate([a, np.zeros(room, a.dtype)], axis)

    def twice(a):
        return np.concatenate([a, a], 0)

    f = {n: np.asarray(a) for n, a in v.items()}
    x, b = f["x"], f["L0_tok_B"]
    q_gu = np.stack([padded(f["L0_ffn_gate_q"], 0), padded(f["L0_ffn_up_q"], 0)])
    s_gu = np.stack([padded(f["L0_ffn_gate_scale"], 0), padded(f["L0_ffn_up_scale"], 0)])
    b_gu = np.stack([padded(f["L0_ffn_gate_B"], 1), padded(f["L0_ffn_up_B"], 1)])
    wqkv = np.stack([f["L0_attn_Wq"], f["L0_attn_Wk"], f["L0_attn_Wv"]])
    bqkv = np.stack([f["L0_attn_bq"], f["L0_attn_bk"], f["L0_attn_bv"]])
    a_gu = np.concatenate([f["L0_ffn_gate_A"], f["L0_ffn_up_A"]], 1)
    at = np.arange(P)
    spread = np.zeros((2, R, 6, 4, R), np.float32)
    for k, m, groups in ((0, 0, (0, 1)), (1, 1, (0, 1)), (2, 0, (2, 3)), (3, 1, (2, 3)),
                         (4, 0, (0, 1)), (4, 1, (2, 3)), (5, 0, (2, 3)), (5, 1, (2, 3))):
        for g in groups:
            spread[m, range(R), k, g, range(R)] = 1.0
    out = {
        "spread_by": spread.reshape(2 * R, 6, P),
        "ssm": np.stack([np.broadcast_to(f["L0_tok_log_dt"], (P, H)), twice(f["L0_tok_inv_A_real"].T),
                         twice(f["L0_tok_A_imag"].T), twice(b[..., 0].T), twice(b[..., 1].T)], 1),
        "c_re": twice(x[..., 0].transpose(2, 1, 0)),
        "c_im": twice(x[..., 1].transpose(2, 1, 0)),
        "w_qkv": wqkv.reshape(3, KT, P, KT, P).transpose(1, 4, 0, 3, 2).reshape(KT, P, 3, D),
        "b_qkv": bqkv.reshape(3, KT, P).transpose(2, 0, 1),
        "w_o": f["L0_attn_Wo"].T.reshape(KT, P, D).transpose(1, 0, 2),
        "b_o": np.broadcast_to(f["L0_attn_bo"], (P, D)),
        "gu_a": a_gu.reshape(KT, P, 2 * R).transpose(1, 0, 2),
        "gu_q": q_gu.reshape(2, IT, P, KT, P).transpose(1, 4, 0, 3, 2).reshape(IT, P, 2, D),
        "gu_scale": s_gu.reshape(2, IT, P).transpose(2, 0, 1),
        "gu_b": np.tile(b_gu.reshape(2, R, IT, P).transpose(2, 1, 0, 3), (1, 4, 1, 1)),
        "down_q": padded(f["L0_ffn_down_q"], 1).T.reshape(IT, P, D).transpose(1, 0, 2),
        "down_scale": np.broadcast_to(f["L0_ffn_down_scale"], (P, D)),
        "down_a": padded(f["L0_ffn_down_A"], 0).reshape(IT, P, R).transpose(1, 0, 2),
        "down_b": np.tile(f["L0_ffn_down_B"], (4, 1)),
        "ident": np.eye(P, dtype=np.float32),
        "mask": np.where(at[:, None] >= at[None, :], 0.0, -3e38).astype(np.float32),
    }
    return {n: np.ascontiguousarray(a) for n, a in out.items()}


def kernel(**inputs):
    import numpy as np
    import concourse.bacc as bacc
    from concourse.bass_utils import run_bass_kernel_spmd

    arrays = layouts(inputs)
    nc = bacc.Bacc("TRN2", target_bir_lowering=False, num_devices=1)
    tensors = {n: nc.dram_tensor("in_" + n, a.shape, mybir.dt.from_np(a.dtype), kind="ExternalInput").ap()
               for n, a in arrays.items()}
    out = nc.dram_tensor("out_tokens", (C, H, D), F32, kind="ExternalOutput").ap()
    vit_tower(nc, tensors, out)
    r = run_bass_kernel_spmd(nc, [{"in_" + n: a for n, a in arrays.items()}], core_ids=[0])
    return np.asarray(r.results[0]["out_tokens"])
```
